# Optimizing a Trainium2 kernel written in Bass

```python
import numpy as np
import jax
import jax.numpy as jnp

def _softmax(x, axis=-1):
    return jax.nn.softmax(x, axis=axis)

def _gelu(x):
    return jax.nn.gelu(x, approximate=True)

def _silu(x):
    return jax.nn.silu(x)

def _sigmoid(x):
    return jax.nn.sigmoid(x)

def _layernorm(x, axis=-1, eps=1e-05):
    m = jnp.mean(x, axis=axis, keepdims=True)
    v = jnp.var(x, axis=axis, keepdims=True)
    return (x - m) / jnp.sqrt(v + eps)

def _scatter_add(tgt, idx, src, axis=0):
    return tgt.at[idx].add(src)

def _segment_sum(src, seg, n):
    return jax.ops.segment_sum(src, seg, n)
kernel_name = 'mk_xattn_ffn_d4_seqx_r4_ac1380'

def setup_inputs(seed: int=0):
    np.random.seed(seed)
    _w = jnp.asarray

    def _rec_inputs():
        import jax
        import jax.numpy as jnp
        _rk = jax.random.key(seed)
        x = 7.22e-05 + 1 * jax.random.normal(jax.random.fold_in(_rk, 1), (8, 256, 256), jnp.float32)
        _lenS = 256 - jax.random.randint(jax.random.fold_in(_rk, 7), (8,), 0, max(1, 256 // 4) + 1, jnp.int32)
        _lenS2 = 256 - jax.random.randint(jax.random.fold_in(_rk, 8), (8,), 0, max(1, 256 // 4) + 1, jnp.int32)
        _ctx_1024P = jax.random.normal(jax.random.fold_in(_rk, 11), (8, 16, 256), jnp.float32)
        _ctx_1024c = jax.random.dirichlet(jax.random.fold_in(_rk, 511), 0.3 * jnp.ones((16,), jnp.float32), (8, 256))
        _ctx_1024t = jnp.einsum('bsk,bkd->bsd', _ctx_1024c, _ctx_1024P)
        _ctx_1024t = _ctx_1024t * jax.lax.rsqrt(jnp.mean(jnp.square(_ctx_1024t)) + 1e-12) * 0.953939
        ctx_1024 = 4.13588e-05 + 0.999923 * (_ctx_1024t + 0.3 * jax.random.normal(jax.random.fold_in(_rk, 611), (8, 256, 256), jnp.float32))
        _validS = jnp.arange(256)[None, :] < _lenS[:, None]
        _validS2 = jnp.arange(256)[None, :] < _lenS2[:, None]
        _causal = jnp.tril(jnp.ones((256, 256), dtype=bool))
        mask_SxS_bc0 = jnp.logical_not(jnp.broadcast_to(_causal[:, :], (256, 256)))
        mask_BxSxS2_if1 = jnp.where(jnp.ones((8, 256, 256), dtype=bool), 1, 0).astype(jnp.int32)
        return (x, ctx_1024, mask_SxS_bc0, mask_BxSxS2_if1)
    x, ctx_1024, mask_SxS_bc0, mask_BxSxS2_if1 = _rec_inputs()

    def _L0_xattn_setup():
        import jax, jax.numpy as jnp
        import numpy as np
        LN_EPS = 1e-05
        key = jax.random.key(seed)
        ks = jax.random.split(key, 12)
        B, S, D = (4, 512, 256)
        s = 1.0 / np.sqrt(D)
        return {'query': jax.random.normal(ks[0], (B, S, D), jnp.float32), 'key_in': jax.random.normal(ks[1], (B, S, D), jnp.float32), 'value': jax.random.normal(ks[2], (B, S, D), jnp.float32), 'Wq': jax.random.normal(ks[3], (D, D), jnp.float32) * s, 'bq': jax.random.normal(ks[4], (D,), jnp.float32) * s, 'Wk': jax.random.normal(ks[5], (D, D), jnp.float32) * s, 'bk': jax.random.normal(ks[6], (D,), jnp.float32) * s, 'Wv': jax.random.normal(ks[7], (D, D), jnp.float32) * s, 'bv': jax.random.normal(ks[8], (D,), jnp.float32) * s, 'gamma': jnp.ones((D,), jnp.float32), 'beta': jnp.zeros((D,), jnp.float32)}
    _L0_xattn_all = _L0_xattn_setup()
    _L0_xattn_in = {k: v for k, v in _L0_xattn_all.items() if k in ('Wq', 'bq', 'Wk', 'bk', 'Wv', 'bv', 'gamma', 'beta')}
    del _L0_xattn_all

    def _L0_ffn_setup():
        import jax, jax.numpy as jnp
        import numpy as np
        HIDDEN_SIZE = 256
        NUM_EXPERTS = 8
        MOE_INTERMEDIATE_SIZE = 352
        NUM_EXPERTS_PER_TOK = 2
        SHARED_EXPERT_INTERMEDIATE_SIZE = 704
        B, T = (2, 256)
        W_SCALE = 0.02
        key = jax.random.key(seed)
        ks = jax.random.split(key, 8)
        H, E, I, SI = (HIDDEN_SIZE, NUM_EXPERTS, MOE_INTERMEDIATE_SIZE, SHARED_EXPERT_INTERMEDIATE_SIZE)
        return {'x': jax.random.normal(ks[0], (B, T, H), jnp.float32), 'gate_w': jax.random.normal(ks[1], (E, H), jnp.float32) * W_SCALE, 'experts_gate_up': jax.random.normal(ks[2], (E, 2 * I, H), jnp.float32) * W_SCALE, 'experts_down': jax.random.normal(ks[3], (E, H, I), jnp.float32) * W_SCALE, 'shared_gate_w': jax.random.normal(ks[4], (SI, H), jnp.float32) * W_SCALE, 'shared_up_w': jax.random.normal(ks[5], (SI, H), jnp.float32) * W_SCALE, 'shared_down_w': jax.random.normal(ks[6], (H, SI), jnp.float32) * W_SCALE, 'shared_expert_gate_w': jax.random.normal(ks[7], (1, H), jnp.float32) * W_SCALE}
    _L0_ffn_all = _L0_ffn_setup()
    _L0_ffn_in = {k: v for k, v in _L0_ffn_all.items() if k in ('gate_w', 'experts_gate_up', 'experts_down', 'shared_gate_w', 'shared_up_w', 'shared_down_w', 'shared_expert_gate_w')}
    del _L0_ffn_all

    def _L1_xattn_setup():
        import jax, jax.numpy as jnp
        import numpy as np
        from jax import lax
        H = 16
        K1, K2 = (3, 3)
        LN_EPS = 1e-05

        def _ln(x, g, b):
            m = jnp.mean(x, axis=-1, keepdims=True)
            v = jnp.mean(jnp.square(x - m), axis=-1, keepdims=True)
            return (x - m) * lax.rsqrt(v + LN_EPS) * g + b

        def _gelu(x):
            return jax.nn.gelu(x, approximate=False)
        key = jax.random.key(seed)
        B, T, D, Th = (4, 256, 256, 64)
        C = 2 * D
        ks = jax.random.split(key, 16)

        def w(k, shape):
            fan_in = shape[0]
            return (jax.random.normal(k, shape, jnp.float32) / np.sqrt(fan_in)).astype(jnp.float32)
        inp = {'x': jax.random.normal(ks[0], (B, T, D), jnp.float32), 'historical_data': jax.random.normal(ks[1], (B, Th, D), jnp.float32), 'Wq': w(ks[2], (D, D)), 'Wk': w(ks[3], (D, D)), 'Wv': w(ks[4], (D, D)), 'hist_W': w(ks[5], (D, C)), 'hist_b': jnp.zeros((C,), jnp.float32), 'hist_ln_g': jnp.ones((C,), jnp.float32), 'hist_ln_b': jnp.zeros((C,), jnp.float32), 'ctx_W1': w(ks[6], (C, C // 4)), 'ctx_b1': jnp.zeros((C // 4,), jnp.float32), 'ctx_W2': w(ks[7], (C // 4, 1)), 'ctx_b2': jnp.zeros((1,), jnp.float32), 'kg_W1': w(ks[8], (C, D)), 'kg_b1': jnp.zeros((D,), jnp.float32), 'kg_ln_g': jnp.ones((D,), jnp.float32), 'kg_ln_b': jnp.zeros((D,), jnp.float32), 'kg_W2': w(ks[9], (D, H * K1 * K2)), 'kg_b2': jnp.zeros((H * K1 * K2,), jnp.float32), 'proj_W': w(ks[10], (D, D)), 'proj_b': jnp.zeros((D,), jnp.float32), 'causal_mask': jnp.triu(jnp.ones((T, T), bool), k=1)}
        return inp
    _L1_xattn_all = _L1_xattn_setup()
    _L1_xattn_in = {k: v for k, v in _L1_xattn_all.items() if k in ('Wq', 'Wk', 'Wv', 'hist_W', 'hist_b', 'hist_ln_g', 'hist_ln_b', 'ctx_W1', 'ctx_b1', 'ctx_W2', 'ctx_b2', 'kg_W1', 'kg_b1', 'kg_ln_g', 'kg_ln_b', 'kg_W2', 'kg_b2', 'proj_W', 'proj_b')}
    del _L1_xattn_all

    def _L1_ffn_setup():
        import jax, jax.numpy as jnp
        import numpy as np
        D_MODEL = 256
        D_HIDDEN = 1024
        NUM_EXPERTS = 8
        B, T = (2, 512)
        key = jax.random.key(seed)
        ks = jax.random.split(key, 8)
        s = 0.02
        x = jax.random.normal(ks[0], (B, T, D_MODEL), dtype=jnp.float32)
        Wg = jax.random.normal(ks[1], (D_MODEL, NUM_EXPERTS), dtype=jnp.float32) * s
        bg = jnp.zeros((NUM_EXPERTS,), dtype=jnp.float32)
        W1 = jax.random.normal(ks[2], (NUM_EXPERTS, D_MODEL, D_HIDDEN), dtype=jnp.float32) * s
        b1 = jnp.zeros((NUM_EXPERTS, D_HIDDEN), dtype=jnp.float32)
        W2 = jax.random.normal(ks[3], (NUM_EXPERTS, D_HIDDEN, D_MODEL), dtype=jnp.float32) * s
        b2 = jnp.zeros((NUM_EXPERTS, D_MODEL), dtype=jnp.float32)
        return {'x': x, 'Wg': Wg, 'bg': bg, 'W1': W1, 'b1': b1, 'W2': W2, 'b2': b2}
    _L1_ffn_all = _L1_ffn_setup()
    _L1_ffn_in = {k: v for k, v in _L1_ffn_all.items() if k in ('Wg', 'bg', 'W1', 'b1', 'W2', 'b2')}
    del _L1_ffn_all

    def _L2_xattn_setup():
        import jax, jax.numpy as jnp
        import numpy as np
        B, S, D, H = (4, 512, 256, 16)
        DK = D // H

        def _split_heads(x):
            b, s, _ = x.shape
            return x.reshape(b, s, H, DK).transpose(0, 2, 1, 3)
        key = jax.random.key(seed)
        ks = jax.random.split(key, 9)
        scale = 1.0 / np.sqrt(D)
        inp = {'query': jax.random.normal(ks[0], (B, S, D), jnp.float32), 'key': jax.random.normal(ks[1], (B, S, D), jnp.float32), 'value': jax.random.normal(ks[2], (B, S, D), jnp.float32), 'mask': jnp.ones((B, S, S), jnp.int32), 'Wq': jax.random.normal(ks[3], (D, D), jnp.float32) * scale, 'bq': jnp.zeros((D,), jnp.float32), 'Wk': jax.random.normal(ks[4], (D, D), jnp.float32) * scale, 'bk': jnp.zeros((D,), jnp.float32), 'Wv': jax.random.normal(ks[5], (D, D), jnp.float32) * scale, 'bv': jnp.zeros((D,), jnp.float32)}
        return inp
    _L2_xattn_all = _L2_xattn_setup()
    _L2_xattn_in = {k: v for k, v in _L2_xattn_all.items() if k in ('Wq', 'bq', 'Wk', 'bk', 'Wv', 'bv')}
    del _L2_xattn_all

    def _L2_ffn_setup():
        import jax, jax.numpy as jnp
        from jax import lax
        import numpy as np
        D_MODEL = 256
        HIDDEN = 128
        N_EXPERTS = 32
        TOP_K = 2
        B, S = (1, 1024)

        def _moe_group(x2, router_w, wg, wu, wd, top_k):
            T = x2.shape[0]
            n_experts = router_w.shape[1]
            logits = x2 @ router_w
            scores = jax.nn.softmax(logits, axis=-1)
            expert_weights, expert_indices = lax.top_k(scores, top_k)
            flat_e = expert_indices.reshape(-1)
            flat_w = expert_weights.reshape(-1)
            flat_t = jnp.repeat(jnp.arange(T), top_k)
            order = jnp.argsort(flat_e)
            tok = flat_t[order]
            xs = x2[tok]
            group_sizes = jnp.bincount(flat_e, length=n_experts).astype(jnp.int32)
            gate = lax.ragged_dot(xs, wg, group_sizes)
            up = lax.ragged_dot(xs, wu, group_sizes)
            ys = lax.ragged_dot(jax.nn.silu(gate) * up, wd, group_sizes)
            ys = ys * flat_w[order][:, None]
            return jnp.zeros_like(x2).at[tok].add(ys)
        key = jax.random.key(seed)
        ks = jax.random.split(key, 9)
        w = lambda k, shape: jax.random.normal(k, shape, dtype=jnp.float32) * 0.02
        return {'x': jax.random.normal(ks[0], (B, S, D_MODEL), dtype=jnp.float32), 'router_w0': w(ks[1], (D_MODEL, N_EXPERTS)), 'wg0': w(ks[2], (N_EXPERTS, D_MODEL, HIDDEN)), 'wu0': w(ks[3], (N_EXPERTS, D_MODEL, HIDDEN)), 'wd0': w(ks[4], (N_EXPERTS, HIDDEN, D_MODEL)), 'router_w1': w(ks[5], (D_MODEL, N_EXPERTS)), 'wg1': w(ks[6], (N_EXPERTS, D_MODEL, HIDDEN)), 'wu1': w(ks[7], (N_EXPERTS, D_MODEL, HIDDEN)), 'wd1': w(ks[8], (N_EXPERTS, HIDDEN, D_MODEL))}
    _L2_ffn_all = _L2_ffn_setup()
    _L2_ffn_in = {k: v for k, v in _L2_ffn_all.items() if k in ('router_w0', 'wg0', 'wu0', 'wd0', 'router_w1', 'wg1', 'wu1', 'wd1')}
    del _L2_ffn_all

    def _L3_xattn_setup():
        import jax, jax.numpy as jnp
        import numpy as np
        EMBED_DIM = 256
        NUM_HEADS = 16
        HEAD_DIM = EMBED_DIM // NUM_HEADS
        key = jax.random.key(seed)
        ks = jax.random.split(key, 11)
        B, S, D = (2, 512, EMBED_DIM)
        scale = 1.0 / np.sqrt(D)
        inp = {'query': jax.random.normal(ks[0], (B, S, D), jnp.float32), 'key': jax.random.normal(ks[1], (B, S, D), jnp.float32), 'value': jax.random.normal(ks[2], (B, S, D), jnp.float32), 'Wq': jax.random.normal(ks[3], (D, D), jnp.float32) * scale, 'bq': jnp.zeros((D,), jnp.float32), 'Wk': jax.random.normal(ks[4], (D, D), jnp.float32) * scale, 'bk': jnp.zeros((D,), jnp.float32), 'Wv': jax.random.normal(ks[5], (D, D), jnp.float32) * scale, 'bv': jnp.zeros((D,), jnp.float32), 'Wo': jax.random.normal(ks[6], (D, D), jnp.float32) * scale, 'bo': jnp.zeros((D,), jnp.float32)}
        return inp
    _L3_xattn_all = _L3_xattn_setup()
    _L3_xattn_in = {k: v for k, v in _L3_xattn_all.items() if k in ('Wq', 'bq', 'Wk', 'bk', 'Wv', 'bv', 'Wo', 'bo')}
    del _L3_xattn_all

    def _L3_ffn_setup():
        import math
        import jax, jax.numpy as jnp
        import numpy as np
        CAPACITY_FACTOR = 1.25
        key = jax.random.key(seed)
        ks = jax.random.split(key, 5)
        B, S, H, F, E = (4, 1024, 256, 256, 32)
        scale_in = 1.0 / math.sqrt(H)
        scale_mid = 1.0 / math.sqrt(F)
        return {'x': jax.random.normal(ks[0], (B, S, H), dtype=jnp.float32), 'w_router': jax.random.normal(ks[1], (H, E), dtype=jnp.float32) * scale_in, 'w_gate': jax.random.normal(ks[2], (E, H, F), dtype=jnp.float32) * scale_in, 'w_up': jax.random.normal(ks[3], (E, H, F), dtype=jnp.float32) * scale_in, 'w_down': jax.random.normal(ks[4], (E, F, H), dtype=jnp.float32) * scale_mid}
    _L3_ffn_all = _L3_ffn_setup()
    _L3_ffn_in = {k: v for k, v in _L3_ffn_all.items() if k in ('w_router', 'w_gate', 'w_up', 'w_down')}
    del _L3_ffn_all
    return {'x': x, 'ctx_1024': ctx_1024, 'mask_SxS_bc0': mask_SxS_bc0, 'mask_BxSxS2_if1': mask_BxSxS2_if1, 'L0_xattn_Wq': _L0_xattn_in['Wq'], 'L0_xattn_bq': _L0_xattn_in['bq'], 'L0_xattn_Wk': _L0_xattn_in['Wk'], 'L0_xattn_bk': _L0_xattn_in['bk'], 'L0_xattn_Wv': _L0_xattn_in['Wv'], 'L0_xattn_bv': _L0_xattn_in['bv'], 'L0_xattn_gamma': _L0_xattn_in['gamma'], 'L0_xattn_beta': _L0_xattn_in['beta'], 'L0_ffn_gate_w': _L0_ffn_in['gate_w'], 'L0_ffn_experts_gate_up': _L0_ffn_in['experts_gate_up'], 'L0_ffn_experts_down': _L0_ffn_in['experts_down'], 'L0_ffn_shared_gate_w': _L0_ffn_in['shared_gate_w'], 'L0_ffn_shared_up_w': _L0_ffn_in['shared_up_w'], 'L0_ffn_shared_down_w': _L0_ffn_in['shared_down_w'], 'L0_ffn_shared_expert_gate_w': _L0_ffn_in['shared_expert_gate_w'], 'L1_xattn_Wq': _L1_xattn_in['Wq'], 'L1_xattn_Wk': _L1_xattn_in['Wk'], 'L1_xattn_Wv': _L1_xattn_in['Wv'], 'L1_xattn_hist_W': _L1_xattn_in['hist_W'], 'L1_xattn_hist_b': _L1_xattn_in['hist_b'], 'L1_xattn_hist_ln_g': _L1_xattn_in['hist_ln_g'], 'L1_xattn_hist_ln_b': _L1_xattn_in['hist_ln_b'], 'L1_xattn_ctx_W1': _L1_xattn_in['ctx_W1'], 'L1_xattn_ctx_b1': _L1_xattn_in['ctx_b1'], 'L1_xattn_ctx_W2': _L1_xattn_in['ctx_W2'], 'L1_xattn_ctx_b2': _L1_xattn_in['ctx_b2'], 'L1_xattn_kg_W1': _L1_xattn_in['kg_W1'], 'L1_xattn_kg_b1': _L1_xattn_in['kg_b1'], 'L1_xattn_kg_ln_g': _L1_xattn_in['kg_ln_g'], 'L1_xattn_kg_ln_b': _L1_xattn_in['kg_ln_b'], 'L1_xattn_kg_W2': _L1_xattn_in['kg_W2'], 'L1_xattn_kg_b2': _L1_xattn_in['kg_b2'], 'L1_xattn_proj_W': _L1_xattn_in['proj_W'], 'L1_xattn_proj_b': _L1_xattn_in['proj_b'], 'L1_ffn_Wg': _L1_ffn_in['Wg'], 'L1_ffn_bg': _L1_ffn_in['bg'], 'L1_ffn_W1': _L1_ffn_in['W1'], 'L1_ffn_b1': _L1_ffn_in['b1'], 'L1_ffn_W2': _L1_ffn_in['W2'], 'L1_ffn_b2': _L1_ffn_in['b2'], 'L2_xattn_Wq': _L2_xattn_in['Wq'], 'L2_xattn_bq': _L2_xattn_in['bq'], 'L2_xattn_Wk': _L2_xattn_in['Wk'], 'L2_xattn_bk': _L2_xattn_in['bk'], 'L2_xattn_Wv': _L2_xattn_in['Wv'], 'L2_xattn_bv': _L2_xattn_in['bv'], 'L2_ffn_router_w0': _L2_ffn_in['router_w0'], 'L2_ffn_wg0': _L2_ffn_in['wg0'], 'L2_ffn_wu0': _L2_ffn_in['wu0'], 'L2_ffn_wd0': _L2_ffn_in['wd0'], 'L2_ffn_router_w1': _L2_ffn_in['router_w1'], 'L2_ffn_wg1': _L2_ffn_in['wg1'], 'L2_ffn_wu1': _L2_ffn_in['wu1'], 'L2_ffn_wd1': _L2_ffn_in['wd1'], 'L3_xattn_Wq': _L3_xattn_in['Wq'], 'L3_xattn_bq': _L3_xattn_in['bq'], 'L3_xattn_Wk': _L3_xattn_in['Wk'], 'L3_xattn_bk': _L3_xattn_in['bk'], 'L3_xattn_Wv': _L3_xattn_in['Wv'], 'L3_xattn_bv': _L3_xattn_in['bv'], 'L3_xattn_Wo': _L3_xattn_in['Wo'], 'L3_xattn_bo': _L3_xattn_in['bo'], 'L3_ffn_w_router': _L3_ffn_in['w_router'], 'L3_ffn_w_gate': _L3_ffn_in['w_gate'], 'L3_ffn_w_up': _L3_ffn_in['w_up'], 'L3_ffn_w_down': _L3_ffn_in['w_down']}

def reference(x, ctx_1024, mask_SxS_bc0, mask_BxSxS2_if1, L0_xattn_Wq, L0_xattn_bq, L0_xattn_Wk, L0_xattn_bk, L0_xattn_Wv, L0_xattn_bv, L0_xattn_gamma, L0_xattn_beta, L0_ffn_gate_w, L0_ffn_experts_gate_up, L0_ffn_experts_down, L0_ffn_shared_gate_w, L0_ffn_shared_up_w, L0_ffn_shared_down_w, L0_ffn_shared_expert_gate_w, L1_xattn_Wq, L1_xattn_Wk, L1_xattn_Wv, L1_xattn_hist_W, L1_xattn_hist_b, L1_xattn_hist_ln_g, L1_xattn_hist_ln_b, L1_xattn_ctx_W1, L1_xattn_ctx_b1, L1_xattn_ctx_W2, L1_xattn_ctx_b2, L1_xattn_kg_W1, L1_xattn_kg_b1, L1_xattn_kg_ln_g, L1_xattn_kg_ln_b, L1_xattn_kg_W2, L1_xattn_kg_b2, L1_xattn_proj_W, L1_xattn_proj_b, L1_ffn_Wg, L1_ffn_bg, L1_ffn_W1, L1_ffn_b1, L1_ffn_W2, L1_ffn_b2, L2_xattn_Wq, L2_xattn_bq, L2_xattn_Wk, L2_xattn_bk, L2_xattn_Wv, L2_xattn_bv, L2_ffn_router_w0, L2_ffn_wg0, L2_ffn_wu0, L2_ffn_wd0, L2_ffn_router_w1, L2_ffn_wg1, L2_ffn_wu1, L2_ffn_wd1, L3_xattn_Wq, L3_xattn_bq, L3_xattn_Wk, L3_xattn_bk, L3_xattn_Wv, L3_xattn_bv, L3_xattn_Wo, L3_xattn_bo, L3_ffn_w_router, L3_ffn_w_gate, L3_ffn_w_up, L3_ffn_w_down):
    import jax
    import jax.numpy as jnp

    def _L0_xattn_ref(query, key_in, value, Wq, bq, Wk, bk, Wv, bv, gamma, beta):
        import jax, jax.numpy as jnp
        import numpy as np
        LN_EPS = 1e-05
        q = jnp.einsum('bsd,df->bsf', query, Wq) + bq
        k = jnp.einsum('bsd,df->bsf', key_in, Wk) + bk
        v = jnp.einsum('bsd,df->bsf', value, Wv) + bv
        attn = jnp.einsum('bqd,bkd->bqk', q, k)
        probs = jax.nn.softmax(attn, axis=-1)
        result = jnp.einsum('bqk,bkd->bqd', probs, v)
        x = result + query
        mu = jnp.mean(x, axis=-1, keepdims=True)
        var = jnp.mean((x - mu) ** 2, axis=-1, keepdims=True)
        return (x - mu) * jax.lax.rsqrt(var + LN_EPS) * gamma + beta

    def _L0_ffn_ref(x, gate_w, experts_gate_up, experts_down, shared_gate_w, shared_up_w, shared_down_w, shared_expert_gate_w):
        import jax, jax.numpy as jnp
        import numpy as np
        HIDDEN_SIZE = 256
        NUM_EXPERTS = 8
        MOE_INTERMEDIATE_SIZE = 352
        NUM_EXPERTS_PER_TOK = 2
        SHARED_EXPERT_INTERMEDIATE_SIZE = 704
        B, T = (2, 256)
        W_SCALE = 0.02
        Bx, Tx, H = x.shape
        E = gate_w.shape[0]
        I = experts_down.shape[2]
        x_flat = x.reshape(Bx * Tx, H)
        logits = x_flat @ gate_w.T
        scores = jax.nn.softmax(logits, axis=-1)
        _, topk_ids = jax.lax.top_k(scores, NUM_EXPERTS_PER_TOK)
        in_topk = jax.nn.one_hot(topk_ids, E, dtype=x.dtype).sum(axis=1)
        w = scores * in_topk
        gu = jnp.einsum('nh,eih->nei', x_flat, experts_gate_up)
        g, u = (gu[..., :I], gu[..., I:])
        h = jax.nn.silu(g) * u
        expert_out = jnp.einsum('nei,ehi->neh', h, experts_down)
        out = jnp.einsum('neh,ne->nh', expert_out, w)
        shared = jax.nn.silu(x_flat @ shared_gate_w.T) * (x_flat @ shared_up_w.T) @ shared_down_w.T
        shared_weight = jax.nn.sigmoid(x_flat @ shared_expert_gate_w.T)
        out = out + shared_weight * shared
        return out.reshape(Bx, Tx, H)

    def _L1_xattn_ref(x, historical_data, Wq, Wk, Wv, hist_W, hist_b, hist_ln_g, hist_ln_b, ctx_W1, ctx_b1, ctx_W2, ctx_b2, kg_W1, kg_b1, kg_ln_g, kg_ln_b, kg_W2, kg_b2, proj_W, proj_b, causal_mask):
        import jax, jax.numpy as jnp
        import numpy as np
        from jax import lax
        H = 16
        K1, K2 = (3, 3)
        LN_EPS = 1e-05

        def _ln(x, g, b):
            m = jnp.mean(x, axis=-1, keepdims=True)
            v = jnp.mean(jnp.square(x - m), axis=-1, keepdims=True)
            return (x - m) * lax.rsqrt(v + LN_EPS) * g + b

        def _gelu(x):
            return jax.nn.gelu(x, approximate=False)
        B, T, D = x.shape
        hd = D // H
        scale = hd ** (-0.5)
        q = (x @ Wq).reshape(B, T, H, hd).transpose(0, 2, 1, 3)
        k = (x @ Wk).reshape(B, T, H, hd).transpose(0, 2, 1, 3)
        v = (x @ Wv).reshape(B, T, H, hd).transpose(0, 2, 1, 3)
        attn = jnp.einsum('bhqd,bhkd->bhqk', q, k) * scale
        eh = _gelu(_ln(historical_data @ hist_W + hist_b, hist_ln_g, hist_ln_b))
        aw = _gelu(eh @ ctx_W1 + ctx_b1) @ ctx_W2 + ctx_b2
        aw = jax.nn.softmax(aw, axis=1)
        cc = jnp.sum(eh * aw, axis=1)
        kp = _gelu(_ln(cc @ kg_W1 + kg_b1, kg_ln_g, kg_ln_b)) @ kg_W2 + kg_b2
        kernels = jax.nn.softmax(kp.reshape(B, H, K1 * K2), axis=-1)
        kernels = kernels.reshape(B * H, 1, K1, K2)
        mask = causal_mask[None, None]
        attn0 = jnp.where(mask, 0.0, attn).reshape(1, B * H, T, T)
        attn = lax.conv_general_dilated(attn0, kernels, window_strides=(1, 1), padding=((K1 // 2, K1 // 2), (K2 // 2, K2 // 2)), feature_group_count=B * H, dimension_numbers=('NCHW', 'OIHW', 'NCHW')).reshape(B, H, T, T)
        attn = jnp.where(mask, -jnp.inf, attn)
        p = jax.nn.softmax(attn, axis=-1)
        out = jnp.einsum('bhqk,bhkd->bhqd', p, v)
        out = out.transpose(0, 2, 1, 3).reshape(B, T, D)
        return out @ proj_W + proj_b

    def _L1_ffn_ref(x, Wg, bg, W1, b1, W2, b2):
        import jax, jax.numpy as jnp
        import numpy as np
        D_MODEL = 256
        D_HIDDEN = 1024
        NUM_EXPERTS = 8
        B, T = (2, 512)
        gate_logits = jnp.einsum('btd,de->bte', x, Wg) + bg
        gate_scores = jax.nn.softmax(gate_logits, axis=-1)
        top1_idx = jnp.argmax(gate_scores, axis=-1)
        top1_mask = jax.nn.one_hot(top1_idx, NUM_EXPERTS, dtype=x.dtype)
        top1_weight = jnp.sum(gate_scores * top1_mask, axis=-1, keepdims=True)
        h = jax.nn.silu(jnp.einsum('btd,edh->bteh', x, W1) + b1)
        o = jnp.einsum('bteh,ehd->bted', h, W2) + b2
        y = jnp.sum(o * top1_mask[..., None], axis=2) * top1_weight
        return y

    def _L2_xattn_ref(query, key, value, mask, Wq, bq, Wk, bk, Wv, bv):
        import jax, jax.numpy as jnp
        import numpy as np
        B, S, D, H = (4, 512, 256, 16)
        DK = D // H

        def _split_heads(x):
            b, s, _ = x.shape
            return x.reshape(b, s, H, DK).transpose(0, 2, 1, 3)
        q = _split_heads(query @ Wq.T + bq)
        k = _split_heads(key @ Wk.T + bk)
        v = _split_heads(value @ Wv.T + bv)
        scores = jnp.einsum('bhqd,bhkd->bhqk', q, k) / np.sqrt(DK).astype(jnp.float32)
        scores = jnp.where(mask[:, None, :, :] == 0, jnp.float32(-1000000000.0), scores)
        p_attn = jax.nn.softmax(scores, axis=-1)
        x = jnp.einsum('bhqk,bhkd->bhqd', p_attn, v)
        return x.transpose(0, 2, 1, 3).reshape(query.shape[0], -1, H * DK)

    def _L2_ffn_ref(x, router_w0, wg0, wu0, wd0, router_w1, wg1, wu1, wd1):
        import jax, jax.numpy as jnp
        from jax import lax
        import numpy as np
        D_MODEL = 256
        HIDDEN = 128
        N_EXPERTS = 32
        TOP_K = 2
        B, S = (1, 1024)

        def _moe_group(x2, router_w, wg, wu, wd, top_k):
            T = x2.shape[0]
            n_experts = router_w.shape[1]
            logits = x2 @ router_w
            scores = jax.nn.softmax(logits, axis=-1)
            expert_weights, expert_indices = lax.top_k(scores, top_k)
            flat_e = expert_indices.reshape(-1)
            flat_w = expert_weights.reshape(-1)
            flat_t = jnp.repeat(jnp.arange(T), top_k)
            order = jnp.argsort(flat_e)
            tok = flat_t[order]
            xs = x2[tok]
            group_sizes = jnp.bincount(flat_e, length=n_experts).astype(jnp.int32)
            gate = lax.ragged_dot(xs, wg, group_sizes)
            up = lax.ragged_dot(xs, wu, group_sizes)
            ys = lax.ragged_dot(jax.nn.silu(gate) * up, wd, group_sizes)
            ys = ys * flat_w[order][:, None]
            return jnp.zeros_like(x2).at[tok].add(ys)
        b, s, d = x.shape
        x2 = x.reshape(-1, d)
        out0 = _moe_group(x2, router_w0, wg0, wu0, wd0, TOP_K)
        out1 = _moe_group(x2, router_w1, wg1, wu1, wd1, TOP_K)
        out = (out0 * TOP_K + out1 * TOP_K) / (TOP_K + TOP_K)
        return out.reshape(b, s, d)

    def _L3_xattn_ref(query, key, value, Wq, bq, Wk, bk, Wv, bv, Wo, bo):
        import jax, jax.numpy as jnp
        import numpy as np
        EMBED_DIM = 256
        NUM_HEADS = 16
        HEAD_DIM = EMBED_DIM // NUM_HEADS
        B, S, D = query.shape
        H, Hd = (NUM_HEADS, HEAD_DIM)

        def split_heads(x):
            return x.reshape(B, S, H, Hd).transpose(0, 2, 1, 3)
        Q = split_heads(query @ Wq.T + bq)
        K = split_heads(key @ Wk.T + bk)
        V = split_heads(value @ Wv.T + bv)
        scores = jnp.einsum('bhqd,bhkd->bhqk', Q, K) / np.sqrt(Hd).astype(jnp.float32)
        attn = jax.nn.softmax(scores, axis=-1)
        out = jnp.einsum('bhqk,bhkd->bhqd', attn, V)
        out = out.transpose(0, 2, 1, 3).reshape(B, S, D)
        return out @ Wo.T + bo

    def _L3_ffn_ref(x, w_router, w_gate, w_up, w_down):
        import math
        import jax, jax.numpy as jnp
        import numpy as np
        CAPACITY_FACTOR = 1.25
        B, S, H = x.shape
        E = w_gate.shape[0]
        T = B * S
        C = int(math.ceil(CAPACITY_FACTOR * T / E))
        xt = x.reshape(T, H)
        logits = xt @ w_router
        probs = jax.nn.softmax(logits, axis=-1)
        top1 = jnp.argmax(probs, axis=-1)
        gate = jnp.take_along_axis(probs, top1[:, None], axis=1)[:, 0]
        onehot = jax.nn.one_hot(top1, E, dtype=jnp.int32)
        pos = jnp.cumsum(onehot, axis=0)[jnp.arange(T), top1] - 1
        accepted = pos < C
        slot = jnp.where(accepted, top1 * C + pos, E * C)
        buf = jnp.zeros((E * C + 1, H), dtype=x.dtype).at[slot].set(xt)
        buf = buf[:E * C].reshape(E, C, H)
        g = jnp.einsum('ech,ehf->ecf', buf, w_gate)
        u = jnp.einsum('ech,ehf->ecf', buf, w_up)
        y = jnp.einsum('ecf,efh->ech', jax.nn.silu(g) * u, w_down)
        out_tok = y.reshape(E * C, H)[jnp.clip(slot, 0, E * C - 1)]
        out_tok = jnp.where(accepted[:, None], out_tok * gate[:, None], 0.0)
        return (xt + out_tok).reshape(B, S, H)
    x = x + _L0_xattn_ref(_layernorm(x, axis=-1), ctx_1024, ctx_1024, L0_xattn_Wq, L0_xattn_bq, L0_xattn_Wk, L0_xattn_bk, L0_xattn_Wv, L0_xattn_bv, L0_xattn_gamma, L0_xattn_beta)
    x = x + _L0_ffn_ref(_layernorm(x, axis=-1), L0_ffn_gate_w, L0_ffn_experts_gate_up, L0_ffn_experts_down, L0_ffn_shared_gate_w, L0_ffn_shared_up_w, L0_ffn_shared_down_w, L0_ffn_shared_expert_gate_w)
    x = x + _L1_xattn_ref(_layernorm(x, axis=-1), ctx_1024, L1_xattn_Wq, L1_xattn_Wk, L1_xattn_Wv, L1_xattn_hist_W, L1_xattn_hist_b, L1_xattn_hist_ln_g, L1_xattn_hist_ln_b, L1_xattn_ctx_W1, L1_xattn_ctx_b1, L1_xattn_ctx_W2, L1_xattn_ctx_b2, L1_xattn_kg_W1, L1_xattn_kg_b1, L1_xattn_kg_ln_g, L1_xattn_kg_ln_b, L1_xattn_kg_W2, L1_xattn_kg_b2, L1_xattn_proj_W, L1_xattn_proj_b, mask_SxS_bc0)
    x = x + _L1_ffn_ref(_layernorm(x, axis=-1), L1_ffn_Wg, L1_ffn_bg, L1_ffn_W1, L1_ffn_b1, L1_ffn_W2, L1_ffn_b2)
    x = x + _L2_xattn_ref(_layernorm(x, axis=-1), ctx_1024, ctx_1024, mask_BxSxS2_if1, L2_xattn_Wq, L2_xattn_bq, L2_xattn_Wk, L2_xattn_bk, L2_xattn_Wv, L2_xattn_bv)
    x = x + _L2_ffn_ref(_layernorm(x, axis=-1), L2_ffn_router_w0, L2_ffn_wg0, L2_ffn_wu0, L2_ffn_wd0, L2_ffn_router_w1, L2_ffn_wg1, L2_ffn_wu1, L2_ffn_wd1)
    x = x + _L3_xattn_ref(_layernorm(x, axis=-1), ctx_1024, ctx_1024, L3_xattn_Wq, L3_xattn_bq, L3_xattn_Wk, L3_xattn_bk, L3_xattn_Wv, L3_xattn_bv, L3_xattn_Wo, L3_xattn_bo)
    x = x + _L3_ffn_ref(_layernorm(x, axis=-1), L3_ffn_w_router, L3_ffn_w_gate, L3_ffn_w_up, L3_ffn_w_down)
    return x

_drawn_inputs = setup_inputs


def setup_inputs(seed=0):
    import zlib

    import numpy as np

    out = dict(_drawn_inputs(seed))
    spreads = {'L0_xattn_gamma': (1.0, 0.2),
     'L0_xattn_beta': (0.0, 0.1),
     'L1_xattn_hist_b': (0.0, 2.0),
     'L1_xattn_hist_ln_g': (1.0, 0.6),
     'L1_xattn_hist_ln_b': (0.0, 2.0),
     'L1_xattn_ctx_b1': (0.0, 2.0),
     'L1_xattn_kg_b1': (0.0, 2.0),
     'L1_xattn_kg_ln_g': (1.0, 0.6),
     'L1_xattn_kg_ln_b': (0.0, 2.0),
     'L1_xattn_kg_b2': (0.0, 2.0),
     'L1_xattn_proj_b': (0.0, 0.407),
     'L1_ffn_bg': (0.0, 0.8),
     'L1_ffn_b1': (0.0, 0.8),
     'L1_ffn_b2': (0.0, 0.739),
     'L2_xattn_bq': (0.0, 2.0),
     'L2_xattn_bk': (0.0, 2.0),
     'L2_xattn_bv': (0.0, 0.55),
     'L3_xattn_bq': (0.0, 2.0),
     'L3_xattn_bk': (0.0, 2.0),
     'L3_xattn_bv': (0.0, 0.8),
     'L3_xattn_bo': (0.0, 0.8)}
    factors = {'L0_xattn_bk': 64.0,
     'L0_ffn_gate_w': 8.0,
     'L0_ffn_experts_gate_up': 8.0,
     'L0_ffn_experts_down': 8.0,
     'L0_ffn_shared_gate_w': 7.264,
     'L0_ffn_shared_up_w': 7.452,
     'L0_ffn_shared_down_w': 7.29,
     'L0_ffn_shared_expert_gate_w': 8.0,
     'L1_xattn_hist_W': 23.115,
     'L1_xattn_ctx_W1': 37.339,
     'L1_xattn_ctx_W2': 35.629,
     'L1_xattn_kg_W1': 15.493,
     'L1_xattn_kg_W2': 12.662,
     'L1_ffn_Wg': 4.022,
     'L1_ffn_W1': 5.077,
     'L1_ffn_W2': 4.851,
     'L2_ffn_router_w0': 8.0,
     'L2_ffn_wg0': 8.0,
     'L2_ffn_wu0': 8.0,
     'L2_ffn_wd0': 8.0,
     'L2_ffn_router_w1': 8.0,
     'L2_ffn_wg1': 8.0,
     'L2_ffn_wu1': 8.0,
     'L2_ffn_wd1': 8.0,
     'L1_xattn_Wq': 2.956,
     'L1_xattn_Wk': 3.309,
     'L3_xattn_Wq': 3.376,
     'L3_xattn_Wk': 2.831,
     'L3_ffn_w_router': 8.0,
     'L3_ffn_w_gate': 8.0,
     'L3_ffn_w_up': 7.878,
     'L3_ffn_w_down': 7.89}
    for name, (base, spread) in spreads.items():
        noise = np.random.default_rng([zlib.crc32(name.encode()), seed]).standard_normal(out[name].shape)
        drawn = base * np.exp(spread * noise) if base else spread * noise
        out[name] = jnp.asarray(drawn.astype(out[name].dtype))
    for name, factor in factors.items():
        out[name] = (out[name] * factor).astype(out[name].dtype)
    return out
```

```python
from contextlib import ExitStack

import concourse.bass as bass
from concourse import mybir

F32 = mybir.dt.float32
BF16 = mybir.dt.bfloat16
I32 = mybir.dt.int32
U32 = mybir.dt.uint32
U8 = mybir.dt.uint8
ALU = mybir.AluOpType
ACT = mybir.ActivationFunctionType
X = mybir.AxisListType.X

P = 128
B, SEQ, D = 8, 256, 256
TILES = B * SEQ // P
DC = D // P
QC = SEQ // P
HEADS, HD = 16, 16
GROUPS = 4
GH = HEADS // GROUPS
LANE = 32
NEG_BIG = -1.0e30
LN_EPS = 1e-5
TAPS = 3
MOST_TILES = 64


class Steps:

    def __init__(self, engine, semaphore):
        self.engine, self.semaphore, self.n = engine, semaphore, 0

    def done(self, instruction):
        instruction.then_inc(self.semaphore, 1)
        self.n = self.n + 1
        self.engine.wait_ge(self.semaphore, self.n)


class Core:

    def __init__(self, nc, whole):
        self.nc, self.whole = nc, whole

    def keep(self, name, shape, dtype=F32):
        return self.whole.enter_context(self.nc.sbuf_tensor(name, shape, dtype))


class Stage:

    def __init__(self, core, name):
        self.core, self.name, self.nc = core, name, core.nc
        self.stack = ExitStack()
        self.sems = []

    def __enter__(self):
        return self

    def __exit__(self, *error):
        self.stack.__exit__(*error)
        if error[0] is None:
            self.nc.clear_and_free_semaphores(self.sems)
            self.nc.all_engine_barrier()

    def sb(self, name, shape, dtype=F32):
        return self.stack.enter_context(self.nc.sbuf_tensor(f"{self.name}_{name}", shape, dtype))

    def psum(self, name, shape, dtype=F32):
        return self.stack.enter_context(self.nc.psum_tensor(f"{self.name}_{name}", shape, dtype))

    def sem(self, name):
        self.sems.append(self.nc.alloc_semaphore(f"{self.name}_{name}"))
        return self.sems[-1]

    def block(self):
        return self.stack.enter_context(self.nc.Block())


def dyn(index, size=P):
    return bass.ds(index * size, size)



def row_statistics(v, steps, src, st, mean, rstd, work, stats_done, var_ready, std_ready):
    with v.Fori(0, TILES) as t:
        v.bn_stats(st[:, t, :], src[:, t, :]).then_inc(stats_done, 1)
    v.wait_ge(stats_done, TILES)
    me, mo, se, so = st[:, :, 1], st[:, :, 4], st[:, :, 2], st[:, :, 5]
    v.tensor_tensor(mean[:, :], me, mo, ALU.add)
    v.tensor_tensor(work[:, 0, :], me, mo, ALU.subtract)
    steps.done(v.tensor_tensor(work[:, 1, :], se, so, ALU.add))
    v.tensor_scalar(mean[:, :], mean[:, :], 0.5, None, ALU.mult)
    v.tensor_scalar(work[:, 1, :], work[:, 1, :], 1.0 / D, LN_EPS, ALU.mult, ALU.add)
    steps.done(v.scalar_tensor_tensor(work[:, 2, :], work[:, 0, :], 0.25, work[:, 0, :],
                                      ALU.mult, ALU.mult))
    v.tensor_tensor(work[:, 3, :], work[:, 1, :], work[:, 2, :], ALU.add).then_inc(var_ready, 1)
    v.wait_ge(std_ready, 1)
    steps.done(v.reciprocal(rstd[:, :], work[:, 4, :]))


def norm_stage(core, name, x, xn, xnT, ident, router=None, logits=None):
    nc = core.nc
    with Stage(core, name) as s:
        st = s.sb("st", [P, TILES, 6])
        mean = s.sb("mean", [P, TILES])
        rstd = s.sb("rstd", [P, TILES])
        work = s.sb("work", [P, 5, TILES])
        row = s.sb("row", [P, 4, D])
        ps_t = s.psum("ps_t", [P, 2, 512])
        stats_done, var_ready, std_ready = s.sem("stats_done"), s.sem("var_ready"), s.sem("std_ready")
        own = s.sem("own")
        row_ready, row_copied = s.sem("row_ready"), s.sem("row_copied")
        turned, tile_free = s.sem("turned"), s.sem("tile_free")
        if router is not None:
            E = router.shape[1] // DC
            w = s.sb("router", [P, DC, E])
            colT = s.sb("colT", [P, 4, DC, P])
            ps_l = s.psum("ps_l", [P, TILES, E])
            w_loaded, col_ready, logits_ready = s.sem("w_loaded"), s.sem("col_ready"), s.sem("logits_ready")
        block = s.block()

        @block.sync
        def _(sp):
            if router is not None:
                sp.dma_start(w[:, :, :], router.rearrange("p (c e) -> p c e", c=DC)).then_inc(w_loaded, 16)

        @block.vector
        def _(v):
            steps = Steps(v, own)
            row_statistics(v, steps, x, st, mean, rstd, work, stats_done, var_ready, std_ready)
            with v.Fori(0, TILES // 4) as i:
                for p in range(4):
                    t = 4 * i + p
                    v.wait_ge(turned, t + 1)
                    v.wait_ge(row_copied, t + 1)
                    v.tensor_scalar(row[:, p, :], x[:, t, :], mean[:, bass.ds(t, 1)], rstd[:, bass.ds(t, 1)],
                                    ALU.subtract, ALU.mult).then_inc(row_ready, 1)
            if router is not None:
                v.wait_ge(logits_ready, TILES + 4)
                v.tensor_copy(logits[:, :, 0:E], ps_l[:, :, :])

        @block.gpsimd
        def _(pool):
            pool.sem_inc(row_copied, 4)
            with pool.Fori(0, TILES // 4) as i:
                for p in range(4):
                    t = 4 * i + p
                    pool.wait_ge(row_ready, t + 1)
                    pool.tensor_copy(xn[:, t, :], row[:, p, :]).then_inc(row_copied, 1)

        @block.scalar
        def _(act):
            act.sem_inc(tile_free, 2)
            act.wait_ge(var_ready, 1)
            act.activation(work[:, 4, :], work[:, 3, :], ACT.Sqrt).then_inc(std_ready, 1)
            with act.Fori(0, TILES // 4) as i:
                for p in range(4):
                    t = 4 * i + p
                    act.wait_ge(turned, t + 5)
                    tile_T = ps_t[:, p % 2, 0:D].rearrange("p (c n) -> p c n", c=DC)
                    if router is not None:
                        act.wait_ge(logits_ready, t + 1)
                        act.copy(colT[:, p, :, :], tile_T).then_inc(col_ready, 1)
                    act.copy(xnT[:, :, dyn(t)], tile_T).then_inc(tile_free, 1)

        @block.tensor
        def _(pe):
            pe.sem_inc(turned, 4)
            if router is not None:
                pe.sem_inc(logits_ready, 4)
                pe.wait_ge(w_loaded, 16)

            def turn(i, p):
                t = 4 * i + p
                pe.wait_ge(row_ready, t + 1)
                pe.wait_ge(tile_free, t + 1)
                for c in range(DC):
                    last = pe.transpose(ps_t[:, p % 2, c * P:(c + 1) * P], row[:, p, c * P:(c + 1) * P], ident[:, :])
                last.then_inc(turned, 1)

            def route(i, p):
                t = 4 * i + p
                pe.wait_ge(col_ready, t + 1)
                for c in range(DC):
                    last = pe.matmul(ps_l[:, t, :], colT[:, p, c, :], w[:, c, :],
                                     start=(c == 0), stop=(c == DC - 1), skip_group_check=True)
                last.then_inc(logits_ready, 1)

            with pe.Fori(0, TILES // 4) as i:
                for step in range(5):
                    if step < 4:
                        turn(i, step)
                    if step >= 1 and router is not None:
                        route(i, step - 1)



def single_head_stage(core, name, xn, xnT, ctxT, w_dram, ident, ones):
    nc = core.nc
    W3 = 3 * DC * D
    with Stage(core, name) as s:
        w = s.sb("w", [P, W3 + 2 * DC + D])
        wq, wk, wv = (w[:, n * DC * D:(n + 1) * DC * D].rearrange("p (c n) -> p c n", c=DC) for n in range(3))
        bq, bk, bv = w[:, W3:W3 + DC], w[:, W3 + DC:W3 + 2 * DC], w[0:1, W3 + 2 * DC:]
        ctx = s.sb("ctx", [P, 2, DC, SEQ])
        qT, kT, vv = s.sb("qT", [P, DC, SEQ]), s.sb("kT", [P, DC, SEQ]), s.sb("v", [P, QC, D])
        probs, probsT = s.sb("probs", [P, QC, SEQ]), s.sb("probsT", [P, QC, SEQ])
        negmax, total, inv = s.sb("negmax", [P, QC]), s.sb("total", [P, QC]), s.sb("inv", [P, QC])
        ps_q, ps_k, ps_v, ps_s, ps_pT, ps_o = (s.psum(n, [P, 2, D]) for n in
                                               ("ps_q", "ps_k", "ps_v", "ps_s", "ps_pT", "ps_o"))
        w_loaded, ctx_loaded = s.sem("w_loaded"), [s.sem("ctx_loaded0"), s.sem("ctx_loaded1")]
        projected, q_ready, k_ready, v_ready = (s.sem(n) for n in ("projected", "q_ready", "k_ready", "v_ready"))
        scored, max_ready, probs_ready = s.sem("scored"), s.sem("max_ready"), s.sem("probs_ready")
        turned, probsT_ready, mixed, added, own = (s.sem(n) for n in
                                                   ("turned", "probsT_ready", "mixed", "added", "own"))
        block = s.block()

        @block.sync
        def _(sp):
            sp.dma_start(w[:, :], w_dram).then_inc(w_loaded, 16)
            with sp.Fori(0, B // 2) as i:
                for p in range(2):
                    b = 2 * i + p
                    sp.wait_ge(projected, 3 * b + 3)
                    sp.dma_start(ctx[:, p, :, :].rearrange("p c n -> p (c n)"), ctxT[dyn(b), :])\
                        .then_inc(ctx_loaded[p], 16)

        @block.tensor
        def _(pe):
            pe.sem_inc(projected, 6)
            pe.wait_ge(w_loaded, 16)
            with pe.Fori(0, B // 2) as i:
                for p in range(2):
                    b = 2 * i + p
                    for oc in range(DC):
                        for c in range(DC):
                            last = pe.matmul(ps_q[:, oc, :], wq[:, c, oc * P:(oc + 1) * P],
                                             xnT[:, c, dyn(b, SEQ)], start=(c == 0), stop=(c == DC - 1))
                    last.then_inc(projected, 1)
                    pe.wait_ge(ctx_loaded[p], 16 * (i + 1))
                    for oc in range(DC):
                        for c in range(DC):
                            last = pe.matmul(ps_k[:, oc, :], wk[:, c, oc * P:(oc + 1) * P],
                                             ctx[:, p, c, :], start=(c == 0), stop=(c == DC - 1))
                    last.then_inc(projected, 1)
                    for tc in range(QC):
                        for c in range(DC):
                            pe.matmul(ps_v[:, tc, :], ctx[:, p, c, tc * P:(tc + 1) * P], wv[:, c, :],
                                      start=(c == 0), stop=False)
                        last = pe.matmul(ps_v[:, tc, :], ones[0:1, 0:P], bv, start=False, stop=True)
                    last.then_inc(projected, 1)
                    pe.wait_ge(q_ready, b + 1)
                    pe.wait_ge(k_ready, b + 1)
                    for qc in range(QC):
                        for c in range(DC):
                            last = pe.matmul(ps_s[:, qc, :], qT[:, c, qc * P:(qc + 1) * P], kT[:, c, :],
                                             start=(c == 0), stop=(c == DC - 1))
                    last.then_inc(scored, 1)
                    pe.wait_ge(probs_ready, b + 1)
                    for kc in range(QC):
                        for qc in range(QC):
                            last = pe.transpose(ps_pT[:, kc, qc * P:(qc + 1) * P],
                                                probs[:, qc, kc * P:(kc + 1) * P], ident[:, :])
                    last.then_inc(turned, 1)
                    pe.wait_ge(probsT_ready, b + 1)
                    pe.wait_ge(v_ready, b + 1)
                    pe.wait_ge(added, b + 1)
                    for qc in range(QC):
                        for kc in range(QC):
                            last = pe.matmul(ps_o[:, qc, :], probsT[:, kc, qc * P:(qc + 1) * P], vv[:, kc, :],
                                             start=(kc == 0), stop=(kc == QC - 1))
                    last.then_inc(mixed, 1)

        @block.scalar
        def _(act):
            with act.Fori(0, B) as b:
                act.wait_ge(projected, 3 * b + 8)
                for c in range(DC):
                    last = act.activation(kT[:, c, :], ps_k[:, c, :], ACT.Identity, bias=bk[:, c:c + 1])
                last.then_inc(k_ready, 1)
                act.wait_ge(projected, 3 * b + 9)
                act.wait_ge(added, b + 1)
                act.copy(vv[:, :, :], ps_v[:, :, :]).then_inc(v_ready, 1)
                act.wait_ge(max_ready, b + 1)
                for qc in range(QC):
                    last = act.activation(probs[:, qc, :], ps_s[:, qc, :], ACT.Exp, bias=negmax[:, qc:qc + 1],
                                          accum_out=total[:, qc:qc + 1])
                last.then_inc(probs_ready, 1)

        @block.vector
        def _(v):
            steps = Steps(v, own)
            v.sem_inc(added, 1)
            with v.Fori(0, B) as b:
                v.wait_ge(projected, 3 * b + 7)
                for c in range(DC):
                    last = v.tensor_scalar(qT[:, c, :], ps_q[:, c, :], bq[:, c:c + 1], None, ALU.add)
                last.then_inc(q_ready, 1)
                v.wait_ge(scored, b + 1)
                v.tensor_reduce(negmax[:, :], ps_s[:, :, :], X, ALU.max, negate=True).then_inc(max_ready, 1)
                v.wait_ge(turned, b + 1)
                v.tensor_copy(probsT[:, :, :], ps_pT[:, :, :]).then_inc(probsT_ready, 1)
                steps.n = b
                steps.done(v.reciprocal(inv[:, :], total[:, :]))
                v.wait_ge(mixed, b + 1)
                for qc in range(QC):
                    last = v.scalar_tensor_tensor(xn[:, 2 * b + qc, :], ps_o[:, qc, :], inv[:, qc:qc + 1],
                                                  xn[:, 2 * b + qc, :], ALU.mult, ALU.add)
                last.then_inc(added, 1)


def post_norm_stage(core, name, x, r, gain_bias):
    with Stage(core, name) as s:
        st, mean, rstd = s.sb("st", [P, TILES, 6]), s.sb("mean", [P, TILES]), s.sb("rstd", [P, TILES])
        work = s.sb("work", [P, 5, TILES])
        row = s.sb("row", [P, 4, D])
        gb = s.sb("gb", [P, 2, D])
        stats_done, var_ready, std_ready = s.sem("stats_done"), s.sem("var_ready"), s.sem("std_ready")
        own, gb_loaded, normed = s.sem("own"), s.sem("gb_loaded"), s.sem("normed")
        scaled, row_free = s.sem("scaled"), s.sem("row_free")
        block = s.block()

        @block.sync
        def _(sp):
            sp.dma_start(gb[:, :, :], gain_bias.rearrange("(o a) n -> o a n", o=1).to_broadcast([P, 2, D]))\
                .then_inc(gb_loaded, 16)

        @block.scalar
        def _(act):
            act.wait_ge(var_ready, 1)
            act.activation(work[:, 4, :], work[:, 3, :], ACT.Sqrt).then_inc(std_ready, 1)

        @block.gpsimd
        def _(pool):
            pool.sem_inc(row_free, 4)
            pool.wait_ge(gb_loaded, 16)
            with pool.Fori(0, TILES // 4) as i:
                for p in range(4):
                    t = 4 * i + p
                    pool.wait_ge(scaled, t + 1)
                    pool.tensor_tensor(row[:, p, :], row[:, p, :], gb[:, 1, :], ALU.add).then_inc(normed, 1)
                    pool.wait_ge(normed, t + 1)
                    pool.tensor_tensor(x[:, t, :], x[:, t, :], row[:, p, :], ALU.add).then_inc(row_free, 1)
            pool.wait_ge(row_free, TILES + 4)

        @block.vector
        def _(v):
            steps = Steps(v, own)
            row_statistics(v, steps, r, st, mean, rstd, work, stats_done, var_ready, std_ready)
            v.wait_ge(gb_loaded, 16)
            start = steps.n
            with v.Fori(0, TILES // 4) as i:
                for p in range(4):
                    t = 4 * i + p
                    v.wait_ge(row_free, t + 1)
                    steps.n = start + t
                    steps.done(v.tensor_scalar(row[:, p, :], r[:, t, :], mean[:, bass.ds(t, 1)],
                                               rstd[:, bass.ds(t, 1)], ALU.subtract, ALU.mult))
                    v.tensor_tensor(row[:, p, :], row[:, p, :], gb[:, 0, :], ALU.mult).then_inc(scaled, 1)



AHEAD = 4


class Tables:

    def __init__(self, core, most_tiles):
        self.row_iota = core.keep("row_iota", [P, P])
        self.column = core.keep("column", [P, 1])
        self.before = core.keep("before", [P, P])
        self.token_id = {1: core.keep("token_id1", [P, TILES]), 2: core.keep("token_id2", [P, TILES * 2])}
        self.zeros = core.keep("zeros", [P, 64])
        self.token_of = core.keep("token_of", [P, most_tiles], U32)
        self.weights_of = core.keep("weights_of", [P, most_tiles], U32)
        self.slot_of = core.keep("slot_of", [P, TILES * 2], U32)
        self.coef = core.keep("coef", [P, TILES * 2])


def route_stage(core, name, lg, E, K, NT, tb, ones, xn, xn_dram, bias=None, capacity=None, factor=1.0):
    NK = TILES * K
    with Stage(core, name) as s:
        top, top_ix = s.sb("top", [P, TILES, 8]), s.sb("top_ix", [P, TILES, 8], U32)
        expert = s.sb("expert", [P, TILES, K])
        ex, hot, pos = (s.sb(n, [P, TILES, E]) for n in ("ex", "hot", "pos"))
        hot_k = s.sb("hot_k", [P, K, TILES, E])
        picked = s.sb("picked", [P, K, TILES, E])
        ek = s.sb("ek", [P, TILES, K])
        den = s.sb("den", [P, 2, TILES])
        earlier = s.sb("earlier", [P, TILES + 1, E])
        count_i = s.sb("count_i", [P, 2, E], I32)
        tiles_of, tiles_end, first = (s.sb(n, [P, E]) for n in ("tiles_of", "tiles_end", "first"))
        ended = s.sb("ended", [P, NT, E])
        tile_expert = s.sb("tile_expert", [P, NT])
        slot = s.sb("slot", [P, TILES, K])
        kept = s.sb("kept", [P, TILES, K])
        slot_i = s.sb("slot_i", [P, 3, NK], I32)
        lo, hi = s.sb("lo", [P, NK]), s.sb("hi", [P, NK])
        lane_hot, tile_hot = s.sb("lane_hot", [P, 2, P]), s.sb("tile_hot", [P, 2, NT])
        ps_pos, ps_all = (s.psum(n, [P, 512])[:, 0:TILES * E].rearrange("p (t e) -> p t e", e=E)
                          for n in ("ps_pos", "ps_all"))
        ps_tok = s.psum("ps_tok", [P, 512])
        own, maxed, shifted, exped = s.sem("own"), s.sem("maxed"), s.sem("shifted"), s.sem("exped")
        hot_ready, counted, perm_ready = s.sem("hot_ready"), s.sem("counted"), s.sem("perm_ready")
        perm_used, xn_stored, bias_loaded = s.sem("perm_used"), s.sem("xn_stored"), s.sem("bias_loaded")
        if bias is not None:
            bias_sb = s.sb("bias", [P, E])
        block = s.block()

        @block.sync
        def _(sp):
            if bias is not None:
                sp.dma_start(bias_sb[:, :], bias.to_broadcast([P, E])).then_inc(bias_loaded, 16)
            if xn_dram is not None:
                sp.dma_start(xn_dram.rearrange("(t p) d -> p t d", p=P), xn[:, :, :]).then_inc(xn_stored, 16)
                sp.wait_ge(xn_stored, 16)

        @block.scalar
        def _(act):
            act.wait_ge(shifted, 2)
            act.activation(ex[:, :, :], ex[:, :, :], ACT.Exp).then_inc(exped, 1)
            act.activation(ek[:, :, :], ek[:, :, :], ACT.Exp).then_inc(exped, 1)

        @block.tensor
        def _(pe):
            pe.wait_ge(hot_ready, 1)
            flat = hot[:, :, :].rearrange("p t e -> p (t e)")
            pe.matmul(ps_pos.rearrange("p t e -> p (t e)"), tb.before[:, :], flat)
            pe.matmul(ps_all.rearrange("p t e -> p (t e)"), ones[:, :], flat).then_inc(counted, 1)
            out = ps_tok[:, 0:NT]
            pe.sem_inc(perm_used, 2)
            pe.matmul(out, ones[:, :], tb.zeros[:, 0:NT], start=True, stop=False, skip_group_check=True)
            with pe.Fori(0, NK // 2) as i:
                for p in range(2):
                    pe.wait_ge(perm_ready, 2 * i + p + 1)
                    pe.matmul(out, lane_hot[:, p, :], tile_hot[:, p, :], start=False, stop=False,
                              skip_group_check=True).then_inc(perm_used, 1)
            pe.matmul(out, ones[:, :], tb.zeros[:, 0:NT], start=False, stop=True,
                      skip_group_check=True).then_inc(perm_used, 1)

        @block.vector
        def _(v):
            steps = Steps(v, own)
            over_e = lambda ap: ap.unsqueeze(2).to_broadcast([P, TILES, E])
            if bias is not None:
                v.wait_ge(bias_loaded, 16)
                steps.done(v.tensor_tensor(lg, lg, bias_sb[:, :].unsqueeze(1).to_broadcast([P, TILES, E]),
                                           ALU.add))
            for t in range(TILES):
                v.max(top[:, t, :], lg[:, t, :]).then_inc(maxed, 1)
            v.wait_ge(maxed, TILES)
            for t in range(TILES):
                v.max_index(top_ix[:, t, :], top[:, t, :], lg[:, t, :]).then_inc(maxed, 1)
            v.tensor_tensor(ex[:, :, :], lg, over_e(top[:, :, 0]), ALU.subtract).then_inc(shifted, 1)
            v.tensor_tensor(ek[:, :, :], top[:, :, 0:K], top[:, :, 0:1].to_broadcast([P, TILES, K]),
                            ALU.subtract).then_inc(shifted, 1)
            v.wait_ge(maxed, 2 * TILES)
            steps.done(v.tensor_copy(expert[:, :, :], top_ix[:, :, 0:K]))
            for k in range(K):
                last = v.tensor_tensor(hot_k[:, k, :, :],
                                       tb.row_iota[:, 0:E].unsqueeze(1).to_broadcast([P, TILES, E]),
                                       over_e(expert[:, :, k]), ALU.is_equal)
            steps.done(last)
            if K == 2:
                v.tensor_tensor(hot[:, :, :], hot_k[:, 0, :, :], hot_k[:, 1, :, :], ALU.add)\
                    .then_inc(hot_ready, 1)
            else:
                v.tensor_copy(hot[:, :, :], hot_k[:, 0, :, :]).then_inc(hot_ready, 1)
            v.wait_ge(exped, 2)
            steps.done(v.reduce_sum(den[:, 0, :], ex[:, :, :], X))
            steps.done(v.reciprocal(den[:, 1, :], den[:, 0, :]))
            coef = tb.coef[:, 0:NK].rearrange("p (t k) -> p t k", k=K)
            steps.done(v.tensor_tensor(coef, ek[:, :, :], den[:, 1, :].unsqueeze(2).to_broadcast([P, TILES, K]),
                                       ALU.mult))
            if factor != 1.0:
                steps.done(v.tensor_scalar(tb.coef[:, 0:NK], tb.coef[:, 0:NK], factor, None, ALU.mult))
            v.memset(earlier[:, 0, :], 0.0).then_inc(own, 1)
            steps.n += 1
            v.wait_ge(own, steps.n)
            v.wait_ge(counted, 1)
            for t in range(TILES):
                steps.done(v.tensor_tensor(earlier[:, t + 1, :], earlier[:, t, :], ps_all[:, t, :], ALU.add))
            steps.done(v.tensor_tensor(pos[:, :, :], ps_pos[:, :, :], earlier[:, 0:TILES, :], ALU.add))
            if capacity is None:
                steps.done(v.tensor_scalar(count_i[:, 0, :], earlier[:, TILES, :], float(P - 1), None, ALU.add))
                steps.done(v.tensor_scalar(count_i[:, 1, :], count_i[:, 0, :], 7, None, ALU.logical_shift_right))
                steps.done(v.tensor_copy(tiles_of[:, :], count_i[:, 1, :]))
                steps.done(v.tensor_tensor_scan(tiles_end[:, :], ones[:, 0:E], tiles_of[:, :], 0.0,
                                                ALU.mult, ALU.add))
                steps.done(v.tensor_tensor(first[:, :], tiles_end[:, :], tiles_of[:, :], ALU.subtract))
                steps.done(v.tensor_scalar(first[:, :], first[:, :], float(P), None, ALU.mult))
                steps.done(v.tensor_tensor(pos[:, :, :], pos[:, :, :],
                                           first[:, :].unsqueeze(1).to_broadcast([P, TILES, E]), ALU.add))
                steps.done(v.tensor_tensor(ended[:, :, :], tiles_end[:, :].unsqueeze(1).to_broadcast([P, NT, E]),
                                           tb.row_iota[:, 0:NT].unsqueeze(2).to_broadcast([P, NT, E]),
                                           ALU.is_le))
                steps.done(v.reduce_sum(tile_expert[:, :], ended[:, :, :], X))
                steps.done(v.tensor_scalar(tile_expert[:, :], tile_expert[:, :], float(E - 1), float(P),
                                           ALU.min, ALU.mult))
            else:
                steps.done(v.tensor_scalar(tile_expert[:, :], tb.row_iota[:, 0:NT], float(P), None, ALU.mult))
            v.tensor_scalar(tb.weights_of[:, 0:NT], tile_expert[:, :], tb.column[:, 0:1], None, ALU.add)
            for k in range(K):
                last = v.tensor_tensor(picked[:, k, :, :], hot_k[:, k, :, :], pos[:, :, :], ALU.mult)
            steps.done(last)
            for k in range(K):
                last = v.reduce_sum(slot[:, :, k], picked[:, k, :, :], X)
            steps.done(last)
            slots = slot[:, :, :].rearrange("p t k -> p (t k)")
            kept_k = kept[:, :, :].rearrange("p t k -> p (t k)")
            if capacity is None:
                steps.done(v.tensor_copy(slot_i[:, 0, :], slots))
                v.tensor_copy(tb.slot_of[:, 0:NK], slots)
                v.tensor_scalar(slot_i[:, 1, :], slot_i[:, 0, :], P - 1, None, ALU.bitwise_and)
                steps.done(v.tensor_scalar(slot_i[:, 2, :], slot_i[:, 0, :], 7, None, ALU.logical_shift_right))
                v.tensor_copy(lo[:, :], slot_i[:, 1, :])
                steps.done(v.tensor_copy(hi[:, :], slot_i[:, 2, :]))
            else:
                steps.done(v.tensor_scalar(kept_k, slots, float(capacity), None, ALU.is_lt))
                v.tensor_tensor(tb.coef[:, 0:NK], tb.coef[:, 0:NK], kept_k, ALU.mult)
                v.tensor_copy(lo[:, :], slots)
                steps.done(v.tensor_copy(hi[:, :], expert[:, :, :].rearrange("p t k -> p (t k)")))
                steps.done(v.tensor_scalar(slots, slots, float(capacity - 1), None, ALU.min))
                v.scalar_tensor_tensor(tb.slot_of[:, 0:NK], hi[:, :], float(capacity), slots,
                                       ALU.mult, ALU.add)
            start = steps.n
            with v.Fori(0, NK // 2) as i:
                for p in range(2):
                    n = 2 * i + p
                    v.wait_ge(perm_used, n + 1)
                    v.tensor_scalar(tile_hot[:, p, :], tb.row_iota[:, 0:NT], hi[:, bass.ds(n, 1)],
                                    tb.token_id[K][:, bass.ds(n, 1)], ALU.is_equal, ALU.mult)
                    v.tensor_scalar(lane_hot[:, p, :], tb.row_iota[:, :], lo[:, bass.ds(n, 1)], None,
                                    ALU.is_equal).then_inc(perm_ready, 1)
            v.wait_ge(perm_used, NK + 3)
            v.tensor_copy(tb.token_of[:, 0:NT], ps_tok[:, 0:NT])


def experts_stage(core, name, NT, rows, chunks, w_dram, tb, xn_dram, y_dram, ident, ones, biased=False):
    F = sum(chunks)
    NF = len(chunks)
    W = w_dram.shape[1]
    HB = -(-NF * P // 512)
    with Stage(core, name) as s:
        w = s.sb("w", [P, AHEAD, W])
        xg, xT = s.sb("xg", [P, AHEAD, D]), s.sb("xT", [P, 2, DC, P])
        x_ix, w_ix = s.sb("x_ix", [P, AHEAD, 1], U32), s.sb("w_ix", [P, AHEAD, 1], U32)
        h = s.sb("h", [P, 2, NF, rows])
        y = s.sb("y", [P, 2, D])
        ps_x = s.psum("ps_x", [P, 2, 512])
        ps_g = s.psum("ps_g", [P, 2, HB * 512])
        if not biased:
            silu = s.sb("silu", [P, 2, NF, rows])
            ps_u = s.psum("ps_u", [P, 2, HB * 512])
        ps_y = s.psum("ps_y", [P, 2, 512])
        x_in, w_in = ([s.sem(f"{n}{u}") for u in range(AHEAD)] for n in ("x_in", "w_in"))
        stored = [s.sem(f"stored{p}") for p in range(2)]
        ix_ready, ix_passed = s.sem("ix_ready"), s.sem("ix_passed")
        turned, xT_ready = s.sem("turned"), s.sem("xT_ready")
        gu_ready, silu_ready, h_ready = s.sem("gu_ready"), s.sem("silu_ready"), s.sem("h_ready")
        y_ready, y_copied = s.sem("y_ready"), s.sem("y_copied")
        block = s.block()

        gate_w = lambda p: w[:, p, 0:DC * F].rearrange("p (c f) -> p c f", c=DC)
        up_w = lambda p: w[:, p, DC * F:2 * DC * F].rearrange("p (c f) -> p c f", c=DC)
        down_at = DC * F if biased else 2 * DC * F
        down_w = lambda p: w[:, p, down_at:down_at + NF * D].rearrange("p (j n) -> p j n", j=NF)
        b1 = lambda p, j: w[:, p, down_at + NF * D + j:down_at + NF * D + j + 1]
        b2 = lambda p: w[0:1, p, down_at + NF * D + NF:down_at + NF * D + NF + D]

        @block.gpsimd
        def _(pool):
            with pool.Fori(0, NT // AHEAD) as i:
                for u in range(AHEAD):
                    j = AHEAD * i + u
                    pool.wait_ge(y_ready, j + 1)
                    pool.tensor_copy(x_ix[:, u, :], tb.token_of[:, bass.ds(j, 1)])
                    pool.tensor_copy(w_ix[:, u, :], tb.weights_of[:, bass.ds(j, 1)]).then_inc(ix_ready, 1)
                    pool.wait_ge(ix_ready, j + 1)
                    pool.sem_inc(ix_passed, 1)
                    pool.indirect_dma_start(xg[:, u, :], None, xn_dram,
                                            bass.IndirectOffsetOnAxis(ap=x_ix[:, u, :], axis=0))\
                        .then_inc(x_in[u], 16)
                    pool.indirect_dma_start(w[:, u, :], None, w_dram,
                                            bass.IndirectOffsetOnAxis(ap=w_ix[:, u, :], axis=0))\
                        .then_inc(w_in[u], 16)

        @block.tensor
        def _(pe):
            pe.sem_inc(y_ready, AHEAD)

            def turn_rows(i, u):
                pe.wait_ge(x_in[u], 16 * (i + 1))
                for c in range(DC):
                    last = pe.transpose(ps_x[:, u % 2, c * P:(c + 1) * P], xg[:, u, c * P:(c + 1) * P], ident[:, :])
                last.then_inc(turned, 1)

            def hidden_layer(i, u):
                p = u % 2
                pe.wait_ge(xT_ready, AHEAD * i + u + 1)
                pe.wait_ge(w_in[u], 16 * (i + 1))
                for ps, wt in ((ps_g, gate_w(u)),) if biased else ((ps_g, gate_w(u)), (ps_u, up_w(u))):
                    for j, m in enumerate(chunks):
                        for c in range(DC):
                            last = pe.matmul(ps[0:m, p, j * P:j * P + rows], wt[:, c, j * P:j * P + m],
                                             xT[:, p, c, 0:rows], start=(c == 0), stop=(c == DC - 1))
                last.then_inc(gu_ready, 1)

            def output_layer(i, u):
                p = u % 2
                pe.wait_ge(h_ready, AHEAD * i + u + 3)
                pe.wait_ge(y_copied, AHEAD * i + u + 1)
                for j, m in enumerate(chunks):
                    last = pe.matmul(ps_y[0:rows, p, 0:D], h[0:m, p, j, :], down_w(u)[0:m, j, :],
                                     start=(j == 0), stop=(j == NF - 1 and not biased))
                if biased:
                    last = pe.matmul(ps_y[0:rows, p, 0:D], ones[0:1, 0:rows], b2(u), start=False, stop=True)
                last.then_inc(y_ready, 1)

            with pe.Fori(0, NT // AHEAD) as i:
                for step in range(AHEAD + 2):
                    for lag, part in enumerate((turn_rows, hidden_layer, output_layer)):
                        if 0 <= step - lag < AHEAD:
                            part(i, step - lag)

        def parts():
            full = [j for j, m in enumerate(chunks) if m == P]
            if full:
                yield P, 0, len(full)
            if len(full) < NF:
                yield chunks[-1], len(full), NF

        def hidden(ps, p, m, a, b):
            return ps[0:m, p, a * P:b * P].rearrange("p (j n) -> p j n", n=P)[:, :, 0:rows]

        @block.scalar
        def _(act):
            if biased:
                act.sem_inc(h_ready, 2)

            def copy_rows(i, u):
                act.wait_ge(turned, AHEAD * i + u + 1)
                act.copy(xT[:, u % 2, :, :], ps_x[:, u % 2, 0:D].rearrange("p (c n) -> p c n", c=DC))\
                    .then_inc(xT_ready, 1)

            def nonlinear(i, u):
                p, j = u % 2, AHEAD * i + u
                act.wait_ge(gu_ready, j + 1)
                if biased:
                    act.wait_ge(y_ready, j + AHEAD - 1)
                    for c in range(NF):
                        last = act.activation(h[:, p, c, :], ps_g[:, p, c * P:c * P + rows], ACT.Silu,
                                              bias=b1(u, c))
                    last.then_inc(h_ready, 1)
                else:
                    act.wait_ge(h_ready, j + 1)
                    for m, a, b in parts():
                        last = act.activation(silu[0:m, p, a:b, :], hidden(ps_g, p, m, a, b), ACT.Silu)
                    last.then_inc(silu_ready, 1)

            with act.Fori(0, NT // AHEAD) as i:
                for step in range(AHEAD + 1):
                    if step < AHEAD:
                        copy_rows(i, step)
                    if step >= 1:
                        nonlinear(i, step - 1)

        @block.vector
        def _(v):
            if not biased:
                v.sem_inc(h_ready, 2)
            v.sem_inc(y_copied, 2)

            def multiply(i, u):
                p = u % 2
                v.wait_ge(silu_ready, AHEAD * i + u + 1)
                for m, a, b in parts():
                    last = v.tensor_tensor(h[0:m, p, a:b, :], hidden(ps_u, p, m, a, b), silu[0:m, p, a:b, :],
                                           ALU.mult)
                last.then_inc(h_ready, 1)

            def copy_out(i, u):
                v.wait_ge(y_ready, AHEAD * i + u + 1 + AHEAD)
                v.wait_ge(stored[u % 2], 16 * (AHEAD // 2 * i + u // 2 + 1))
                v.tensor_copy(y[0:rows, u % 2, :], ps_y[0:rows, u % 2, 0:D]).then_inc(y_copied, 1)

            with v.Fori(0, NT // AHEAD) as i:
                for step in range(AHEAD + 1):
                    if step < AHEAD and not biased:
                        multiply(i, step)
                    if step >= 1:
                        copy_out(i, step - 1)

        @block.sync
        def _(sp):
            for p in range(2):
                sp.sem_inc(stored[p], 16)
            with sp.Fori(0, NT // 2) as i:
                for p in range(2):
                    j = 2 * i + p
                    sp.wait_ge(y_copied, j + 3)
                    sp.dma_start(y_dram[dyn(j, rows), :], y[0:rows, p, :]).then_inc(stored[p], 16)
            for p in range(2):
                sp.wait_ge(stored[p], 16 * (NT // 2 + 1))


def combine_stage(core, name, K, tb, y_dram, x, xn=None):
    with Stage(core, name) as s:
        yg = s.sb("yg", [P, 2, K, D])
        ix = s.sb("ix", [P, 2, K], U32)
        y_in = [[s.sem(f"y_in{p}{k}") for k in range(K)] for p in range(2)]
        ix_ready, ix_passed, used, own = s.sem("ix_ready"), s.sem("ix_passed"), s.sem("used"), s.sem("own")
        block = s.block()

        @block.gpsimd
        def _(pool):
            with pool.Fori(0, TILES // 2) as i:
                for p in range(2):
                    t = 2 * i + p
                    pool.wait_ge(used, t + 1)
                    pool.tensor_copy(ix[:, p, :], tb.slot_of[:, dyn(t, K)]).then_inc(ix_ready, 1)
                    pool.wait_ge(ix_ready, t + 1)
                    pool.sem_inc(ix_passed, 1)
                    for k in range(K):
                        pool.indirect_dma_start(yg[:, p, k, :], None, y_dram,
                                                bass.IndirectOffsetOnAxis(ap=ix[:, p, k:k + 1], axis=0))\
                            .then_inc(y_in[p][k], 16)

        @block.vector
        def _(v):
            v.sem_inc(used, 2)
            if xn is not None:
                v.tensor_tensor(x[:, :, :], x[:, :, :], xn[:, :, :], ALU.add).then_inc(own, 1)
                v.wait_ge(own, 1)
            first = 1 if xn is not None else 0
            with v.Fori(0, TILES // 2) as i:
                for p in range(2):
                    t = 2 * i + p
                    for k in range(K):
                        v.wait_ge(y_in[p][k], 16 * (i + 1))
                        if k == K - 1:
                            if K == 2:
                                v.wait_ge(own, first + t + 1)
                            v.scalar_tensor_tensor(x[:, t, :], yg[:, p, k, :], tb.coef[:, bass.ds(t * K + k, 1)],
                                                   x[:, t, :], ALU.mult, ALU.add).then_inc(used, 1)
                        else:
                            v.scalar_tensor_tensor(x[:, t, :], yg[:, p, k, :], tb.coef[:, bass.ds(t * K + k, 1)],
                                                   x[:, t, :], ALU.mult, ALU.add).then_inc(own, 1)


def shared_stage(core, name, xnT, gate_logit, w_dram, x):
    F = 704
    chunks = [P] * (F // P) + [F % P]
    NF = len(chunks)
    BANKS = NF // 2

    def bank_parts(n):
        return ((P, 2 * n, 2 * n + 2),) if chunks[2 * n + 1] == P else ((P, 2 * n, 2 * n + 1),
                                                                       (chunks[-1], 2 * n + 1, 2 * n + 2))

    with Stage(core, name) as s:
        w = s.sb("w", [P, w_dram.shape[1]])
        gate_w = w[:, 0:DC * F].rearrange("p (c f) -> p c f", c=DC)
        up_w = w[:, DC * F:2 * DC * F].rearrange("p (c f) -> p c f", c=DC)
        down_w = w[:, 2 * DC * F:].rearrange("p (j n) -> p j n", j=NF)
        silu, h = s.sb("silu", [P, NF, SEQ]), s.sb("h", [P, NF, SEQ])
        share = s.sb("share", [P, TILES])
        ps_g, ps_u, ps_y = (s.psum(n, [P, m, 256]) for n, m in (("ps_g", NF), ("ps_u", NF), ("ps_y", 2)))
        w_loaded, share_ready, gu_ready, silu_ready = (s.sem(n) for n in
                                                       ("w_loaded", "share_ready", "gu_ready", "silu_ready"))
        h_ready, y_ready, added = s.sem("h_ready"), s.sem("y_ready"), s.sem("added")
        block = s.block()

        @block.sync
        def _(sp):
            sp.dma_start(w[:, :], w_dram).then_inc(w_loaded, 16)

        @block.tensor
        def _(pe):
            pe.wait_ge(w_loaded, 16)
            with pe.Fori(0, B) as b:
                for j, m in enumerate(chunks):
                    for ps, wt in ((ps_g, gate_w), (ps_u, up_w)):
                        for c in range(DC):
                            last = pe.matmul(ps[0:m, j, :], wt[:, c, j * P:j * P + m], xnT[:, c, dyn(b, SEQ)],
                                             start=(c == 0), stop=(c == DC - 1))
                    if j % 2:
                        last.then_inc(gu_ready, 1)
                pe.wait_ge(h_ready, BANKS * (b + 1))
                pe.wait_ge(added, b + 1)
                for q in range(QC):
                    for j, m in enumerate(chunks):
                        last = pe.matmul(ps_y[:, q, :], h[0:m, j, q * P:(q + 1) * P], down_w[0:m, j, :],
                                         start=(j == 0), stop=(j == NF - 1))
                last.then_inc(y_ready, 1)

        @block.scalar
        def _(act):
            act.activation(share[:, :], gate_logit, ACT.Sigmoid).then_inc(share_ready, 1)
            with act.Fori(0, B) as b:
                for n in range(BANKS):
                    act.wait_ge(gu_ready, b * BANKS + n + 1)
                    for m, j0, j1 in bank_parts(n):
                        last = act.activation(silu[0:m, j0:j1, :], ps_g[0:m, j0:j1, :], ACT.Silu)
                    last.then_inc(silu_ready, 1)

        @block.vector
        def _(v):
            v.sem_inc(added, 1)
            v.wait_ge(share_ready, 1)
            with v.Fori(0, B) as b:
                for n in range(BANKS):
                    v.wait_ge(silu_ready, b * BANKS + n + 1)
                    for m, j0, j1 in bank_parts(n):
                        last = v.tensor_tensor(h[0:m, j0:j1, :], ps_u[0:m, j0:j1, :], silu[0:m, j0:j1, :],
                                               ALU.mult)
                    last.then_inc(h_ready, 1)
                v.wait_ge(y_ready, b + 1)
                for q in range(QC):
                    t = 2 * b + q
                    last = v.scalar_tensor_tensor(x[:, t, :], ps_y[:, q, :], share[:, bass.ds(t, 1)],
                                                  x[:, t, :], ALU.mult, ALU.add)
                last.then_inc(added, 1)



GW = GH * LANE
GV = GH * HD
PAIRS = B // 2
BODY = 2 * GH
PLAIN, MASKED, CONV = range(3)


def heads_stage(core, name, mode, xnT, ctxT, w_dram, dst, ident, mask=None, ident16=None, kernels=None,
                ones=None):
    WQ, WK, WV = DC * GW, 2 * DC * GW, 2 * DC * GW + DC * GV
    conv = mode == CONV
    with Stage(core, name) as s:
        w = s.sb("w", [P, 2, w_dram.shape[1]])
        ctx = s.sb("ctx", [P, 2, DC, SEQ])
        qT, kT, vv = s.sb("qT", [P, 2, SEQ]), s.sb("kT", [P, 2, SEQ]), s.sb("v", [P, 2, QC, GV])
        probs, probsT = s.sb("probs", [P, 2, QC, SEQ]), s.sb("probsT", [P, 2, QC, SEQ])
        negmax = s.sb("negmax", [P, 2, QC])
        total, inv = s.sb("total", [P, BODY, QC]), s.sb("inv", [P, BODY, QC])
        mixed_sb = s.sb("mixed_sb", [P, 2, QC, GH, HD])
        ps_s, ps_t, ps_o = (s.psum(n, [P, 2, 512]) for n in ("ps_s", "ps_t", "ps_o"))
        in_ready = [s.sem("in_ready0"), s.sem("in_ready1")]
        projected, placed, scored, maxed = (s.sem(n) for n in ("projected", "placed", "scored", "maxed"))
        exped, turned, probsT_ready, mixed, own = (s.sem(n) for n in
                                                   ("exped", "turned", "probsT_ready", "mixed", "own"))
        loads = 2
        if mode == MASKED:
            mask_in = s.sb("mask_in", [P, 2, QC * SEQ], I32)
            mask_add = s.sb("mask_add", [P, 2, QC * SEQ], BF16)
            loads = 3
        if conv:
            mask_in = s.sb("mask_in", [P, 2, QC * SEQ], U8)
            keepT = s.sb("keepT", [P, QC, SEQ])
            mask_add = s.sb("mask_add", [P, QC * SEQ], BF16)
            shifts = s.sb("shifts", [P, TAPS, P + 2])
            band = s.sb("band", [P, 2, TAPS, P + 2])
            taps = s.sb("taps", [P, 2, GH, TAPS * TAPS])
            sT = s.sb("sT", [P, 2, QC, SEQ + 2])
            ps_c = s.psum("ps_c", [P, 2, 512])
            masks_loaded, masks_ready, shifts_ready = s.sem("masks_loaded"), s.sem("masks_ready"), s.sem("shifts_ready")
            masked, convolved, band_free, band_begun, band_ready, taps_ready = (
                s.sem(n) for n in ("masked", "convolved", "band_free", "band_begun", "band_ready", "taps_ready"))
        block = s.block()

        def bias(p, at):
            return w[:, p, WV + at:WV + at + 1]

        def tap(h, dq, d):
            return taps[:, h // GH, h % GH, dq * TAPS + d:dq * TAPS + d + 1]

        @block.sync
        def _(sp):
            if conv:
                sp.dma_start(mask_in[:, :, :], mask.rearrange("p (a n) -> p a n", a=2)).then_inc(masks_loaded, 16)
            with sp.Fori(0, GROUPS) as g:
                with sp.Fori(0, PAIRS) as i:
                    for p in range(2):
                        b = 2 * i + p
                        sp.wait_ge(placed, 2 * (g * PAIRS + i) + p + 1)
                        sp.dma_start(w[:, p, :], w_dram[dyn(g), :]).then_inc(in_ready[p], 16)
                        if ctxT is None:
                            sp.dma_start(ctx[:, p, :, :], xnT[:, :, dyn(b, SEQ)]).then_inc(in_ready[p], 16)
                        else:
                            sp.dma_start(ctx[:, p, :, :].rearrange("p c n -> p (c n)"), ctxT[dyn(b), :])\
                                .then_inc(in_ready[p], 16)
                        if mode == MASKED:
                            sp.dma_start(mask_in[:, p, :], mask[dyn(b), :]).then_inc(in_ready[p], 16)

        @block.tensor
        def _(pe):
            pe.sem_inc(turned, 2)
            pe.sem_inc(mixed, 2)
            if conv:
                pe.sem_inc(convolved, 2)
                pe.wait_ge(masks_ready, 1)

            def project(p, g, i):
                pe.wait_ge(in_ready[p], 16 * loads * (g * PAIRS + i + 1))
                for c in range(DC):
                    pe.matmul(ps_s[:, p, 0:SEQ], w[:, p, c * GW:(c + 1) * GW], xnT[:, c, dyn(2 * i + p, SEQ)],
                              start=(c == 0), stop=(c == DC - 1))
                for c in range(DC):
                    pe.matmul(ps_s[:, p, SEQ:2 * SEQ], w[:, p, WQ + c * GW:WQ + (c + 1) * GW], ctx[:, p, c, :],
                              start=(c == 0), stop=(c == DC - 1))
                for tc in range(QC):
                    out = ps_t[:, p, tc * GV:(tc + 1) * GV]
                    for c in range(DC):
                        pe.matmul(out, ctx[:, p, c, tc * P:(tc + 1) * P], w[:, p, WK + c * GV:WK + (c + 1) * GV],
                                  start=(c == 0), stop=False)
                    last = pe.matmul(out, ones[0:1, 0:P], w[0:1, p, WV + 2:WV + 2 + GV], start=False, stop=True)
                last.then_inc(projected, 1)

            def score(h, done):
                p, r = h // GH, slice(LANE * (h % GH), LANE * (h % GH) + HD)
                out = ps_s[:, h % 2, :]
                if conv:
                    pe.wait_ge(masked, done + h + 1)
                    for kc in range(QC):
                        last = pe.matmul(out[:, kc * SEQ:(kc + 1) * SEQ], kT[r, p, kc * P:(kc + 1) * P], qT[r, p, :],
                                         start=True, stop=True)
                else:
                    pe.wait_ge(exped, done + h + 1)
                    if mode == MASKED:
                        pe.matmul(out, ident16[:, :], mask_add[:, p, :], start=True, stop=False,
                                  skip_group_check=True)
                    for qc in range(QC):
                        last = pe.matmul(out[:, qc * SEQ:(qc + 1) * SEQ], qT[r, p, qc * P:(qc + 1) * P], kT[r, p, :],
                                         start=(mode == PLAIN), stop=(qc == QC - 1 or mode == PLAIN),
                                         skip_group_check=True)
                last.then_inc(scored, 1)

            def convolve(h, done):
                out = ps_c[:, h % 2, :]
                pe.wait_ge(exped, done + h + 1)
                pe.matmul(out, ident16[:, :], mask_add[:, :], start=True, stop=False, skip_group_check=True)
                pe.wait_ge(masked, done + h + 3)
                pe.wait_ge(band_ready, done + h + 1)
                for qc in range(QC):
                    for kc in range(QC):
                        k0, k1 = max(kc * P - 1, 0), min(kc * P + P + 1, SEQ)
                        w0 = k0 - (kc * P - 1)
                        for dq in range(TAPS):
                            last = pe.matmul(out[:, qc * SEQ + k0:qc * SEQ + k1],
                                             sT[:, h % 2, kc, qc * P + dq:qc * P + dq + P],
                                             band[:, h % 2, dq, w0:w0 + k1 - k0], start=False,
                                             stop=(qc == kc == QC - 1 and dq == TAPS - 1), skip_group_check=True)
                last.then_inc(convolved, 1)

            def turn(h, done):
                pe.wait_ge(exped, done + h + 3)
                pe.wait_ge(probsT_ready, done + h + 1)
                for kc in range(QC):
                    for qc in range(QC):
                        last = pe.transpose(ps_t[:, h % 2, kc * SEQ + qc * P:kc * SEQ + (qc + 1) * P],
                                            probs[:, h % 2, qc, kc * P:(kc + 1) * P], ident[:, :])
                last.then_inc(turned, 1)

            def mix(h, done):
                p, j = h // GH, h % GH
                pe.wait_ge(probsT_ready, done + h + 3)
                for qc in range(QC):
                    for kc in range(QC):
                        last = pe.matmul(ps_o[:, p, (qc * GH + j) * HD:(qc * GH + j + 1) * HD],
                                         probsT[:, h % 2, kc, qc * P:(qc + 1) * P],
                                         vv[:, p, kc, j * HD:(j + 1) * HD],
                                         start=(kc == 0), stop=(kc == QC - 1), skip_group_check=True)
                last.then_inc(mixed, 1)

            parts = (score, convolve, turn, mix) if conv else (score, turn, mix)
            with pe.Fori(0, GROUPS) as g:
                with pe.Fori(0, PAIRS) as i:
                    turns = g * PAIRS + i
                    for p in range(2):
                        project(p, g, i)
                    pe.wait_ge(placed, 2 * turns + 4)
                    for step in range(BODY + len(parts) - 1):
                        for lag, part in enumerate(parts):
                            if 0 <= step - lag < BODY:
                                part(step - lag, BODY * turns)

        def copy_turned(engine, copy, h, done):
            engine.wait_ge(turned, done + h + 3)
            engine.wait_ge(mixed, done + h + 1)
            copy(probsT[:, h % 2, :, :], ps_t[:, h % 2, :].rearrange("p (k n) -> p k n", k=QC))\
                .then_inc(probsT_ready, 1)

        @block.scalar
        def _(act):
            act.sem_inc(exped, 2)
            if conv:
                act.sem_inc(probsT_ready, 2)
            with act.Fori(0, GROUPS) as g:
                with act.Fori(0, PAIRS) as i:
                    done = BODY * (g * PAIRS + i)
                    for step in range(BODY + conv):
                        h = step
                        if h < BODY:
                            act.wait_ge(maxed, done + h + 1)
                            act.wait_ge(turned, done + h + 1)
                            ps = (ps_c if conv else ps_s)[:, h % 2, :]
                            for qc in range(QC):
                                last = act.activation(probs[:, h % 2, qc, :], ps[:, qc * SEQ:(qc + 1) * SEQ], ACT.Exp,
                                                      bias=negmax[:, h % 2, qc:qc + 1],
                                                      accum_out=total[:, h, qc:qc + 1])
                            last.then_inc(exped, 1)
                        if conv and step >= 1:
                            copy_turned(act, act.copy, step - 1, done)

        if conv:
            @block.gpsimd
            def _(pool):
                pool.memset(sT[:, :, :, :], 0.0)
                pool.memset(shifts[:, :, :], 0.0).then_inc(shifts_ready, 1)
                pool.wait_ge(shifts_ready, 1)
                for d in range(TAPS):
                    last = pool.affine_select(out=shifts[:, d, :], in_=shifts[:, d, :], compare_op=ALU.not_equal,
                                              fill=1.0, base=d - 2, pattern=[[1, P + 2]], channel_multiplier=-1)
                last.then_inc(shifts_ready, 1)
                pool.wait_ge(shifts_ready, 2)
                with pool.Fori(0, GROUPS) as g:
                    with pool.Fori(0, PAIRS) as i:
                        done = BODY * (g * PAIRS + i)
                        pool.wait_ge(convolved, done + 2)
                        for p in range(2):
                            last = pool.tensor_copy(
                                taps[:, p, :, :].rearrange("p j t -> p (j t)"),
                                kernels[:, dyn((2 * i + p) * GROUPS + g, GH * TAPS * TAPS)])
                        last.then_inc(taps_ready, 1)
                        pool.wait_ge(taps_ready, g * PAIRS + i + 1)
                        for h in range(BODY):
                            pool.wait_ge(convolved, done + h + 1)
                            pool.sem_inc(band_free, 1)
                            for dq in range(TAPS):
                                last = pool.tensor_scalar(band[:, h % 2, dq, :], shifts[:, 0, :], tap(h, dq, 0), None,
                                                          ALU.mult)
                            last.then_inc(band_begun, 1)

        @block.vector
        def _(v):
            steps = Steps(v, own)
            v.sem_inc(placed, 2)
            if conv:
                v.sem_inc(masked, 2)
                v.wait_ge(masks_loaded, 16)
                v.tensor_scalar(keepT[:, :, :].rearrange("p k n -> p (k n)"), mask_in[:, 1, :], -1.0, 1.0,
                                ALU.mult, ALU.add).then_inc(own, 1)
                v.tensor_scalar(mask_add[:, :], mask_in[:, 0, :], NEG_BIG, None, ALU.mult).then_inc(masks_ready, 1)
                v.wait_ge(own, 1)
                v.wait_ge(shifts_ready, 1)
            else:
                v.sem_inc(probsT_ready, 2)
            first = steps.n + conv
            per_turn = 2 * (2 + (mode == MASKED)) + BODY * conv

            def place(p, turns):
                v.wait_ge(projected, 2 * turns + p + 1)
                v.tensor_scalar(qT[:, p, :], ps_s[:, p, 0:SEQ], bias(p, 0), HD ** -0.5, ALU.add, ALU.mult)
                v.tensor_scalar(kT[:, p, :], ps_s[:, p, SEQ:2 * SEQ], bias(p, 1), None, ALU.add)
                if mode == MASKED:
                    v.tensor_scalar(mask_add[:, p, :], mask_in[:, p, :], 0.0, -1.0e9, ALU.is_equal, ALU.mult)
                v.tensor_copy(vv[:, p, :, :], ps_t[:, p, 0:QC * GV].rearrange("p (k n) -> p k n", k=QC))\
                    .then_inc(placed, 1)

            def drop_masked(h, done):
                v.wait_ge(scored, done + h + 1)
                v.wait_ge(convolved, done + h + 1)
                v.tensor_tensor(sT[:, h % 2, :, 1:SEQ + 1], ps_s[:, h % 2, :].rearrange("p (k n) -> p k n", k=QC),
                                keepT[:, :, :], ALU.mult).then_inc(masked, 1)

            def widen_band(h, done):
                v.wait_ge(band_begun, done + h + 1)
                for d in range(1, TAPS):
                    for dq in range(TAPS):
                        out = band[:, h % 2, dq, :]
                        last = v.scalar_tensor_tensor(out, shifts[:, d, :], tap(h, dq, d), out, ALU.mult, ALU.add)
                    if d < TAPS - 1:
                        steps.done(last)
                last.then_inc(band_ready, 1)

            def row_max(h, done):
                ps = ps_c if conv else ps_s
                if conv:
                    v.wait_ge(convolved, done + h + 3)
                else:
                    v.wait_ge(scored, done + h + 1)
                v.tensor_reduce(negmax[:, h % 2, :], ps[:, h % 2, :].rearrange("p (k n) -> p k n", k=QC), X,
                                ALU.max, negate=True).then_inc(maxed, 1)

            def turned_back(h, done):
                copy_turned(v, v.tensor_copy, h, done)

            def finish(p, g, i, turns, done):
                v.wait_ge(mixed, done + GH * (p + 1) + 2)
                steps.done(v.reciprocal(inv[:, GH * p:GH * (p + 1), :], total[:, GH * p:GH * (p + 1), :]))
                factor = inv[:, GH * p:GH * (p + 1), :].rearrange("p j q -> p q j").unsqueeze(3)\
                    .to_broadcast([P, QC, GH, HD])
                steps.done(v.tensor_tensor(mixed_sb[:, p, :, :, :],
                                           ps_o[:, p, 0:QC * GV].rearrange("p (q j d) -> p q j d", q=QC, j=GH),
                                           factor, ALU.mult))
                out = dst[:, dyn(2 * i + p, QC), dyn(g, GV)]
                got = mixed_sb[:, p, :, :, :].rearrange("p q j d -> p q (j d)")
                if mode == MASKED:
                    steps.done(v.tensor_tensor(out, out, got, ALU.add))
                else:
                    v.tensor_copy(out, got)

            def mask_and_band(h, done):
                drop_masked(h, done)
                widen_band(h, done)

            parts = (mask_and_band, row_max) if conv else (row_max, turned_back)
            with v.Fori(0, GROUPS) as g:
                with v.Fori(0, PAIRS) as i:
                    turns = g * PAIRS + i
                    done = BODY * turns
                    steps.n = first + per_turn * turns
                    for p in range(2):
                        place(p, turns)
                    for step in range(BODY + 1):
                        for lag, part in enumerate(parts):
                            if 0 <= step - lag < BODY:
                                part(step - lag, done)
                    for p in range(2):
                        finish(p, g, i, turns, done)


def project_stage(core, name, x, mixed, w_dram, ident, ones):
    with Stage(core, name) as s:
        w = s.sb("w", [P, DC * D + D])
        row, rowT = s.sb("row", [P, 4, D]), s.sb("rowT", [P, 2, DC, P])
        ps_t, ps_y = s.psum("ps_t", [P, 2, 512]), s.psum("ps_y", [P, 2, 512])
        w_loaded, row_ready, turned, rowT_ready, summed, added = (
            s.sem(n) for n in ("w_loaded", "row_ready", "turned", "rowT_ready", "summed", "added"))
        block = s.block()

        @block.sync
        def _(sp):
            sp.dma_start(w[:, :], w_dram).then_inc(w_loaded, 16)

        @block.gpsimd
        def _(pool):
            with pool.Fori(0, TILES // 4) as i:
                for p in range(4):
                    pool.wait_ge(turned, 4 * i + p + 1)
                    pool.tensor_copy(row[:, p, :], mixed[:, 4 * i + p, :]).then_inc(row_ready, 1)

        @block.scalar
        def _(act):
            with act.Fori(0, TILES // 4) as i:
                for p in range(4):
                    act.wait_ge(turned, 4 * i + p + 5)
                    act.wait_ge(added, 4 * i + p + 1)
                    act.copy(rowT[:, p % 2, :, :], ps_t[:, p % 2, 0:D].rearrange("p (c n) -> p c n", c=DC))\
                        .then_inc(rowT_ready, 1)

        @block.tensor
        def _(pe):
            pe.sem_inc(turned, 4)
            pe.sem_inc(rowT_ready, 2)
            pe.wait_ge(w_loaded, 16)

            def turn(i, p):
                pe.wait_ge(row_ready, 4 * i + p + 1)
                pe.wait_ge(rowT_ready, 4 * i + p + 1)
                for c in range(DC):
                    last = pe.transpose(ps_t[:, p % 2, c * P:(c + 1) * P], row[:, p, c * P:(c + 1) * P], ident[:, :])
                last.then_inc(turned, 1)

            def product(i, p):
                out = ps_y[:, p % 2, 0:D]
                pe.wait_ge(rowT_ready, 4 * i + p + 3)
                for c in range(DC):
                    pe.matmul(out, rowT[:, p % 2, c, :], w[:, c * D:(c + 1) * D], start=(c == 0), stop=False)
                pe.matmul(out, ones[0:1, 0:P], w[0:1, DC * D:], start=False, stop=True).then_inc(summed, 1)

            with pe.Fori(0, TILES // 4) as i:
                for step in range(5):
                    if step < 4:
                        turn(i, step)
                    if step >= 1:
                        product(i, step - 1)

        @block.vector
        def _(v):
            v.sem_inc(added, 2)
            with v.Fori(0, TILES // 2) as i:
                for p in range(2):
                    t = 2 * i + p
                    v.wait_ge(summed, t + 1)
                    v.tensor_tensor(x[:, t, :], x[:, t, :], ps_y[:, p, 0:D], ALU.add).then_inc(added, 1)



def context_kernels_stage(core, name, ctxT, a, ident, ones, tb, kernels):
    C, A1, T9 = 2 * D, P, HEADS * TAPS * TAPS
    CC = C // P
    with Stage(core, name) as s:
        hist = s.sb("hist", [P, DC * C + C])
        gb = s.sb("gb", [P, 2, C])
        w1 = s.sb("w1", [P, CC * A1 + 3])
        kg1 = s.sb("kg1", [P, CC * D + D])
        kg_gb = s.sb("kg_gb", [P, 2, D])
        kg2 = s.sb("kg2", [P, DC * T9 + T9])
        ctx = s.sb("ctx", [P, 2, DC, SEQ])
        z = s.sb("z", [P, TILES, C])
        st = s.sb("st", [P, TILES, 6])
        mean, rstd, work = s.sb("mean", [P, TILES]), s.sb("rstd", [P, TILES]), s.sb("work", [P, 5, TILES])
        row = s.sb("row", [P, 2, C])
        rowT = s.sb("rowT", [P, 2, CC, P])
        a1 = s.sb("a1", [P, 2, P])
        pool_w = s.sb("pool_w", [1, B, SEQ])
        pool_n = s.sb("pool_n", [1, 3, B])
        w_cols = s.sb("w_cols", [P, TILES, B])
        cc, ccT = s.sb("cc", [B, C]), s.sb("ccT", [P, CC, B])
        k1, k1T = s.sb("k1", [B, D]), s.sb("k1T", [P, DC, B])
        k_st, k_work = s.sb("k_st", [B, 6]), s.sb("k_work", [B, 8])
        taps = s.sb("taps", [B, HEADS, TAPS * TAPS])
        taps_n = s.sb("taps_n", [B, 3, HEADS])
        pick = s.sb("pick", [B, B, P])
        ps_a, ps_b = s.psum("ps_a", [P, 2, 512]), s.psum("ps_b", [P, 2, 512])
        ps_c, ps_d = s.psum("ps_c", [P, 2, 512]), s.psum("ps_d", [P, 2, 512])
        loaded, ctx_in = s.sem("loaded"), [s.sem("ctx_in0"), s.sem("ctx_in1")]
        hidden, copied, measured = s.sem("hidden"), s.sem("copied"), s.sem("measured")
        var_ready, std_ready, own, pool_own = (s.sem(n) for n in ("var_ready", "std_ready", "own", "pool_own"))
        normed, scaled, gelued, turned = (s.sem(n) for n in ("normed", "scaled", "gelued", "turned"))
        rowT_ready, a1_summed, a1_ready, weighed, weights_kept = (
            s.sem(n) for n in ("rowT_ready", "a1_summed", "a1_ready", "weighed", "weights_kept"))
        relay = s.sem("relay")
        block = s.block()
        (POOL_SHIFTED, POOL_EXPED, POOL_NORMED, COLUMNS, COLUMNS_SPREAD, POOLED, POOLED_COPIED, POOLED_TURNED,
         POOLED_T_COPIED, KG_SUMMED, KG_VAR, KG_STD, KG_NORMED, KG_GELUED, KG_TURNED, KG_T_COPIED, TAPS_SUMMED,
         TAPS_SHIFTED, TAPS_EXPED, TAPS_NORMED, TAPS_SPREAD) = range(1, 22)
        b1, w2, b2 = w1[:, CC * A1:CC * A1 + 1], w1[:, CC * A1 + 1:CC * A1 + 2], w1[0:1, CC * A1 + 2:CC * A1 + 3]

        @block.sync
        def _(sp):
            for to, of in ((hist, a["hist"]), (w1, a["ctx_net"]), (kg1, a["kg1"]), (kg2, a["kg2"])):
                sp.dma_start(to[:, :], of).then_inc(loaded, 16)
            for to, of, n in ((gb, a["hist_gb"], C), (kg_gb, a["kg_gb"], D)):
                sp.dma_start(to[:, :, :], of.rearrange("(o a) n -> o a n", o=1).to_broadcast([P, 2, n]))\
                    .then_inc(loaded, 16)
            with sp.Fori(0, B // 2) as i:
                for p in range(2):
                    sp.wait_ge(hidden, 2 * (2 * i + p) + 2)
                    sp.dma_start(ctx[:, p, :, :].rearrange("p c n -> p (c n)"), ctxT[dyn(2 * i + p), :])\
                        .then_inc(ctx_in[p], 16)

        @block.tensor
        def _(pe):
            pe.sem_inc(hidden, 4)
            pe.sem_inc(turned, 2)
            pe.wait_ge(loaded, 96)
            with pe.Fori(0, B // 2) as i:
                for p in range(2):
                    pe.wait_ge(ctx_in[p], 16 * (i + 1))
                    for q in range(QC):
                        t = 2 * (2 * i + p) + q
                        pe.wait_ge(copied, t + 1)
                        pe.wait_ge(measured, t + 1)
                        for c in range(DC):
                            pe.matmul(ps_a[:, q, :], ctx[:, p, c, q * P:(q + 1) * P], hist[:, c * C:(c + 1) * C],
                                      start=(c == 0), stop=False)
                        pe.matmul(ps_a[:, q, :], ones[0:1, 0:P], hist[0:1, DC * C:], start=False, stop=True)\
                            .then_inc(hidden, 1)
            with pe.Fori(0, TILES // 2) as i:
                for p in range(2):
                    t = 2 * i + p
                    pe.wait_ge(gelued, t + 1)
                    for c in range(CC):
                        last = pe.transpose(ps_b[:, p, c * P:(c + 1) * P], row[:, p, c * P:(c + 1) * P], ident[:, :])
                    last.then_inc(turned, 1)
                    pe.wait_ge(rowT_ready, t + 1)
                    for c in range(CC):
                        last = pe.matmul(ps_c[:, p, 0:P], w1[:, c * A1:(c + 1) * A1], rowT[:, p, c, :],
                                         start=(c == 0), stop=(c == CC - 1))
                    last.then_inc(a1_summed, 1)
                    pe.wait_ge(a1_ready, t + 1)
                    pe.wait_ge(weights_kept, t + 1)
                    pe.matmul(ps_d[0:1, p, 0:P], w2, a1[:, p, :]).then_inc(weighed, 1)
            pe.wait_ge(relay, POOL_NORMED)
            for t in range(TILES):
                last = pe.matmul(ps_a[:, 0, t:t + 1], pool_w[0:1, t // QC, (t % QC) * P:(t % QC + 1) * P],
                                 ones[0:1, 0:1])
            last.then_inc(relay, 1)
            pe.wait_ge(relay, COLUMNS_SPREAD)
            for t in range(TILES):
                last = pe.matmul(ps_b[0:B, 0, :], w_cols[:, t, :], z[:, t, :], start=(t == 0), stop=(t == TILES - 1))
            last.then_inc(relay, 1)
            pe.wait_ge(relay, POOLED_COPIED)
            for c in range(CC):
                last = pe.transpose(ps_c[:, 0, c * B:(c + 1) * B], cc[:, c * P:(c + 1) * P], ident[0:B, 0:B])
            last.then_inc(relay, 1)
            pe.wait_ge(relay, POOLED_T_COPIED)
            for c in range(CC):
                pe.matmul(ps_d[0:B, 0, 0:D], ccT[:, c, :], kg1[:, c * D:(c + 1) * D], start=(c == 0), stop=False)
            pe.matmul(ps_d[0:B, 0, 0:D], ones[0:1, 0:B], kg1[0:1, CC * D:], start=False, stop=True).then_inc(relay, 1)
            pe.wait_ge(relay, KG_GELUED)
            for c in range(DC):
                last = pe.transpose(ps_c[:, 1, c * B:(c + 1) * B], k1[:, c * P:(c + 1) * P], ident[0:B, 0:B])
            last.then_inc(relay, 1)
            pe.wait_ge(relay, KG_T_COPIED)
            for c in range(DC):
                pe.matmul(ps_d[0:B, 1, 0:T9], k1T[:, c, :], kg2[:, c * T9:(c + 1) * T9], start=(c == 0), stop=False)
            pe.matmul(ps_d[0:B, 1, 0:T9], ones[0:1, 0:B], kg2[0:1, DC * T9:], start=False, stop=True)\
                .then_inc(relay, 1)
            pe.wait_ge(relay, TAPS_NORMED)
            pe.wait_ge(pool_own, 2)
            for b in range(B):
                bank = (ps_a[:, 1], ps_b[:, 1], ps_c[:, 1])[b // 3]
                last = pe.matmul(bank[:, (b % 3) * T9:(b % 3 + 1) * T9], pick[:, b, :],
                                 taps[:, :, :].rearrange("b h t -> b (h t)"), start=True, stop=True,
                                 skip_group_check=True)
            last.then_inc(relay, 1)

        @block.gpsimd
        def _(pool):
            pool.memset(w_cols[:, :, :], 0.0)
            pool.memset(pick[:, :, :], 1.0).then_inc(pool_own, 1)
            pool.wait_ge(pool_own, 1)
            pool.affine_select(out=pick[:, :, :], in_=pick[:, :, :], compare_op=ALU.is_equal, fill=0.0, base=0,
                               pattern=[[-1, B], [0, P]], channel_multiplier=1).then_inc(pool_own, 1)
            pool.wait_ge(loaded, 96)
            with pool.Fori(0, TILES // 2) as i:
                for p in range(2):
                    t = 2 * i + p
                    pool.wait_ge(scaled, t + 1)
                    pool.tensor_tensor(row[:, p, :], row[:, p, :], gb[:, 1, :], ALU.add).then_inc(normed, 1)

        @block.scalar
        def _(act):
            act.sem_inc(copied, 2)
            with act.Fori(0, TILES // 2) as i:
                for p in range(2):
                    t = 2 * i + p
                    act.wait_ge(hidden, t + 5)
                    act.wait_ge(measured, t + 3)
                    act.copy(z[:, t, :], ps_a[:, p, :]).then_inc(copied, 1)
            act.wait_ge(var_ready, 1)
            act.activation(work[:, 4, :], work[:, 3, :], ACT.Sqrt).then_inc(std_ready, 1)
            with act.Fori(0, TILES // 2) as i:
                for p in range(2):
                    t = 2 * i + p
                    act.wait_ge(normed, t + 1)
                    act.activation(row[:, p, :], row[:, p, :], ACT.Gelu).then_inc(gelued, 1)
                    act.wait_ge(gelued, t + 1)
                    act.copy(z[:, t, :], row[:, p, :])
                    act.wait_ge(a1_summed, t + 1)
                    act.activation(a1[:, p, :], ps_c[:, p, 0:P], ACT.Gelu, bias=b1).then_inc(a1_ready, 1)
            act.wait_ge(relay, POOL_SHIFTED)
            act.activation(pool_w[:, :, :], pool_w[:, :, :], ACT.Exp).then_inc(relay, 1)
            act.wait_ge(relay, KG_VAR)
            act.activation(k_work[:, 5:6], k_work[:, 4:5], ACT.Sqrt).then_inc(relay, 1)
            act.wait_ge(relay, KG_NORMED)
            act.activation(k1[:, :], k1[:, :], ACT.Gelu).then_inc(relay, 1)
            act.wait_ge(relay, TAPS_SHIFTED)
            act.activation(taps[:, :, :], taps[:, :, :], ACT.Exp).then_inc(relay, 1)

        @block.vector
        def _(v):
            steps = Steps(v, own)
            v.sem_inc(measured, 2)
            v.sem_inc(weights_kept, 2)
            v.wait_ge(loaded, 96)
            with v.Fori(0, TILES // 2) as i:
                for p in range(2):
                    t = 2 * i + p
                    v.wait_ge(hidden, t + 5)
                    v.bn_stats(st[:, t, :], ps_a[:, p, :]).then_inc(measured, 1)
            v.wait_ge(measured, TILES + 2)
            me, mo, se, so = st[:, :, 1], st[:, :, 4], st[:, :, 2], st[:, :, 5]
            v.tensor_tensor(mean[:, :], me, mo, ALU.add)
            v.tensor_tensor(work[:, 0, :], me, mo, ALU.subtract)
            steps.done(v.tensor_tensor(work[:, 1, :], se, so, ALU.add))
            v.tensor_scalar(mean[:, :], mean[:, :], 0.5, None, ALU.mult)
            v.tensor_scalar(work[:, 1, :], work[:, 1, :], 1.0 / C, LN_EPS, ALU.mult, ALU.add)
            steps.done(v.scalar_tensor_tensor(work[:, 2, :], work[:, 0, :], 0.25, work[:, 0, :],
                                              ALU.mult, ALU.mult))
            v.tensor_tensor(work[:, 3, :], work[:, 1, :], work[:, 2, :], ALU.add).then_inc(var_ready, 1)
            v.wait_ge(std_ready, 1)
            steps.done(v.reciprocal(rstd[:, :], work[:, 4, :]))
            v.wait_ge(copied, TILES + 2)
            start = steps.n
            with v.Fori(0, TILES // 2) as i:
                for p in range(2):
                    t = 2 * i + p
                    v.wait_ge(turned, t + 1)
                    steps.n = start + t
                    steps.done(v.tensor_scalar(row[:, p, :], z[:, t, :], mean[:, bass.ds(t, 1)],
                                               rstd[:, bass.ds(t, 1)], ALU.subtract, ALU.mult))
                    v.tensor_tensor(row[:, p, :], row[:, p, :], gb[:, 0, :], ALU.mult).then_inc(scaled, 1)
                    v.wait_ge(turned, t + 3)
                    v.tensor_copy(rowT[:, p, :, :], ps_b[:, p, :].rearrange("p (c n) -> p c n", c=CC))\
                        .then_inc(rowT_ready, 1)
                    v.wait_ge(weighed, t + 1)
                    v.tensor_scalar(pool_w[0:1, bass.ds(i, 1), p * P:(p + 1) * P],
                                    ps_d[0:1, p:p + 1, 0:P], b2, None, ALU.add).then_inc(weights_kept, 1)
            steps.n = start + TILES
            v.wait_ge(weights_kept, TILES + 2)
            steps.done(v.tensor_reduce(pool_n[:, 0, :], pool_w[:, :, :], X, ALU.max, negate=True))
            v.tensor_tensor(pool_w[:, :, :], pool_w[:, :, :],
                            pool_n[:, 0, :].unsqueeze(2).to_broadcast([1, B, SEQ]), ALU.add).then_inc(relay, 1)
            v.wait_ge(relay, POOL_EXPED)
            steps.done(v.reduce_sum(pool_n[:, 1, :], pool_w[:, :, :], X))
            steps.done(v.reciprocal(pool_n[:, 2, :], pool_n[:, 1, :]))
            v.tensor_tensor(pool_w[:, :, :], pool_w[:, :, :],
                            pool_n[:, 2, :].unsqueeze(2).to_broadcast([1, B, SEQ]), ALU.mult).then_inc(relay, 1)
            v.wait_ge(relay, COLUMNS)
            v.wait_ge(pool_own, 1)
            for b in range(B):
                last = v.tensor_copy(w_cols[:, b * QC:(b + 1) * QC, b:b + 1],
                                     ps_a[:, 0, b * QC:(b + 1) * QC].unsqueeze(2))
            last.then_inc(relay, 1)
            v.wait_ge(relay, POOLED)
            v.tensor_copy(cc[:, :], ps_b[0:B, 0, :]).then_inc(relay, 1)
            v.wait_ge(relay, POOLED_TURNED)
            v.tensor_copy(ccT[:, :, :], ps_c[:, 0, 0:CC * B].rearrange("p (c b) -> p c b", c=CC)).then_inc(relay, 1)
            v.wait_ge(relay, KG_SUMMED)
            steps.done(v.bn_stats(k_st[:, :], ps_d[0:B, 0, 0:D]))
            v.tensor_tensor(k_work[:, 0:1], k_st[:, 1:2], k_st[:, 4:5], ALU.add)
            v.tensor_tensor(k_work[:, 1:2], k_st[:, 1:2], k_st[:, 4:5], ALU.subtract)
            steps.done(v.tensor_tensor(k_work[:, 2:3], k_st[:, 2:3], k_st[:, 5:6], ALU.add))
            v.tensor_scalar(k_work[:, 0:1], k_work[:, 0:1], 0.5, None, ALU.mult)
            v.tensor_scalar(k_work[:, 2:3], k_work[:, 2:3], 1.0 / D, LN_EPS, ALU.mult, ALU.add)
            steps.done(v.scalar_tensor_tensor(k_work[:, 3:4], k_work[:, 1:2], 0.25, k_work[:, 1:2],
                                              ALU.mult, ALU.mult))
            v.tensor_tensor(k_work[:, 4:5], k_work[:, 2:3], k_work[:, 3:4], ALU.add).then_inc(relay, 1)
            v.wait_ge(relay, KG_STD)
            steps.done(v.reciprocal(k_work[:, 6:7], k_work[:, 5:6]))
            steps.done(v.tensor_scalar(k1[:, :], ps_d[0:B, 0, 0:D], k_work[:, 0:1], k_work[:, 6:7],
                                       ALU.subtract, ALU.mult))
            steps.done(v.tensor_tensor(k1[:, :], k1[:, :], kg_gb[0:B, 0, :], ALU.mult))
            v.tensor_tensor(k1[:, :], k1[:, :], kg_gb[0:B, 1, :], ALU.add).then_inc(relay, 1)
            v.wait_ge(relay, KG_TURNED)
            v.tensor_copy(k1T[:, :, :], ps_c[:, 1, 0:DC * B].rearrange("p (c b) -> p c b", c=DC)).then_inc(relay, 1)
            v.wait_ge(relay, TAPS_SUMMED)
            kp = ps_d[0:B, 1, 0:T9].rearrange("b (h t) -> b h t", h=HEADS)
            over_taps = lambda n: taps_n[:, n, :].unsqueeze(2).to_broadcast([B, HEADS, TAPS * TAPS])
            steps.done(v.tensor_reduce(taps_n[:, 0, :], kp, X, ALU.max, negate=True))
            v.tensor_tensor(taps[:, :, :], kp, over_taps(0), ALU.add).then_inc(relay, 1)
            v.wait_ge(relay, TAPS_EXPED)
            steps.done(v.reduce_sum(taps_n[:, 1, :], taps[:, :, :], X))
            steps.done(v.reciprocal(taps_n[:, 2, :], taps_n[:, 1, :]))
            v.tensor_tensor(taps[:, :, :], taps[:, :, :], over_taps(2), ALU.mult).then_inc(relay, 1)
            v.wait_ge(relay, TAPS_SPREAD)
            for n, ps in enumerate((ps_a, ps_b, ps_c)):
                m = min(3, B - 3 * n)
                v.tensor_copy(kernels[:, 3 * n * T9:(3 * n + m) * T9], ps[:, 1, 0:m * T9])



def build(nc, ins, outs, stages=99):
    i = ins
    with ExitStack() as whole:
        core = Core(nc, whole)
        x = core.keep("x", [P, TILES, D])
        xn = core.keep("xn", [P, TILES, D])
        xnT = core.keep("xnT", [P, DC, TILES * P])
        ident = core.keep("ident", [P, P])
        ones = core.keep("ones", [P, P])
        ident16 = core.keep("ident16", [P, P], BF16)
        logits = core.keep("logits", [P, TILES, 64])
        tb = Tables(core, MOST_TILES)
        xn_dram = nc.dram_tensor("xn_rows", (TILES * P, D), F32).ap()
        y_dram = nc.dram_tensor("y_rows", (MOST_TILES * P, D), F32).ap()
        x_rows = i["x"].rearrange("(t p) d -> p t d", p=P)

        with Stage(core, "load") as s:
            x_loaded, zeroed = s.sem("x_loaded"), s.sem("zeroed")
            block = s.block()

            @block.sync
            def _(sp):
                sp.dma_start(x[:, :, :], x_rows).then_inc(x_loaded, 16)
                sp.wait_ge(x_loaded, 16)

            @block.gpsimd
            def _(pool):
                pool.memset(ones[:, :], 1.0)
                pool.memset(tb.zeros[:, :], 0.0)
                pool.iota(tb.row_iota[:, :], [[1, P]], base=0, channel_multiplier=0,
                          allow_small_or_imprecise_dtypes=True)
                pool.iota(tb.column[:, :], [[0, 1]], base=0, channel_multiplier=1,
                          allow_small_or_imprecise_dtypes=True)
                for k in (1, 2):
                    pool.iota(tb.token_id[k][:, :].rearrange("p (t k) -> p t k", k=k), [[P, TILES], [0, k]],
                              base=0, channel_multiplier=1, allow_small_or_imprecise_dtypes=True)
                pool.memset(tb.before[:, :], 1.0).then_inc(zeroed, 1)
                pool.memset(ident16[:, :], 0.0)
                pool.memset(ident[:, :], 0.0).then_inc(zeroed, 1)
                pool.wait_ge(zeroed, 2)
                pool.affine_select(out=tb.before[:, :], in_=tb.before[:, :], compare_op=ALU.is_gt, fill=0.0,
                                   base=0, pattern=[[1, P]], channel_multiplier=-1)
                for eye in (ident, ident16):
                    pool.affine_select(out=eye[:, :], in_=eye[:, :], compare_op=ALU.not_equal, fill=1.0,
                                       base=0, pattern=[[-1, P]], channel_multiplier=1)

        norm_stage(core, "norm0", x, xn, xnT, ident)
        single_head_stage(core, "attn0", xn, xnT, i["ctxT"], i["w0"], ident, ones)
        post_norm_stage(core, "post0", x, xn, i["gb0"])
        norm_stage(core, "norm0f", x, xn, xnT, ident, i["router0"], logits)
        NT = TILES * 2 + 8
        route_stage(core, "route0", logits[:, :, 0:8], 8, 2, NT, tb, ones, xn, xn_dram)
        experts_stage(core, "experts0", NT, P, [128, 128, 96], i["experts0"], tb, xn_dram, y_dram, ident, ones)
        shared_stage(core, "shared0", xnT, logits[:, :, 8], i["shared0"], x)
        combine_stage(core, "combine0", 2, tb, y_dram[0:NT * P, :], x)
        kernels = core.keep("kernels", [P, B * HEADS * TAPS * TAPS])
        context_kernels_stage(core, "kernels1", i["ctxT"], i, ident, ones, tb, kernels)
        norm_stage(core, "norm1", x, xn, xnT, ident)
        heads_stage(core, "heads1", CONV, xnT, None, i["heads1"], xn, ident, mask=i["mask1"],
                    ident16=ident16, kernels=kernels, ones=ones)
        project_stage(core, "proj1", x, xn, i["proj1"], ident, ones)
        norm_stage(core, "norm1f", x, xn, xnT, ident, i["router1"], logits)
        NT = TILES + 8
        route_stage(core, "route1", logits[:, :, 0:8], 8, 1, NT, tb, ones, xn, xn_dram, bias=i["router_bias1"])
        experts_stage(core, "experts1", NT, P, [P] * 8, i["experts1"], tb, xn_dram, y_dram, ident, ones,
                      biased=True)
        combine_stage(core, "combine1", 1, tb, y_dram[0:NT * P, :], x)
        norm_stage(core, "norm2", x, xn, xnT, ident)
        heads_stage(core, "heads2", MASKED, xnT, i["ctxT"], i["heads2"], x, ident, mask=i["mask2"],
                    ident16=ident16, ones=ones)
        norm_stage(core, "norm2f", x, xn, xnT, ident, i["router2"], logits)
        NT = TILES * 2 + 32
        for n in range(2):
            route_stage(core, f"route2_{n}", logits[:, :, 32 * n:32 * n + 32], 32, 2, NT, tb, ones, xn,
                        None if n else xn_dram, factor=0.5)
            experts_stage(core, f"experts2_{n}", NT, P, [P], i[f"experts2_{n}"], tb, xn_dram, y_dram, ident, ones)
            combine_stage(core, f"combine2_{n}", 2, tb, y_dram[0:NT * P, :], x)
        norm_stage(core, "norm3", x, xn, xnT, ident)
        heads_stage(core, "heads3", PLAIN, xnT, i["ctxT"], i["heads3"], xn, ident, ones=ones)
        project_stage(core, "proj3", x, xn, i["proj3"], ident, ones)
        norm_stage(core, "norm3f", x, xn, xnT, ident, i["router3"], logits)
        CAP = -(-5 * TILES * P // (4 * 32))
        route_stage(core, "route3", logits[:, :, 0:32], 32, 1, 32, tb, ones, xn, xn_dram, capacity=CAP)
        experts_stage(core, "experts3", 32, CAP, [P, P], i["experts3"], tb, xn_dram, y_dram, ident, ones)
        combine_stage(core, "combine3", 1, tb, y_dram[0:32 * CAP, :], x, xn)
        with Stage(core, "store") as s:
            stored = s.sem("stored")
            block = s.block()

            @block.sync
            def _(sp):
                sp.dma_start(outs.rearrange("(t p) d -> p t d", p=P), x[:, :, :]).then_inc(stored, 16)
                sp.wait_ge(stored, 16)


def _columns(w):
    K, n = w.shape
    return w.reshape(K // P, P, n).transpose(1, 0, 2).reshape(P, -1)


def _in_partition_0(row):
    import numpy as np

    out = np.zeros((P, row.size), row.dtype)
    out[0] = row.reshape(-1)
    return out


def _layouts(a):
    import numpy as np

    cat = lambda *parts: np.ascontiguousarray(np.concatenate(parts, axis=1))
    o = {"x": a["x"].reshape(B * SEQ, D)}
    o["ctxT"] = a["ctx_1024"].transpose(0, 2, 1).reshape(B, DC, P, SEQ).transpose(0, 2, 1, 3).reshape(B * P, DC * SEQ)
    col = lambda b: b.reshape(DC, P).T
    g = lambda n: a[n]
    o["w0"] = cat(_columns(g("L0_xattn_Wq")), _columns(g("L0_xattn_Wk")), _columns(g("L0_xattn_Wv")),
                  col(g("L0_xattn_bq")), col(g("L0_xattn_bk")), _in_partition_0(g("L0_xattn_bv")))
    o["gb0"] = np.stack([g("L0_xattn_gamma"), g("L0_xattn_beta")])

    def expert_rows(gate, up, down):
        E, _, F = gate.shape
        NF = -(-F // P)
        parts = [m.reshape(E, DC, P, F).transpose(0, 2, 1, 3).reshape(E, P, DC * F) for m in (gate, up) if m is not None]
        full = np.zeros((E, NF * P, D), down.dtype)
        full[:, :F] = down
        parts.append(full.reshape(E, NF, P, D).transpose(0, 2, 1, 3).reshape(E, P, NF * D))
        return np.concatenate(parts, axis=2).reshape(E * P, -1)

    swap = lambda m: np.swapaxes(m, -1, -2)
    I = g("L0_ffn_experts_down").shape[2]
    gu = swap(g("L0_ffn_experts_gate_up"))
    o["experts0"] = expert_rows(gu[:, :, :I], gu[:, :, I:], swap(g("L0_ffn_experts_down")))
    o["shared0"] = expert_rows(g("L0_ffn_shared_gate_w").T[None], g("L0_ffn_shared_up_w").T[None],
                               g("L0_ffn_shared_down_w").T[None])
    o["router0"] = _columns(cat(g("L0_ffn_gate_w").T, g("L0_ffn_shared_expert_gate_w").T))
    w1 = expert_rows(g("L1_ffn_W1"), None, g("L1_ffn_W2")).reshape(8, P, -1)
    b1 = g("L1_ffn_b1").reshape(8, -1, P).transpose(0, 2, 1)
    b2 = np.zeros((8, P, D), w1.dtype)
    b2[:, 0] = g("L1_ffn_b2")
    o["experts1"] = np.concatenate([w1, b1, b2], axis=2).reshape(8 * P, -1)
    o["router1"], o["router_bias1"] = _columns(g("L1_ffn_Wg")), g("L1_ffn_bg").reshape(1, -1)
    o["router2"] = _columns(cat(g("L2_ffn_router_w0"), g("L2_ffn_router_w1")))
    for n in "01":
        o["experts2_" + n] = expert_rows(g("L2_ffn_wg" + n), g("L2_ffn_wu" + n), g("L2_ffn_wd" + n))
    o["router3"] = _columns(g("L3_ffn_w_router"))
    o["experts3"] = expert_rows(g("L3_ffn_w_gate"), g("L3_ffn_w_up"), g("L3_ffn_w_down"))

    def heads_rows(wq, bq, wk, bk, wv, bv):
        def lanes(m):
            out = np.zeros((m.shape[0], HEADS, LANE), m.dtype)
            out[:, :, :HD] = m.reshape(-1, HEADS, HD)
            return out.reshape(-1, GROUPS, GH * LANE)
        wq, wk = lanes(wq), lanes(wk)
        bq, bk = lanes(bq[None])[0], lanes(bk[None])[0]
        wv, bv = wv.reshape(D, GROUPS, -1), bv.reshape(GROUPS, -1)
        return np.concatenate([cat(_columns(wq[:, n]), _columns(wk[:, n]), _columns(wv[:, n]),
                                   bq[n][:, None], bk[n][:, None], _in_partition_0(bv[n]))
                               for n in range(GROUPS)])

    none = np.zeros(D, a["x"].dtype)
    o["heads1"] = heads_rows(g("L1_xattn_Wq"), none, g("L1_xattn_Wk"), none, g("L1_xattn_Wv"), none)
    for n in "23":
        L = f"L{n}_xattn_"
        o["heads" + n] = heads_rows(g(L + "Wq").T, g(L + "bq"), g(L + "Wk").T, g(L + "bk"), g(L + "Wv").T, g(L + "bv"))
    o["proj1"] = cat(_columns(g("L1_xattn_proj_W")), _in_partition_0(g("L1_xattn_proj_b")))
    o["proj3"] = cat(_columns(g("L3_xattn_Wo").T), _in_partition_0(g("L3_xattn_bo")))
    m = g("mask_SxS_bc0")
    o["mask1"] = cat(_columns(m), _columns(m.T))
    o["mask2"] = g("mask_BxSxS2_if1").reshape(B, QC, P, SEQ).transpose(0, 2, 1, 3).reshape(B * P, QC * SEQ)

    L = "L1_xattn_"
    o["hist"] = cat(_columns(g(L + "hist_W")), _in_partition_0(g(L + "hist_b")))
    o["hist_gb"] = np.stack([g(L + "hist_ln_g"), g(L + "hist_ln_b")])
    o["ctx_net"] = cat(_columns(g(L + "ctx_W1")), g(L + "ctx_b1")[:, None], g(L + "ctx_W2"),
                       _in_partition_0(g(L + "ctx_b2")))
    o["kg1"] = cat(_columns(g(L + "kg_W1")), _in_partition_0(g(L + "kg_b1")))
    o["kg_gb"] = np.stack([g(L + "kg_ln_g"), g(L + "kg_ln_b")])
    o["kg2"] = cat(_columns(g(L + "kg_W2")), _in_partition_0(g(L + "kg_b2")))
    return {k: np.ascontiguousarray(v) for k, v in o.items()}


def kernel(**inputs):
    import numpy as _np
    import concourse.bacc as _bacc
    from concourse.bass_utils import run_bass_kernel_spmd as _run

    nc = _bacc.Bacc("TRN2", target_bir_lowering=False, num_devices=1)
    arrays = _layouts({k: _np.asarray(v) for k, v in inputs.items()})
    ins = {k: nc.dram_tensor(f"in_{k}_dram", v.shape, mybir.dt.from_np(v.dtype), kind="ExternalInput").ap()
           for k, v in arrays.items()}
    out = nc.dram_tensor("out", (B * SEQ, D), F32, kind="ExternalOutput").ap()
    build(nc, ins, out)
    r = _run(nc, [{f"in_{k}_dram": v for k, v in arrays.items()}], core_ids=[0])
    return r.results[0]["out"].reshape(B, SEQ, D)
```

```python
from contextlib import ExitStack

import concourse.bass as bass
from concourse import mybir

F32 = mybir.dt.float32
BF16 = mybir.dt.bfloat16
I32 = mybir.dt.int32
U32 = mybir.dt.uint32
U8 = mybir.dt.uint8
ALU = mybir.AluOpType
ACT = mybir.ActivationFunctionType
X = mybir.AxisListType.X

P = 128
B, SEQ, D = 8, 256, 256
TILES = B * SEQ // P
DC = D // P
QC = SEQ // P
HEADS, HD = 16, 16
GROUPS = 4
GH = HEADS // GROUPS
LANE = 32
NEG_BIG = -1.0e30
LN_EPS = 1e-5
TAPS = 3
MOST_TILES = 64


class Steps:

    def __init__(self, engine, semaphore):
        self.engine, self.semaphore, self.n = engine, semaphore, 0

    def done(self, instruction):
        instruction.then_inc(self.semaphore, 1)
        self.n = self.n + 1
        self.engine.wait_ge(self.semaphore, self.n)


class Core:

    def __init__(self, nc, whole):
        self.nc, self.whole = nc, whole

    def keep(self, name, shape, dtype=F32):
        return self.whole.enter_context(self.nc.sbuf_tensor(name, shape, dtype))


class Stage:

    def __init__(self, core, name):
        self.core, self.name, self.nc = core, name, core.nc
        self.stack = ExitStack()
        self.sems = []

    def __enter__(self):
        return self

    def __exit__(self, *error):
        self.stack.__exit__(*error)
        if error[0] is None:
            self.nc.clear_and_free_semaphores(self.sems)
            self.nc.all_engine_barrier()

    def sb(self, name, shape, dtype=F32):
        return self.stack.enter_context(self.nc.sbuf_tensor(f"{self.name}_{name}", shape, dtype))

    def psum(self, name, shape, dtype=F32):
        return self.stack.enter_context(self.nc.psum_tensor(f"{self.name}_{name}", shape, dtype))

    def sem(self, name):
        self.sems.append(self.nc.alloc_semaphore(f"{self.name}_{name}"))
        return self.sems[-1]

    def block(self):
        return self.stack.enter_context(self.nc.Block())


def dyn(index, size=P):
    return bass.ds(index * size, size)



def row_statistics(v, steps, src, st, mean, rstd, work, stats_done, var_ready, std_ready):
    with v.Fori(0, TILES) as t:
        v.bn_stats(st[:, t, :], src[:, t, :]).then_inc(stats_done, 1)
    v.wait_ge(stats_done, TILES)
    me, mo, se, so = st[:, :, 1], st[:, :, 4], st[:, :, 2], st[:, :, 5]
    v.tensor_tensor(mean[:, :], me, mo, ALU.add)
    v.tensor_tensor(work[:, 0, :], me, mo, ALU.subtract)
    steps.done(v.tensor_tensor(work[:, 1, :], se, so, ALU.add))
    v.tensor_scalar(mean[:, :], mean[:, :], 0.5, None, ALU.mult)
    v.tensor_scalar(work[:, 1, :], work[:, 1, :], 1.0 / D, LN_EPS, ALU.mult, ALU.add)
    steps.done(v.scalar_tensor_tensor(work[:, 2, :], work[:, 0, :], 0.25, work[:, 0, :],
                                      ALU.mult, ALU.mult))
    v.tensor_tensor(work[:, 3, :], work[:, 1, :], work[:, 2, :], ALU.add).then_inc(var_ready, 1)
    v.wait_ge(std_ready, 1)
    steps.done(v.reciprocal(rstd[:, :], work[:, 4, :]))


def norm_stage(core, name, x, xn, xnT, ident, router=None, logits=None):
    nc = core.nc
    with Stage(core, name) as s:
        st = s.sb("st", [P, TILES, 6])
        mean = s.sb("mean", [P, TILES])
        rstd = s.sb("rstd", [P, TILES])
        work = s.sb("work", [P, 5, TILES])
        row = s.sb("row", [P, 4, D])
        ps_t = s.psum("ps_t", [P, 2, 512])
        stats_done, var_ready, std_ready = s.sem("stats_done"), s.sem("var_ready"), s.sem("std_ready")
        own = s.sem("own")
        row_ready, row_copied = s.sem("row_ready"), s.sem("row_copied")
        turned, tile_free = s.sem("turned"), s.sem("tile_free")
        if router is not None:
            E = router.shape[1] // DC
            w = s.sb("router", [P, DC, E])
            colT = s.sb("colT", [P, 4, DC, P])
            ps_l = s.psum("ps_l", [P, TILES, E])
            w_loaded, col_ready, logits_ready = s.sem("w_loaded"), s.sem("col_ready"), s.sem("logits_ready")
        block = s.block()

        @block.sync
        def _(sp):
            if router is not None:
                sp.dma_start(w[:, :, :], router.rearrange("p (c e) -> p c e", c=DC)).then_inc(w_loaded, 16)

        @block.vector
        def _(v):
            steps = Steps(v, own)
            row_statistics(v, steps, x, st, mean, rstd, work, stats_done, var_ready, std_ready)
            with v.Fori(0, TILES // 4) as i:
                for p in range(4):
                    t = 4 * i + p
                    v.wait_ge(turned, t + 1)
                    v.wait_ge(row_copied, t + 1)
                    v.tensor_scalar(row[:, p, :], x[:, t, :], mean[:, bass.ds(t, 1)], rstd[:, bass.ds(t, 1)],
                                    ALU.subtract, ALU.mult).then_inc(row_ready, 1)
            if router is not None:
                v.wait_ge(logits_ready, TILES + 4)
                v.tensor_copy(logits[:, :, 0:E], ps_l[:, :, :])

        @block.gpsimd
        def _(pool):
            pool.sem_inc(row_copied, 4)
            with pool.Fori(0, TILES // 4) as i:
                for p in range(4):
                    t = 4 * i + p
                    pool.wait_ge(row_ready, t + 1)
                    pool.tensor_copy(xn[:, t, :], row[:, p, :]).then_inc(row_copied, 1)

        @block.scalar
        def _(act):
            act.sem_inc(tile_free, 2)
            act.wait_ge(var_ready, 1)
            act.activation(work[:, 4, :], work[:, 3, :], ACT.Sqrt).then_inc(std_ready, 1)
            with act.Fori(0, TILES // 4) as i:
                for p in range(4):
                    t = 4 * i + p
                    act.wait_ge(turned, t + 5)
                    tile_T = ps_t[:, p % 2, 0:D].rearrange("p (c n) -> p c n", c=DC)
                    if router is not None:
                        act.wait_ge(logits_ready, t + 1)
                        act.copy(colT[:, p, :, :], tile_T).then_inc(col_ready, 1)
                    act.copy(xnT[:, :, dyn(t)], tile_T).then_inc(tile_free, 1)

        @block.tensor
        def _(pe):
            pe.sem_inc(turned, 4)
            if router is not None:
                pe.sem_inc(logits_ready, 4)
                pe.wait_ge(w_loaded, 16)

            def turn(i, p):
                t = 4 * i + p
                pe.wait_ge(row_ready, t + 1)
                pe.wait_ge(tile_free, t + 1)
                for c in range(DC):
                    last = pe.transpose(ps_t[:, p % 2, c * P:(c + 1) * P], row[:, p, c * P:(c + 1) * P], ident[:, :])
                last.then_inc(turned, 1)

            def route(i, p):
                t = 4 * i + p
                pe.wait_ge(col_ready, t + 1)
                for c in range(DC):
                    last = pe.matmul(ps_l[:, t, :], colT[:, p, c, :], w[:, c, :],
                                     start=(c == 0), stop=(c == DC - 1), skip_group_check=True)
                last.then_inc(logits_ready, 1)

            with pe.Fori(0, TILES // 4) as i:
                for step in range(5):
                    if step < 4:
                        turn(i, step)
                    if step >= 1 and router is not None:
                        route(i, step - 1)



def single_head_stage(core, name, xn, xnT, ctxT, w_dram, ident, ones):
    nc = core.nc
    W3 = 3 * DC * D
    with Stage(core, name) as s:
        w = s.sb("w", [P, W3 + 2 * DC + D])
        wq, wk, wv = (w[:, n * DC * D:(n + 1) * DC * D].rearrange("p (c n) -> p c n", c=DC) for n in range(3))
        bq, bk, bv = w[:, W3:W3 + DC], w[:, W3 + DC:W3 + 2 * DC], w[0:1, W3 + 2 * DC:]
        ctx = s.sb("ctx", [P, 2, DC, SEQ])
        qT, kT, vv = s.sb("qT", [P, DC, SEQ]), s.sb("kT", [P, DC, SEQ]), s.sb("v", [P, QC, D])
        probs, probsT = s.sb("probs", [P, QC, SEQ]), s.sb("probsT", [P, QC, SEQ])
        negmax, total, inv = s.sb("negmax", [P, QC]), s.sb("total", [P, QC]), s.sb("inv", [P, QC])
        ps_q, ps_k, ps_v, ps_s, ps_pT, ps_o = (s.psum(n, [P, 2, D]) for n in
                                               ("ps_q", "ps_k", "ps_v", "ps_s", "ps_pT", "ps_o"))
        w_loaded, ctx_loaded = s.sem("w_loaded"), [s.sem("ctx_loaded0"), s.sem("ctx_loaded1")]
        projected, q_ready, k_ready, v_ready = (s.sem(n) for n in ("projected", "q_ready", "k_ready", "v_ready"))
        scored, max_ready, probs_ready = s.sem("scored"), s.sem("max_ready"), s.sem("probs_ready")
        turned, probsT_ready, mixed, added, own = (s.sem(n) for n in
                                                   ("turned", "probsT_ready", "mixed", "added", "own"))
        block = s.block()

        @block.sync
        def _(sp):
            sp.dma_start(w[:, :], w_dram).then_inc(w_loaded, 16)
            with sp.Fori(0, B // 2) as i:
                for p in range(2):
                    b = 2 * i + p
                    sp.wait_ge(projected, 3 * b + 3)
                    sp.dma_start(ctx[:, p, :, :].rearrange("p c n -> p (c n)"), ctxT[dyn(b), :])\
                        .then_inc(ctx_loaded[p], 16)

        @block.tensor
        def _(pe):
            pe.sem_inc(projected, 6)
            pe.wait_ge(w_loaded, 16)
            with pe.Fori(0, B // 2) as i:
                for p in range(2):
                    b = 2 * i + p
                    for oc in range(DC):
                        for c in range(DC):
                            last = pe.matmul(ps_q[:, oc, :], wq[:, c, oc * P:(oc + 1) * P],
                                             xnT[:, c, dyn(b, SEQ)], start=(c == 0), stop=(c == DC - 1))
                    last.then_inc(projected, 1)
                    pe.wait_ge(ctx_loaded[p], 16 * (i + 1))
                    for oc in range(DC):
                        for c in range(DC):
                            last = pe.matmul(ps_k[:, oc, :], wk[:, c, oc * P:(oc + 1) * P],
                                             ctx[:, p, c, :], start=(c == 0), stop=(c == DC - 1))
                    last.then_inc(projected, 1)
                    for tc in range(QC):
                        for c in range(DC):
                            pe.matmul(ps_v[:, tc, :], ctx[:, p, c, tc * P:(tc + 1) * P], wv[:, c, :],
                                      start=(c == 0), stop=False)
                        last = pe.matmul(ps_v[:, tc, :], ones[0:1, 0:P], bv, start=False, stop=True)
                    last.then_inc(projected, 1)
                    pe.wait_ge(q_ready, b + 1)
                    pe.wait_ge(k_ready, b + 1)
                    for qc in range(QC):
                        for c in range(DC):
                            last = pe.matmul(ps_s[:, qc, :], qT[:, c, qc * P:(qc + 1) * P], kT[:, c, :],
                                             start=(c == 0), stop=(c == DC - 1))
                    last.then_inc(scored, 1)
                    pe.wait_ge(probs_ready, b + 1)
                    for kc in range(QC):
                        for qc in range(QC):
                            last = pe.transpose(ps_pT[:, kc, qc * P:(qc + 1) * P],
                                                probs[:, qc, kc * P:(kc + 1) * P], ident[:, :])
                    last.then_inc(turned, 1)
                    pe.wait_ge(probsT_ready, b + 1)
                    pe.wait_ge(v_ready, b + 1)
                    pe.wait_ge(added, b + 1)
                    for qc in range(QC):
                        for kc in range(QC):
                            last = pe.matmul(ps_o[:, qc, :], probsT[:, kc, qc * P:(qc + 1) * P], vv[:, kc, :],
                                             start=(kc == 0), stop=(kc == QC - 1))
                    last.then_inc(mixed, 1)

        @block.scalar
        def _(act):
            with act.Fori(0, B) as b:
                act.wait_ge(projected, 3 * b + 8)
                for c in range(DC):
                    last = act.activation(kT[:, c, :], ps_k[:, c, :], ACT.Identity, bias=bk[:, c:c + 1])
                last.then_inc(k_ready, 1)
                act.wait_ge(projected, 3 * b + 9)
                act.wait_ge(added, b + 1)
                act.copy(vv[:, :, :], ps_v[:, :, :]).then_inc(v_ready, 1)
                act.wait_ge(max_ready, b + 1)
                for qc in range(QC):
                    last = act.activation(probs[:, qc, :], ps_s[:, qc, :], ACT.Exp, bias=negmax[:, qc:qc + 1],
                                          accum_out=total[:, qc:qc + 1])
                last.then_inc(probs_ready, 1)

        @block.vector
        def _(v):
            steps = Steps(v, own)
            v.sem_inc(added, 1)
            with v.Fori(0, B) as b:
                v.wait_ge(projected, 3 * b + 7)
                for c in range(DC):
                    last = v.tensor_scalar(qT[:, c, :], ps_q[:, c, :], bq[:, c:c + 1], None, ALU.add)
                last.then_inc(q_ready, 1)
                v.wait_ge(scored, b + 1)
                v.tensor_reduce(negmax[:, :], ps_s[:, :, :], X, ALU.max, negate=True).then_inc(max_ready, 1)
                v.wait_ge(turned, b + 1)
                v.tensor_copy(probsT[:, :, :], ps_pT[:, :, :]).then_inc(probsT_ready, 1)
                steps.n = b
                steps.done(v.reciprocal(inv[:, :], total[:, :]))
                v.wait_ge(mixed, b + 1)
                for qc in range(QC):
                    last = v.scalar_tensor_tensor(xn[:, 2 * b + qc, :], ps_o[:, qc, :], inv[:, qc:qc + 1],
                                                  xn[:, 2 * b + qc, :], ALU.mult, ALU.add)
                last.then_inc(added, 1)


def post_norm_stage(core, name, x, r, gain_bias):
    with Stage(core, name) as s:
        st, mean, rstd = s.sb("st", [P, TILES, 6]), s.sb("mean", [P, TILES]), s.sb("rstd", [P, TILES])
        work = s.sb("work", [P, 5, TILES])
        row = s.sb("row", [P, 4, D])
        gb = s.sb("gb", [P, 2, D])
        stats_done, var_ready, std_ready = s.sem("stats_done"), s.sem("var_ready"), s.sem("std_ready")
        own, gb_loaded, normed = s.sem("own"), s.sem("gb_loaded"), s.sem("normed")
        scaled, row_free = s.sem("scaled"), s.sem("row_free")
        block = s.block()

        @block.sync
        def _(sp):
            sp.dma_start(gb[:, :, :], gain_bias.rearrange("(o a) n -> o a n", o=1).to_broadcast([P, 2, D]))\
                .then_inc(gb_loaded, 16)

        @block.scalar
        def _(act):
            act.wait_ge(var_ready, 1)
            act.activation(work[:, 4, :], work[:, 3, :], ACT.Sqrt).then_inc(std_ready, 1)

        @block.gpsimd
        def _(pool):
            pool.sem_inc(row_free, 4)
            pool.wait_ge(gb_loaded, 16)
            with pool.Fori(0, TILES // 4) as i:
                for p in range(4):
                    t = 4 * i + p
                    pool.wait_ge(scaled, t + 1)
                    pool.tensor_tensor(row[:, p, :], row[:, p, :], gb[:, 1, :], ALU.add).then_inc(normed, 1)
                    pool.wait_ge(normed, t + 1)
                    pool.tensor_tensor(x[:, t, :], x[:, t, :], row[:, p, :], ALU.add).then_inc(row_free, 1)
            pool.wait_ge(row_free, TILES + 4)

        @block.vector
        def _(v):
            steps = Steps(v, own)
            row_statistics(v, steps, r, st, mean, rstd, work, stats_done, var_ready, std_ready)
            v.wait_ge(gb_loaded, 16)
            start = steps.n
            with v.Fori(0, TILES // 4) as i:
                for p in range(4):
                    t = 4 * i + p
                    v.wait_ge(row_free, t + 1)
                    steps.n = start + t
                    steps.done(v.tensor_scalar(row[:, p, :], r[:, t, :], mean[:, bass.ds(t, 1)],
                                               rstd[:, bass.ds(t, 1)], ALU.subtract, ALU.mult))
                    v.tensor_tensor(row[:, p, :], row[:, p, :], gb[:, 0, :], ALU.mult).then_inc(scaled, 1)



AHEAD = 4


class Tables:

    def __init__(self, core, most_tiles):
        self.row_iota = core.keep("row_iota", [P, P])
        self.column = core.keep("column", [P, 1])
        self.before = core.keep("before", [P, P])
        self.token_id = {1: core.keep("token_id1", [P, TILES]), 2: core.keep("token_id2", [P, TILES * 2])}
        self.zeros = core.keep("zeros", [P, 64])
        self.token_of = core.keep("token_of", [P, most_tiles], U32)
        self.weights_of = core.keep("weights_of", [P, most_tiles], U32)
        self.slot_of = core.keep("slot_of", [P, TILES * 2], U32)
        self.coef = core.keep("coef", [P, TILES * 2])


def route_stage(core, name, lg, E, K, NT, tb, ones, xn, xn_dram, bias=None, capacity=None, factor=1.0):
    NK = TILES * K
    with Stage(core, name) as s:
        top, top_ix = s.sb("top", [P, TILES, 8]), s.sb("top_ix", [P, TILES, 8], U32)
        expert = s.sb("expert", [P, TILES, K])
        ex, hot, pos = (s.sb(n, [P, TILES, E]) for n in ("ex", "hot", "pos"))
        hot_k = s.sb("hot_k", [P, K, TILES, E])
        picked = s.sb("picked", [P, K, TILES, E])
        ek = s.sb("ek", [P, TILES, K])
        den = s.sb("den", [P, 2, TILES])
        earlier = s.sb("earlier", [P, TILES + 1, E])
        count_i = s.sb("count_i", [P, 2, E], I32)
        tiles_of, tiles_end, first = (s.sb(n, [P, E]) for n in ("tiles_of", "tiles_end", "first"))
        ended = s.sb("ended", [P, NT, E])
        tile_expert = s.sb("tile_expert", [P, NT])
        slot = s.sb("slot", [P, TILES, K])
        kept = s.sb("kept", [P, TILES, K])
        slot_i = s.sb("slot_i", [P, 3, NK], I32)
        lo, hi = s.sb("lo", [P, NK]), s.sb("hi", [P, NK])
        lane_hot, tile_hot = s.sb("lane_hot", [P, 2, P]), s.sb("tile_hot", [P, 2, NT])
        ps_pos, ps_all = (s.psum(n, [P, 512])[:, 0:TILES * E].rearrange("p (t e) -> p t e", e=E)
                          for n in ("ps_pos", "ps_all"))
        ps_tok = s.psum("ps_tok", [P, 512])
        own, maxed, shifted, exped = s.sem("own"), s.sem("maxed"), s.sem("shifted"), s.sem("exped")
        hot_ready, counted, perm_ready = s.sem("hot_ready"), s.sem("counted"), s.sem("perm_ready")
        perm_used, xn_stored, bias_loaded = s.sem("perm_used"), s.sem("xn_stored"), s.sem("bias_loaded")
        if bias is not None:
            bias_sb = s.sb("bias", [P, E])
        block = s.block()

        @block.sync
        def _(sp):
            if bias is not None:
                sp.dma_start(bias_sb[:, :], bias.to_broadcast([P, E])).then_inc(bias_loaded, 16)
            if xn_dram is not None:
                sp.dma_start(xn_dram.rearrange("(t p) d -> p t d", p=P), xn[:, :, :]).then_inc(xn_stored, 16)
                sp.wait_ge(xn_stored, 16)

        @block.scalar
        def _(act):
            act.wait_ge(shifted, 2)
            act.activation(ex[:, :, :], ex[:, :, :], ACT.Exp).then_inc(exped, 1)
            act.activation(ek[:, :, :], ek[:, :, :], ACT.Exp).then_inc(exped, 1)

        @block.tensor
        def _(pe):
            pe.wait_ge(hot_ready, 1)
            flat = hot[:, :, :].rearrange("p t e -> p (t e)")
            pe.matmul(ps_pos.rearrange("p t e -> p (t e)"), tb.before[:, :], flat)
            pe.matmul(ps_all.rearrange("p t e -> p (t e)"), ones[:, :], flat).then_inc(counted, 1)
            out = ps_tok[:, 0:NT]
            pe.sem_inc(perm_used, 2)
            pe.matmul(out, ones[:, :], tb.zeros[:, 0:NT], start=True, stop=False, skip_group_check=True)
            with pe.Fori(0, NK // 2) as i:
                for p in range(2):
                    pe.wait_ge(perm_ready, 2 * i + p + 1)
                    pe.matmul(out, lane_hot[:, p, :], tile_hot[:, p, :], start=False, stop=False,
                              skip_group_check=True).then_inc(perm_used, 1)
            pe.matmul(out, ones[:, :], tb.zeros[:, 0:NT], start=False, stop=True,
                      skip_group_check=True).then_inc(perm_used, 1)

        @block.vector
        def _(v):
            steps = Steps(v, own)
            over_e = lambda ap: ap.unsqueeze(2).to_broadcast([P, TILES, E])
            if bias is not None:
                v.wait_ge(bias_loaded, 16)
                steps.done(v.tensor_tensor(lg, lg, bias_sb[:, :].unsqueeze(1).to_broadcast([P, TILES, E]),
                                           ALU.add))
            for t in range(TILES):
                v.max(top[:, t, :], lg[:, t, :]).then_inc(maxed, 1)
            v.wait_ge(maxed, TILES)
            for t in range(TILES):
                v.max_index(top_ix[:, t, :], top[:, t, :], lg[:, t, :]).then_inc(maxed, 1)
            v.tensor_tensor(ex[:, :, :], lg, over_e(top[:, :, 0]), ALU.subtract).then_inc(shifted, 1)
            v.tensor_tensor(ek[:, :, :], top[:, :, 0:K], top[:, :, 0:1].to_broadcast([P, TILES, K]),
                            ALU.subtract).then_inc(shifted, 1)
            v.wait_ge(maxed, 2 * TILES)
            steps.done(v.tensor_copy(expert[:, :, :], top_ix[:, :, 0:K]))
            for k in range(K):
                last = v.tensor_tensor(hot_k[:, k, :, :],
                                       tb.row_iota[:, 0:E].unsqueeze(1).to_broadcast([P, TILES, E]),
                                       over_e(expert[:, :, k]), ALU.is_equal)
            steps.done(last)
            if K == 2:
                v.tensor_tensor(hot[:, :, :], hot_k[:, 0, :, :], hot_k[:, 1, :, :], ALU.add)\
                    .then_inc(hot_ready, 1)
            else:
                v.tensor_copy(hot[:, :, :], hot_k[:, 0, :, :]).then_inc(hot_ready, 1)
            v.wait_ge(exped, 2)
            steps.done(v.reduce_sum(den[:, 0, :], ex[:, :, :], X))
            steps.done(v.reciprocal(den[:, 1, :], den[:, 0, :]))
            coef = tb.coef[:, 0:NK].rearrange("p (t k) -> p t k", k=K)
            steps.done(v.tensor_tensor(coef, ek[:, :, :], den[:, 1, :].unsqueeze(2).to_broadcast([P, TILES, K]),
                                       ALU.mult))
            if factor != 1.0:
                steps.done(v.tensor_scalar(tb.coef[:, 0:NK], tb.coef[:, 0:NK], factor, None, ALU.mult))
            v.memset(earlier[:, 0, :], 0.0).then_inc(own, 1)
            steps.n += 1
            v.wait_ge(own, steps.n)
            v.wait_ge(counted, 1)
            for t in range(TILES):
                steps.done(v.tensor_tensor(earlier[:, t + 1, :], earlier[:, t, :], ps_all[:, t, :], ALU.add))
            steps.done(v.tensor_tensor(pos[:, :, :], ps_pos[:, :, :], earlier[:, 0:TILES, :], ALU.add))
            if capacity is None:
                steps.done(v.tensor_scalar(count_i[:, 0, :], earlier[:, TILES, :], float(P - 1), None, ALU.add))
                steps.done(v.tensor_scalar(count_i[:, 1, :], count_i[:, 0, :], 7, None, ALU.logical_shift_right))
                steps.done(v.tensor_copy(tiles_of[:, :], count_i[:, 1, :]))
                steps.done(v.tensor_tensor_scan(tiles_end[:, :], ones[:, 0:E], tiles_of[:, :], 0.0,
                                                ALU.mult, ALU.add))
                steps.done(v.tensor_tensor(first[:, :], tiles_end[:, :], tiles_of[:, :], ALU.subtract))
                steps.done(v.tensor_scalar(first[:, :], first[:, :], float(P), None, ALU.mult))
                steps.done(v.tensor_tensor(pos[:, :, :], pos[:, :, :],
                                           first[:, :].unsqueeze(1).to_broadcast([P, TILES, E]), ALU.add))
                steps.done(v.tensor_tensor(ended[:, :, :], tiles_end[:, :].unsqueeze(1).to_broadcast([P, NT, E]),
                                           tb.row_iota[:, 0:NT].unsqueeze(2).to_broadcast([P, NT, E]),
                                           ALU.is_le))
                steps.done(v.reduce_sum(tile_expert[:, :], ended[:, :, :], X))
                steps.done(v.tensor_scalar(tile_expert[:, :], tile_expert[:, :], float(E - 1), float(P),
                                           ALU.min, ALU.mult))
            else:
                steps.done(v.tensor_scalar(tile_expert[:, :], tb.row_iota[:, 0:NT], float(P), None, ALU.mult))
            v.tensor_scalar(tb.weights_of[:, 0:NT], tile_expert[:, :], tb.column[:, 0:1], None, ALU.add)
            for k in range(K):
                last = v.tensor_tensor(picked[:, k, :, :], hot_k[:, k, :, :], pos[:, :, :], ALU.mult)
            steps.done(last)
            for k in range(K):
                last = v.reduce_sum(slot[:, :, k], picked[:, k, :, :], X)
            steps.done(last)
            slots = slot[:, :, :].rearrange("p t k -> p (t k)")
            kept_k = kept[:, :, :].rearrange("p t k -> p (t k)")
            if capacity is None:
                steps.done(v.tensor_copy(slot_i[:, 0, :], slots))
                v.tensor_copy(tb.slot_of[:, 0:NK], slots)
                v.tensor_scalar(slot_i[:, 1, :], slot_i[:, 0, :], P - 1, None, ALU.bitwise_and)
                steps.done(v.tensor_scalar(slot_i[:, 2, :], slot_i[:, 0, :], 7, None, ALU.logical_shift_right))
                v.tensor_copy(lo[:, :], slot_i[:, 1, :])
                steps.done(v.tensor_copy(hi[:, :], slot_i[:, 2, :]))
            else:
                steps.done(v.tensor_scalar(kept_k, slots, float(capacity), None, ALU.is_lt))
                v.tensor_tensor(tb.coef[:, 0:NK], tb.coef[:, 0:NK], kept_k, ALU.mult)
                v.tensor_copy(lo[:, :], slots)
                steps.done(v.tensor_copy(hi[:, :], expert[:, :, :].rearrange("p t k -> p (t k)")))
                steps.done(v.tensor_scalar(slots, slots, float(capacity - 1), None, ALU.min))
                v.scalar_tensor_tensor(tb.slot_of[:, 0:NK], hi[:, :], float(capacity), slots,
                                       ALU.mult, ALU.add)
            start = steps.n
            with v.Fori(0, NK // 2) as i:
                for p in range(2):
                    n = 2 * i + p
                    v.wait_ge(perm_used, n + 1)
                    v.tensor_scalar(tile_hot[:, p, :], tb.row_iota[:, 0:NT], hi[:, bass.ds(n, 1)],
                                    tb.token_id[K][:, bass.ds(n, 1)], ALU.is_equal, ALU.mult)
                    v.tensor_scalar(lane_hot[:, p, :], tb.row_iota[:, :], lo[:, bass.ds(n, 1)], None,
                                    ALU.is_equal).then_inc(perm_ready, 1)
            v.wait_ge(perm_used, NK + 3)
            v.tensor_copy(tb.token_of[:, 0:NT], ps_tok[:, 0:NT])


def experts_stage(core, name, NT, rows, chunks, w_dram, tb, xn_dram, y_dram, ident, ones, biased=False):
    F = sum(chunks)
    NF = len(chunks)
    W = w_dram.shape[1]
    HB = -(-NF * P // 512)
    with Stage(core, name) as s:
        w = s.sb("w", [P, AHEAD, W])
        xg, xT = s.sb("xg", [P, AHEAD, D]), s.sb("xT", [P, 2, DC, P])
        x_ix, w_ix = s.sb("x_ix", [P, AHEAD, 1], U32), s.sb("w_ix", [P, AHEAD, 1], U32)
        h = s.sb("h", [P, 2, NF, rows])
        y = s.sb("y", [P, 2, D])
        ps_x = s.psum("ps_x", [P, 2, 512])
        ps_g = s.psum("ps_g", [P, 2, HB * 512])
        if not biased:
            silu = s.sb("silu", [P, 2, NF, rows])
            ps_u = s.psum("ps_u", [P, 2, HB * 512])
        ps_y = s.psum("ps_y", [P, 2, 512])
        x_in, w_in = ([s.sem(f"{n}{u}") for u in range(AHEAD)] for n in ("x_in", "w_in"))
        stored = [s.sem(f"stored{p}") for p in range(2)]
        ix_ready, ix_passed = s.sem("ix_ready"), s.sem("ix_passed")
        turned, xT_ready = s.sem("turned"), s.sem("xT_ready")
        gu_ready, silu_ready, h_ready = s.sem("gu_ready"), s.sem("silu_ready"), s.sem("h_ready")
        y_ready, y_copied = s.sem("y_ready"), s.sem("y_copied")
        block = s.block()

        gate_w = lambda p: w[:, p, 0:DC * F].rearrange("p (c f) -> p c f", c=DC)
        up_w = lambda p: w[:, p, DC * F:2 * DC * F].rearrange("p (c f) -> p c f", c=DC)
        down_at = DC * F if biased else 2 * DC * F
        down_w = lambda p: w[:, p, down_at:down_at + NF * D].rearrange("p (j n) -> p j n", j=NF)
        b1 = lambda p, j: w[:, p, down_at + NF * D + j:down_at + NF * D + j + 1]
        b2 = lambda p: w[0:1, p, down_at + NF * D + NF:down_at + NF * D + NF + D]

        @block.gpsimd
        def _(pool):
            with pool.Fori(0, NT // AHEAD) as i:
                for u in range(AHEAD):
                    j = AHEAD * i + u
                    pool.wait_ge(y_ready, j + 1)
                    pool.tensor_copy(x_ix[:, u, :], tb.token_of[:, bass.ds(j, 1)])
                    pool.tensor_copy(w_ix[:, u, :], tb.weights_of[:, bass.ds(j, 1)]).then_inc(ix_ready, 1)
                    pool.wait_ge(ix_ready, j + 1)
                    pool.sem_inc(ix_passed, 1)
                    pool.indirect_dma_start(xg[:, u, :], None, xn_dram,
                                            bass.IndirectOffsetOnAxis(ap=x_ix[:, u, :], axis=0))\
                        .then_inc(x_in[u], 16)
                    pool.indirect_dma_start(w[:, u, :], None, w_dram,
                                            bass.IndirectOffsetOnAxis(ap=w_ix[:, u, :], axis=0))\
                        .then_inc(w_in[u], 16)

        @block.tensor
        def _(pe):
            pe.sem_inc(y_ready, AHEAD)

            def turn_rows(i, u):
                pe.wait_ge(x_in[u], 16 * (i + 1))
                for c in range(DC):
                    last = pe.transpose(ps_x[:, u % 2, c * P:(c + 1) * P], xg[:, u, c * P:(c + 1) * P], ident[:, :])
                last.then_inc(turned, 1)

            def hidden_layer(i, u):
                p = u % 2
                pe.wait_ge(xT_ready, AHEAD * i + u + 1)
                pe.wait_ge(w_in[u], 16 * (i + 1))
                for ps, wt in ((ps_g, gate_w(u)),) if biased else ((ps_g, gate_w(u)), (ps_u, up_w(u))):
                    for j, m in enumerate(chunks):
                        for c in range(DC):
                            last = pe.matmul(ps[0:m, p, j * P:j * P + rows], wt[:, c, j * P:j * P + m],
                                             xT[:, p, c, 0:rows], start=(c == 0), stop=(c == DC - 1))
                last.then_inc(gu_ready, 1)

            def output_layer(i, u):
                p = u % 2
                pe.wait_ge(h_ready, AHEAD * i + u + 3)
                pe.wait_ge(y_copied, AHEAD * i + u + 1)
                for j, m in enumerate(chunks):
                    last = pe.matmul(ps_y[0:rows, p, 0:D], h[0:m, p, j, :], down_w(u)[0:m, j, :],
                                     start=(j == 0), stop=(j == NF - 1 and not biased))
                if biased:
                    last = pe.matmul(ps_y[0:rows, p, 0:D], ones[0:1, 0:rows], b2(u), start=False, stop=True)
                last.then_inc(y_ready, 1)

            with pe.Fori(0, NT // AHEAD) as i:
                for step in range(AHEAD + 2):
                    for lag, part in enumerate((turn_rows, hidden_layer, output_layer)):
                        if 0 <= step - lag < AHEAD:
                            part(i, step - lag)

        def parts():
            full = [j for j, m in enumerate(chunks) if m == P]
            if full:
                yield P, 0, len(full)
            if len(full) < NF:
                yield chunks[-1], len(full), NF

        def hidden(ps, p, m, a, b):
            return ps[0:m, p, a * P:b * P].rearrange("p (j n) -> p j n", n=P)[:, :, 0:rows]

        @block.scalar
        def _(act):
            if biased:
                act.sem_inc(h_ready, 2)

            def copy_rows(i, u):
                act.wait_ge(turned, AHEAD * i + u + 1)
                act.copy(xT[:, u % 2, :, :], ps_x[:, u % 2, 0:D].rearrange("p (c n) -> p c n", c=DC))\
                    .then_inc(xT_ready, 1)

            def nonlinear(i, u):
                p, j = u % 2, AHEAD * i + u
                act.wait_ge(gu_ready, j + 1)
                if biased:
                    act.wait_ge(y_ready, j + AHEAD - 1)
                    for c in range(NF):
                        last = act.activation(h[:, p, c, :], ps_g[:, p, c * P:c * P + rows], ACT.Silu,
                                              bias=b1(u, c))
                    last.then_inc(h_ready, 1)
                else:
                    act.wait_ge(h_ready, j + 1)
                    for m, a, b in parts():
                        last = act.activation(silu[0:m, p, a:b, :], hidden(ps_g, p, m, a, b), ACT.Silu)
                    last.then_inc(silu_ready, 1)

            with act.Fori(0, NT // AHEAD) as i:
                for step in range(AHEAD + 1):
                    if step < AHEAD:
                        copy_rows(i, step)
                    if step >= 1:
                        nonlinear(i, step - 1)

        @block.vector
        def _(v):
            if not biased:
                v.sem_inc(h_ready, 2)
            v.sem_inc(y_copied, 2)

            def multiply(i, u):
                p = u % 2
                v.wait_ge(silu_ready, AHEAD * i + u + 1)
                for m, a, b in parts():
                    last = v.tensor_tensor(h[0:m, p, a:b, :], hidden(ps_u, p, m, a, b), silu[0:m, p, a:b, :],
                                           ALU.mult)
                last.then_inc(h_ready, 1)

            def copy_out(i, u):
                v.wait_ge(y_ready, AHEAD * i + u + 1 + AHEAD)
                v.wait_ge(stored[u % 2], 16 * (AHEAD // 2 * i + u // 2 + 1))
                v.tensor_copy(y[0:rows, u % 2, :], ps_y[0:rows, u % 2, 0:D]).then_inc(y_copied, 1)

            with v.Fori(0, NT // AHEAD) as i:
                for step in range(AHEAD + 1):
                    if step < AHEAD and not biased:
                        multiply(i, step)
                    if step >= 1:
                        copy_out(i, step - 1)

        @block.sync
        def _(sp):
            for p in range(2):
                sp.sem_inc(stored[p], 16)
            with sp.Fori(0, NT // 2) as i:
                for p in range(2):
                    j = 2 * i + p
                    sp.wait_ge(y_copied, j + 3)
                    sp.dma_start(y_dram[dyn(j, rows), :], y[0:rows, p, :]).then_inc(stored[p], 16)
            for p in range(2):
                sp.wait_ge(stored[p], 16 * (NT // 2 + 1))


def combine_stage(core, name, K, tb, y_dram, x, xn=None):
    with Stage(core, name) as s:
        yg = s.sb("yg", [P, 2, K, D])
        ix = s.sb("ix", [P, 2, K], U32)
        y_in = [[s.sem(f"y_in{p}{k}") for k in range(K)] for p in range(2)]
        ix_ready, ix_passed, used, own = s.sem("ix_ready"), s.sem("ix_passed"), s.sem("used"), s.sem("own")
        block = s.block()

        @block.gpsimd
        def _(pool):
            with pool.Fori(0, TILES // 2) as i:
                for p in range(2):
                    t = 2 * i + p
                    pool.wait_ge(used, t + 1)
                    pool.tensor_copy(ix[:, p, :], tb.slot_of[:, dyn(t, K)]).then_inc(ix_ready, 1)
                    pool.wait_ge(ix_ready, t + 1)
                    pool.sem_inc(ix_passed, 1)
                    for k in range(K):
                        pool.indirect_dma_start(yg[:, p, k, :], None, y_dram,
                                                bass.IndirectOffsetOnAxis(ap=ix[:, p, k:k + 1], axis=0))\
                            .then_inc(y_in[p][k], 16)

        @block.vector
        def _(v):
            v.sem_inc(used, 2)
            if xn is not None:
                v.tensor_tensor(x[:, :, :], x[:, :, :], xn[:, :, :], ALU.add).then_inc(own, 1)
                v.wait_ge(own, 1)
            first = 1 if xn is not None else 0
            with v.Fori(0, TILES // 2) as i:
                for p in range(2):
                    t = 2 * i + p
                    for k in range(K):
                        v.wait_ge(y_in[p][k], 16 * (i + 1))
                        if k == K - 1:
                            if K == 2:
                                v.wait_ge(own, first + t + 1)
                            v.scalar_tensor_tensor(x[:, t, :], yg[:, p, k, :], tb.coef[:, bass.ds(t * K + k, 1)],
                                                   x[:, t, :], ALU.mult, ALU.add).then_inc(used, 1)
                        else:
                            v.scalar_tensor_tensor(x[:, t, :], yg[:, p, k, :], tb.coef[:, bass.ds(t * K + k, 1)],
                                                   x[:, t, :], ALU.mult, ALU.add).then_inc(own, 1)


def shared_stage(core, name, xnT, gate_logit, w_dram, x):
    F = 704
    chunks = [P] * (F // P) + [F % P]
    NF = len(chunks)
    BANKS = NF // 2

    def bank_parts(n):
        return ((P, 2 * n, 2 * n + 2),) if chunks[2 * n + 1] == P else ((P, 2 * n, 2 * n + 1),
                                                                       (chunks[-1], 2 * n + 1, 2 * n + 2))

    with Stage(core, name) as s:
        w = s.sb("w", [P, w_dram.shape[1]])
        gate_w = w[:, 0:DC * F].rearrange("p (c f) -> p c f", c=DC)
        up_w = w[:, DC * F:2 * DC * F].rearrange("p (c f) -> p c f", c=DC)
        down_w = w[:, 2 * DC * F:].rearrange("p (j n) -> p j n", j=NF)
        silu, h = s.sb("silu", [P, NF, SEQ]), s.sb("h", [P, NF, SEQ])
        share = s.sb("share", [P, TILES])
        ps_g, ps_u, ps_y = (s.psum(n, [P, m, 256]) for n, m in (("ps_g", NF), ("ps_u", NF), ("ps_y", 2)))
        w_loaded, share_ready, gu_ready, silu_ready = (s.sem(n) for n in
                                                       ("w_loaded", "share_ready", "gu_ready", "silu_ready"))
        h_ready, y_ready, added = s.sem("h_ready"), s.sem("y_ready"), s.sem("added")
        block = s.block()

        @block.sync
        def _(sp):
            sp.dma_start(w[:, :], w_dram).then_inc(w_loaded, 16)

        @block.tensor
        def _(pe):
            pe.wait_ge(w_loaded, 16)
            with pe.Fori(0, B) as b:
                for j, m in enumerate(chunks):
                    for ps, wt in ((ps_g, gate_w), (ps_u, up_w)):
                        for c in range(DC):
                            last = pe.matmul(ps[0:m, j, :], wt[:, c, j * P:j * P + m], xnT[:, c, dyn(b, SEQ)],
                                             start=(c == 0), stop=(c == DC - 1))
                    if j % 2:
                        last.then_inc(gu_ready, 1)
                pe.wait_ge(h_ready, BANKS * (b + 1))
                pe.wait_ge(added, b + 1)
                for q in range(QC):
                    for j, m in enumerate(chunks):
                        last = pe.matmul(ps_y[:, q, :], h[0:m, j, q * P:(q + 1) * P], down_w[0:m, j, :],
                                         start=(j == 0), stop=(j == NF - 1))
                last.then_inc(y_ready, 1)

        @block.scalar
        def _(act):
            act.activation(share[:, :], gate_logit, ACT.Sigmoid).then_inc(share_ready, 1)
            with act.Fori(0, B) as b:
                for n in range(BANKS):
                    act.wait_ge(gu_ready, b * BANKS + n + 1)
                    for m, j0, j1 in bank_parts(n):
                        last = act.activation(silu[0:m, j0:j1, :], ps_g[0:m, j0:j1, :], ACT.Silu)
                    last.then_inc(silu_ready, 1)

        @block.vector
        def _(v):
            v.sem_inc(added, 1)
            v.wait_ge(share_ready, 1)
            with v.Fori(0, B) as b:
                for n in range(BANKS):
                    v.wait_ge(silu_ready, b * BANKS + n + 1)
                    for m, j0, j1 in bank_parts(n):
                        last = v.tensor_tensor(h[0:m, j0:j1, :], ps_u[0:m, j0:j1, :], silu[0:m, j0:j1, :],
                                               ALU.mult)
                    last.then_inc(h_ready, 1)
                v.wait_ge(y_ready, b + 1)
                for q in range(QC):
                    t = 2 * b + q
                    last = v.scalar_tensor_tensor(x[:, t, :], ps_y[:, q, :], share[:, bass.ds(t, 1)],
                                                  x[:, t, :], ALU.mult, ALU.add)
                last.then_inc(added, 1)



GW = GH * LANE
GV = GH * HD
PAIRS = B // 2
BODY = 2 * GH
PLAIN, MASKED, CONV = range(3)


def heads_stage(core, name, mode, xnT, ctxT, w_dram, dst, ident, mask=None, ident16=None, kernels=None,
                ones=None):
    WQ, WK, WV = DC * GW, 2 * DC * GW, 2 * DC * GW + DC * GV
    conv = mode == CONV
    with Stage(core, name) as s:
        w = s.sb("w", [P, 2, w_dram.shape[1]])
        ctx = s.sb("ctx", [P, 2, DC, SEQ])
        qT, kT, vv = s.sb("qT", [P, 2, SEQ]), s.sb("kT", [P, 2, SEQ]), s.sb("v", [P, 2, QC, GV])
        probs, probsT = s.sb("probs", [P, 2, QC, SEQ]), s.sb("probsT", [P, 2, QC, SEQ])
        negmax = s.sb("negmax", [P, 2, QC])
        total, inv = s.sb("total", [P, BODY, QC]), s.sb("inv", [P, BODY, QC])
        mixed_sb = s.sb("mixed_sb", [P, 2, QC, GH, HD])
        ps_s, ps_t, ps_o = (s.psum(n, [P, 2, 512]) for n in ("ps_s", "ps_t", "ps_o"))
        in_ready = [s.sem("in_ready0"), s.sem("in_ready1")]
        projected, placed, scored, maxed = (s.sem(n) for n in ("projected", "placed", "scored", "maxed"))
        exped, turned, probsT_ready, mixed, own = (s.sem(n) for n in
                                                   ("exped", "turned", "probsT_ready", "mixed", "own"))
        loads = 2
        if mode == MASKED:
            mask_in = s.sb("mask_in", [P, 2, QC * SEQ], I32)
            mask_add = s.sb("mask_add", [P, 2, QC * SEQ], BF16)
            loads = 3
        if conv:
            mask_in = s.sb("mask_in", [P, 2, QC * SEQ], U8)
            keepT = s.sb("keepT", [P, QC, SEQ])
            mask_add = s.sb("mask_add", [P, QC * SEQ], BF16)
            shifts = s.sb("shifts", [P, TAPS, P + 2])
            band = s.sb("band", [P, 2, TAPS, P + 2])
            taps = s.sb("taps", [P, 2, GH, TAPS * TAPS])
            sT = s.sb("sT", [P, 2, QC, SEQ + 2])
            ps_c = s.psum("ps_c", [P, 2, 512])
            masks_loaded, masks_ready, shifts_ready = s.sem("masks_loaded"), s.sem("masks_ready"), s.sem("shifts_ready")
            masked, convolved, band_free, band_begun, band_ready, taps_ready = (
                s.sem(n) for n in ("masked", "convolved", "band_free", "band_begun", "band_ready", "taps_ready"))
        block = s.block()

        def bias(p, at):
            return w[:, p, WV + at:WV + at + 1]

        def tap(h, dq, d):
            return taps[:, h // GH, h % GH, dq * TAPS + d:dq * TAPS + d + 1]

        @block.sync
        def _(sp):
            if conv:
                sp.dma_start(mask_in[:, :, :], mask.rearrange("p (a n) -> p a n", a=2)).then_inc(masks_loaded, 16)
            with sp.Fori(0, GROUPS) as g:
                with sp.Fori(0, PAIRS) as i:
                    for p in range(2):
                        b = 2 * i + p
                        sp.wait_ge(placed, 2 * (g * PAIRS + i) + p + 1)
                        sp.dma_start(w[:, p, :], w_dram[dyn(g), :]).then_inc(in_ready[p], 16)
                        if ctxT is None:
                            sp.dma_start(ctx[:, p, :, :], xnT[:, :, dyn(b, SEQ)]).then_inc(in_ready[p], 16)
                        else:
                            sp.dma_start(ctx[:, p, :, :].rearrange("p c n -> p (c n)"), ctxT[dyn(b), :])\
                                .then_inc(in_ready[p], 16)
                        if mode == MASKED:
                            sp.dma_start(mask_in[:, p, :], mask[dyn(b), :]).then_inc(in_ready[p], 16)

        @block.tensor
        def _(pe):
            pe.sem_inc(turned, 2)
            pe.sem_inc(mixed, 2)
            if conv:
                pe.sem_inc(convolved, 2)
                pe.wait_ge(masks_ready, 1)

            def project(p, g, i):
                pe.wait_ge(in_ready[p], 16 * loads * (g * PAIRS + i + 1))
                for c in range(DC):
                    pe.matmul(ps_s[:, p, 0:SEQ], w[:, p, c * GW:(c + 1) * GW], xnT[:, c, dyn(2 * i + p, SEQ)],
                              start=(c == 0), stop=(c == DC - 1))
                for c in range(DC):
                    pe.matmul(ps_s[:, p, SEQ:2 * SEQ], w[:, p, WQ + c * GW:WQ + (c + 1) * GW], ctx[:, p, c, :],
                              start=(c == 0), stop=(c == DC - 1))
                for tc in range(QC):
                    out = ps_t[:, p, tc * GV:(tc + 1) * GV]
                    for c in range(DC):
                        pe.matmul(out, ctx[:, p, c, tc * P:(tc + 1) * P], w[:, p, WK + c * GV:WK + (c + 1) * GV],
                                  start=(c == 0), stop=False)
                    last = pe.matmul(out, ones[0:1, 0:P], w[0:1, p, WV + 2:WV + 2 + GV], start=False, stop=True)
                last.then_inc(projected, 1)

            def score(h, done):
                p, r = h // GH, slice(LANE * (h % GH), LANE * (h % GH) + HD)
                out = ps_s[:, h % 2, :]
                if conv:
                    pe.wait_ge(masked, done + h + 1)
                    for kc in range(QC):
                        last = pe.matmul(out[:, kc * SEQ:(kc + 1) * SEQ], kT[r, p, kc * P:(kc + 1) * P], qT[r, p, :],
                                         start=True, stop=True)
                else:
                    pe.wait_ge(exped, done + h + 1)
                    if mode == MASKED:
                        pe.matmul(out, ident16[:, :], mask_add[:, p, :], start=True, stop=False,
                                  skip_group_check=True)
                    for qc in range(QC):
                        last = pe.matmul(out[:, qc * SEQ:(qc + 1) * SEQ], qT[r, p, qc * P:(qc + 1) * P], kT[r, p, :],
                                         start=(mode == PLAIN), stop=(qc == QC - 1 or mode == PLAIN),
                                         skip_group_check=True)
                last.then_inc(scored, 1)

            def convolve(h, done):
                out = ps_c[:, h % 2, :]
                pe.wait_ge(exped, done + h + 1)
                pe.matmul(out, ident16[:, :], mask_add[:, :], start=True, stop=False, skip_group_check=True)
                pe.wait_ge(masked, done + h + 3)
                pe.wait_ge(band_ready, done + h + 1)
                for qc in range(QC):
                    for kc in range(QC):
                        k0, k1 = max(kc * P - 1, 0), min(kc * P + P + 1, SEQ)
                        w0 = k0 - (kc * P - 1)
                        for dq in range(TAPS):
                            last = pe.matmul(out[:, qc * SEQ + k0:qc * SEQ + k1],
                                             sT[:, h % 2, kc, qc * P + dq:qc * P + dq + P],
                                             band[:, h % 2, dq, w0:w0 + k1 - k0], start=False,
                                             stop=(qc == kc == QC - 1 and dq == TAPS - 1), skip_group_check=True)
                last.then_inc(convolved, 1)

            def turn(h, done):
                pe.wait_ge(exped, done + h + 3)
                pe.wait_ge(probsT_ready, done + h + 1)
                for kc in range(QC):
                    for qc in range(QC):
                        last = pe.transpose(ps_t[:, h % 2, kc * SEQ + qc * P:kc * SEQ + (qc + 1) * P],
                                            probs[:, h % 2, qc, kc * P:(kc + 1) * P], ident[:, :])
                last.then_inc(turned, 1)

            def mix(h, done):
                p, j = h // GH, h % GH
                pe.wait_ge(probsT_ready, done + h + 3)
                for qc in range(QC):
                    for kc in range(QC):
                        last = pe.matmul(ps_o[:, p, (qc * GH + j) * HD:(qc * GH + j + 1) * HD],
                                         probsT[:, h % 2, kc, qc * P:(qc + 1) * P],
                                         vv[:, p, kc, j * HD:(j + 1) * HD],
                                         start=(kc == 0), stop=(kc == QC - 1), skip_group_check=True)
                last.then_inc(mixed, 1)

            parts = (score, convolve, turn, mix) if conv else (score, turn, mix)
            with pe.Fori(0, GROUPS) as g:
                with pe.Fori(0, PAIRS) as i:
                    turns = g * PAIRS + i
                    for p in range(2):
                        project(p, g, i)
                    pe.wait_ge(placed, 2 * turns + 4)
                    for step in range(BODY + len(parts) - 1):
                        for lag, part in enumerate(parts):
                            if 0 <= step - lag < BODY:
                                part(step - lag, BODY * turns)

        def copy_turned(engine, copy, h, done):
            engine.wait_ge(turned, done + h + 3)
            engine.wait_ge(mixed, done + h + 1)
            copy(probsT[:, h % 2, :, :], ps_t[:, h % 2, :].rearrange("p (k n) -> p k n", k=QC))\
                .then_inc(probsT_ready, 1)

        @block.scalar
        def _(act):
            act.sem_inc(exped, 2)
            if conv:
                act.sem_inc(probsT_ready, 2)
            with act.Fori(0, GROUPS) as g:
                with act.Fori(0, PAIRS) as i:
                    done = BODY * (g * PAIRS + i)
                    for step in range(BODY + conv):
                        h = step
                        if h < BODY:
                            act.wait_ge(maxed, done + h + 1)
                            act.wait_ge(turned, done + h + 1)
                            ps = (ps_c if conv else ps_s)[:, h % 2, :]
                            for qc in range(QC):
                                last = act.activation(probs[:, h % 2, qc, :], ps[:, qc * SEQ:(qc + 1) * SEQ], ACT.Exp,
                                                      bias=negmax[:, h % 2, qc:qc + 1],
                                                      accum_out=total[:, h, qc:qc + 1])
                            last.then_inc(exped, 1)
                        if conv and step >= 1:
                            copy_turned(act, act.copy, step - 1, done)

        if conv:
            @block.gpsimd
            def _(pool):
                pool.memset(sT[:, :, :, :], 0.0)
                pool.memset(shifts[:, :, :], 0.0).then_inc(shifts_ready, 1)
                pool.wait_ge(shifts_ready, 1)
                for d in range(TAPS):
                    last = pool.affine_select(out=shifts[:, d, :], in_=shifts[:, d, :], compare_op=ALU.not_equal,
                                              fill=1.0, base=d - 2, pattern=[[1, P + 2]], channel_multiplier=-1)
                last.then_inc(shifts_ready, 1)
                pool.wait_ge(shifts_ready, 2)
                with pool.Fori(0, GROUPS) as g:
                    with pool.Fori(0, PAIRS) as i:
                        done = BODY * (g * PAIRS + i)
                        pool.wait_ge(convolved, done + 2)
                        for p in range(2):
                            last = pool.tensor_copy(
                                taps[:, p, :, :].rearrange("p j t -> p (j t)"),
                                kernels[:, dyn((2 * i + p) * GROUPS + g, GH * TAPS * TAPS)])
                        last.then_inc(taps_ready, 1)
                        pool.wait_ge(taps_ready, g * PAIRS + i + 1)
                        for h in range(BODY):
                            pool.wait_ge(convolved, done + h + 1)
                            pool.sem_inc(band_free, 1)
                            for dq in range(TAPS):
                                last = pool.tensor_scalar(band[:, h % 2, dq, :], shifts[:, 0, :], tap(h, dq, 0), None,
                                                          ALU.mult)
                            last.then_inc(band_begun, 1)

        @block.vector
        def _(v):
            steps = Steps(v, own)
            v.sem_inc(placed, 2)
            if conv:
                v.sem_inc(masked, 2)
                v.wait_ge(masks_loaded, 16)
                v.tensor_scalar(keepT[:, :, :].rearrange("p k n -> p (k n)"), mask_in[:, 1, :], -1.0, 1.0,
                                ALU.mult, ALU.add).then_inc(own, 1)
                v.tensor_scalar(mask_add[:, :], mask_in[:, 0, :], NEG_BIG, None, ALU.mult).then_inc(masks_ready, 1)
                v.wait_ge(own, 1)
                v.wait_ge(shifts_ready, 1)
            else:
                v.sem_inc(probsT_ready, 2)
            first = steps.n + conv
            per_turn = 2 * (2 + (mode == MASKED)) + BODY * conv

            def place(p, turns):
                v.wait_ge(projected, 2 * turns + p + 1)
                v.tensor_scalar(qT[:, p, :], ps_s[:, p, 0:SEQ], bias(p, 0), HD ** -0.5, ALU.add, ALU.mult)
                v.tensor_scalar(kT[:, p, :], ps_s[:, p, SEQ:2 * SEQ], bias(p, 1), None, ALU.add)
                if mode == MASKED:
                    v.tensor_scalar(mask_add[:, p, :], mask_in[:, p, :], 0.0, -1.0e9, ALU.is_equal, ALU.mult)
                v.tensor_copy(vv[:, p, :, :], ps_t[:, p, 0:QC * GV].rearrange("p (k n) -> p k n", k=QC))\
                    .then_inc(placed, 1)

            def drop_masked(h, done):
                v.wait_ge(scored, done + h + 1)
                v.wait_ge(convolved, done + h + 1)
                v.tensor_tensor(sT[:, h % 2, :, 1:SEQ + 1], ps_s[:, h % 2, :].rearrange("p (k n) -> p k n", k=QC),
                                keepT[:, :, :], ALU.mult).then_inc(masked, 1)

            def widen_band(h, done):
                v.wait_ge(band_begun, done + h + 1)
                for d in range(1, TAPS):
                    for dq in range(TAPS):
                        out = band[:, h % 2, dq, :]
                        last = v.scalar_tensor_tensor(out, shifts[:, d, :], tap(h, dq, d), out, ALU.mult, ALU.add)
                    if d < TAPS - 1:
                        steps.done(last)
                last.then_inc(band_ready, 1)

            def row_max(h, done):
                ps = ps_c if conv else ps_s
                if conv:
                    v.wait_ge(convolved, done + h + 3)
                else:
                    v.wait_ge(scored, done + h + 1)
                v.tensor_reduce(negmax[:, h % 2, :], ps[:, h % 2, :].rearrange("p (k n) -> p k n", k=QC), X,
                                ALU.max, negate=True).then_inc(maxed, 1)

            def turned_back(h, done):
                copy_turned(v, v.tensor_copy, h, done)

            def finish(p, g, i, turns, done):
                v.wait_ge(mixed, done + GH * (p + 1) + 2)
                steps.done(v.reciprocal(inv[:, GH * p:GH * (p + 1), :], total[:, GH * p:GH * (p + 1), :]))
                factor = inv[:, GH * p:GH * (p + 1), :].rearrange("p j q -> p q j").unsqueeze(3)\
                    .to_broadcast([P, QC, GH, HD])
                steps.done(v.tensor_tensor(mixed_sb[:, p, :, :, :],
                                           ps_o[:, p, 0:QC * GV].rearrange("p (q j d) -> p q j d", q=QC, j=GH),
                                           factor, ALU.mult))
                out = dst[:, dyn(2 * i + p, QC), dyn(g, GV)]
                got = mixed_sb[:, p, :, :, :].rearrange("p q j d -> p q (j d)")
                if mode == MASKED:
                    steps.done(v.tensor_tensor(out, out, got, ALU.add))
                else:
                    v.tensor_copy(out, got)

            def mask_and_band(h, done):
                drop_masked(h, done)
                widen_band(h, done)

            parts = (mask_and_band, row_max) if conv else (row_max, turned_back)
            with v.Fori(0, GROUPS) as g:
                with v.Fori(0, PAIRS) as i:
                    turns = g * PAIRS + i
                    done = BODY * turns
                    steps.n = first + per_turn * turns
                    for p in range(2):
                        place(p, turns)
                    for step in range(BODY + 1):
                        for lag, part in enumerate(parts):
                            if 0 <= step - lag < BODY:
                                part(step - lag, done)
                    for p in range(2):
                        finish(p, g, i, turns, done)


def project_stage(core, name, x, mixed, w_dram, ident, ones):
    with Stage(core, name) as s:
        w = s.sb("w", [P, DC * D + D])
        row, rowT = s.sb("row", [P, 4, D]), s.sb("rowT", [P, 2, DC, P])
        ps_t, ps_y = s.psum("ps_t", [P, 2, 512]), s.psum("ps_y", [P, 2, 512])
        w_loaded, row_ready, turned, rowT_ready, summed, added = (
            s.sem(n) for n in ("w_loaded", "row_ready", "turned", "rowT_ready", "summed", "added"))
        block = s.block()

        @block.sync
        def _(sp):
            sp.dma_start(w[:, :], w_dram).then_inc(w_loaded, 16)

        @block.gpsimd
        def _(pool):
            with pool.Fori(0, TILES // 4) as i:
                for p in range(4):
                    pool.wait_ge(turned, 4 * i + p + 1)
                    pool.tensor_copy(row[:, p, :], mixed[:, 4 * i + p, :]).then_inc(row_ready, 1)

        @block.scalar
        def _(act):
            with act.Fori(0, TILES // 4) as i:
                for p in range(4):
                    act.wait_ge(turned, 4 * i + p + 5)
                    act.wait_ge(added, 4 * i + p + 1)
                    act.copy(rowT[:, p % 2, :, :], ps_t[:, p % 2, 0:D].rearrange("p (c n) -> p c n", c=DC))\
                        .then_inc(rowT_ready, 1)

        @block.tensor
        def _(pe):
            pe.sem_inc(turned, 4)
            pe.sem_inc(rowT_ready, 2)
            pe.wait_ge(w_loaded, 16)

            def turn(i, p):
                pe.wait_ge(row_ready, 4 * i + p + 1)
                pe.wait_ge(rowT_ready, 4 * i + p + 1)
                for c in range(DC):
                    last = pe.transpose(ps_t[:, p % 2, c * P:(c + 1) * P], row[:, p, c * P:(c + 1) * P], ident[:, :])
                last.then_inc(turned, 1)

            def product(i, p):
                out = ps_y[:, p % 2, 0:D]
                pe.wait_ge(rowT_ready, 4 * i + p + 3)
                for c in range(DC):
                    pe.matmul(out, rowT[:, p % 2, c, :], w[:, c * D:(c + 1) * D], start=(c == 0), stop=False)
                pe.matmul(out, ones[0:1, 0:P], w[0:1, DC * D:], start=False, stop=True).then_inc(summed, 1)

            with pe.Fori(0, TILES // 4) as i:
                for step in range(5):
                    if step < 4:
                        turn(i, step)
                    if step >= 1:
                        product(i, step - 1)

        @block.vector
        def _(v):
            v.sem_inc(added, 2)
            with v.Fori(0, TILES // 2) as i:
                for p in range(2):
                    t = 2 * i + p
                    v.wait_ge(summed, t + 1)
                    v.tensor_tensor(x[:, t, :], x[:, t, :], ps_y[:, p, 0:D], ALU.add).then_inc(added, 1)



def context_kernels_stage(core, name, ctxT, a, ident, ones, tb, kernels):
    C, A1, T9 = 2 * D, P, HEADS * TAPS * TAPS
    CC = C // P
    with Stage(core, name) as s:
        hist = s.sb("hist", [P, DC * C + C])
        gb = s.sb("gb", [P, 2, C])
        w1 = s.sb("w1", [P, CC * A1 + 3])
        kg1 = s.sb("kg1", [P, CC * D + D])
        kg_gb = s.sb("kg_gb", [P, 2, D])
        kg2 = s.sb("kg2", [P, DC * T9 + T9])
        ctx = s.sb("ctx", [P, 2, DC, SEQ])
        z = s.sb("z", [P, TILES, C])
        st = s.sb("st", [P, TILES, 6])
        mean, rstd, work = s.sb("mean", [P, TILES]), s.sb("rstd", [P, TILES]), s.sb("work", [P, 5, TILES])
        row = s.sb("row", [P, 2, C])
        rowT = s.sb("rowT", [P, 2, CC, P])
        a1 = s.sb("a1", [P, 2, P])
        pool_w = s.sb("pool_w", [1, B, SEQ])
        pool_n = s.sb("pool_n", [1, 3, B])
        w_cols = s.sb("w_cols", [P, TILES, B])
        cc, ccT = s.sb("cc", [B, C]), s.sb("ccT", [P, CC, B])
        k1, k1T = s.sb("k1", [B, D]), s.sb("k1T", [P, DC, B])
        k_st, k_work = s.sb("k_st", [B, 6]), s.sb("k_work", [B, 8])
        taps = s.sb("taps", [B, HEADS, TAPS * TAPS])
        taps_n = s.sb("taps_n", [B, 3, HEADS])
        pick = s.sb("pick", [B, B, P])
        ps_a, ps_b = s.psum("ps_a", [P, 2, 512]), s.psum("ps_b", [P, 2, 512])
        ps_c, ps_d = s.psum("ps_c", [P, 2, 512]), s.psum("ps_d", [P, 2, 512])
        loaded, ctx_in = s.sem("loaded"), [s.sem("ctx_in0"), s.sem("ctx_in1")]
        hidden, copied, measured = s.sem("hidden"), s.sem("copied"), s.sem("measured")
        var_ready, std_ready, own, pool_own = (s.sem(n) for n in ("var_ready", "std_ready", "own", "pool_own"))
        normed, scaled, gelued, turned = (s.sem(n) for n in ("normed", "scaled", "gelued", "turned"))
        rowT_ready, a1_summed, a1_ready, weighed, weights_kept = (
            s.sem(n) for n in ("rowT_ready", "a1_summed", "a1_ready", "weighed", "weights_kept"))
        relay = s.sem("relay")
        block = s.block()
        (POOL_SHIFTED, POOL_EXPED, POOL_NORMED, COLUMNS, COLUMNS_SPREAD, POOLED, POOLED_COPIED, POOLED_TURNED,
         POOLED_T_COPIED, KG_SUMMED, KG_VAR, KG_STD, KG_NORMED, KG_GELUED, KG_TURNED, KG_T_COPIED, TAPS_SUMMED,
         TAPS_SHIFTED, TAPS_EXPED, TAPS_NORMED, TAPS_SPREAD) = range(1, 22)
        b1, w2, b2 = w1[:, CC * A1:CC * A1 + 1], w1[:, CC * A1 + 1:CC * A1 + 2], w1[0:1, CC * A1 + 2:CC * A1 + 3]

        @block.sync
        def _(sp):
            for to, of in ((hist, a["hist"]), (w1, a["ctx_net"]), (kg1, a["kg1"]), (kg2, a["kg2"])):
                sp.dma_start(to[:, :], of).then_inc(loaded, 16)
            for to, of, n in ((gb, a["hist_gb"], C), (kg_gb, a["kg_gb"], D)):
                sp.dma_start(to[:, :, :], of.rearrange("(o a) n -> o a n", o=1).to_broadcast([P, 2, n]))\
                    .then_inc(loaded, 16)
            with sp.Fori(0, B // 2) as i:
                for p in range(2):
                    sp.wait_ge(hidden, 2 * (2 * i + p) + 2)
                    sp.dma_start(ctx[:, p, :, :].rearrange("p c n -> p (c n)"), ctxT[dyn(2 * i + p), :])\
                        .then_inc(ctx_in[p], 16)

        @block.tensor
        def _(pe):
            pe.sem_inc(hidden, 4)
            pe.sem_inc(turned, 2)
            pe.wait_ge(loaded, 96)
            with pe.Fori(0, B // 2) as i:
                for p in range(2):
                    pe.wait_ge(ctx_in[p], 16 * (i + 1))
                    for q in range(QC):
                        t = 2 * (2 * i + p) + q
                        pe.wait_ge(copied, t + 1)
                        pe.wait_ge(measured, t + 1)
                        for c in range(DC):
                            pe.matmul(ps_a[:, q, :], ctx[:, p, c, q * P:(q + 1) * P], hist[:, c * C:(c + 1) * C],
                                      start=(c == 0), stop=False)
                        pe.matmul(ps_a[:, q, :], ones[0:1, 0:P], hist[0:1, DC * C:], start=False, stop=True)\
                            .then_inc(hidden, 1)
            with pe.Fori(0, TILES // 2) as i:
                for p in range(2):
                    t = 2 * i + p
                    pe.wait_ge(gelued, t + 1)
                    for c in range(CC):
                        last = pe.transpose(ps_b[:, p, c * P:(c + 1) * P], row[:, p, c * P:(c + 1) * P], ident[:, :])
                    last.then_inc(turned, 1)
                    pe.wait_ge(rowT_ready, t + 1)
                    for c in range(CC):
                        last = pe.matmul(ps_c[:, p, 0:P], w1[:, c * A1:(c + 1) * A1], rowT[:, p, c, :],
                                         start=(c == 0), stop=(c == CC - 1))
                    last.then_inc(a1_summed, 1)
                    pe.wait_ge(a1_ready, t + 1)
                    pe.wait_ge(weights_kept, t + 1)
                    pe.matmul(ps_d[0:1, p, 0:P], w2, a1[:, p, :]).then_inc(weighed, 1)
            pe.wait_ge(relay, POOL_NORMED)
            for t in range(TILES):
                last = pe.matmul(ps_a[:, 0, t:t + 1], pool_w[0:1, t // QC, (t % QC) * P:(t % QC + 1) * P],
                                 ones[0:1, 0:1])
            last.then_inc(relay, 1)
            pe.wait_ge(relay, COLUMNS_SPREAD)
            for t in range(TILES):
                last = pe.matmul(ps_b[0:B, 0, :], w_cols[:, t, :], z[:, t, :], start=(t == 0), stop=(t == TILES - 1))
            last.then_inc(relay, 1)
            pe.wait_ge(relay, POOLED_COPIED)
            for c in range(CC):
                last = pe.transpose(ps_c[:, 0, c * B:(c + 1) * B], cc[:, c * P:(c + 1) * P], ident[0:B, 0:B])
            last.then_inc(relay, 1)
            pe.wait_ge(relay, POOLED_T_COPIED)
            for c in range(CC):
                pe.matmul(ps_d[0:B, 0, 0:D], ccT[:, c, :], kg1[:, c * D:(c + 1) * D], start=(c == 0), stop=False)
            pe.matmul(ps_d[0:B, 0, 0:D], ones[0:1, 0:B], kg1[0:1, CC * D:], start=False, stop=True).then_inc(relay, 1)
            pe.wait_ge(relay, KG_GELUED)
            for c in range(DC):
                last = pe.transpose(ps_c[:, 1, c * B:(c + 1) * B], k1[:, c * P:(c + 1) * P], ident[0:B, 0:B])
            last.then_inc(relay, 1)
            pe.wait_ge(relay, KG_T_COPIED)
            for c in range(DC):
                pe.matmul(ps_d[0:B, 1, 0:T9], k1T[:, c, :], kg2[:, c * T9:(c + 1) * T9], start=(c == 0), stop=False)
            pe.matmul(ps_d[0:B, 1, 0:T9], ones[0:1, 0:B], kg2[0:1, DC * T9:], start=False, stop=True)\
                .then_inc(relay, 1)
            pe.wait_ge(relay, TAPS_NORMED)
            pe.wait_ge(pool_own, 2)
            for b in range(B):
                bank = (ps_a[:, 1], ps_b[:, 1], ps_c[:, 1])[b // 3]
                last = pe.matmul(bank[:, (b % 3) * T9:(b % 3 + 1) * T9], pick[:, b, :],
                                 taps[:, :, :].rearrange("b h t -> b (h t)"), start=True, stop=True,
                                 skip_group_check=True)
            last.then_inc(relay, 1)

        @block.gpsimd
        def _(pool):
            pool.memset(w_cols[:, :, :], 0.0)
            pool.memset(pick[:, :, :], 1.0).then_inc(pool_own, 1)
            pool.wait_ge(pool_own, 1)
            pool.affine_select(out=pick[:, :, :], in_=pick[:, :, :], compare_op=ALU.is_equal, fill=0.0, base=0,
                               pattern=[[-1, B], [0, P]], channel_multiplier=1).then_inc(pool_own, 1)
            pool.wait_ge(loaded, 96)
            with pool.Fori(0, TILES // 2) as i:
                for p in range(2):
                    t = 2 * i + p
                    pool.wait_ge(scaled, t + 1)
                    pool.tensor_tensor(row[:, p, :], row[:, p, :], gb[:, 1, :], ALU.add).then_inc(normed, 1)

        @block.scalar
        def _(act):
            act.sem_inc(copied, 2)
            with act.Fori(0, TILES // 2) as i:
                for p in range(2):
                    t = 2 * i + p
                    act.wait_ge(hidden, t + 5)
                    act.wait_ge(measured, t + 3)
                    act.copy(z[:, t, :], ps_a[:, p, :]).then_inc(copied, 1)
            act.wait_ge(var_ready, 1)
            act.activation(work[:, 4, :], work[:, 3, :], ACT.Sqrt).then_inc(std_ready, 1)
            with act.Fori(0, TILES // 2) as i:
                for p in range(2):
                    t = 2 * i + p
                    act.wait_ge(normed, t + 1)
                    act.activation(row[:, p, :], row[:, p, :], ACT.Gelu).then_inc(gelued, 1)
                    act.wait_ge(gelued, t + 1)
                    act.copy(z[:, t, :], row[:, p, :])
                    act.wait_ge(a1_summed, t + 1)
                    act.activation(a1[:, p, :], ps_c[:, p, 0:P], ACT.Gelu, bias=b1).then_inc(a1_ready, 1)
            act.wait_ge(relay, POOL_SHIFTED)
            act.activation(pool_w[:, :, :], pool_w[:, :, :], ACT.Exp).then_inc(relay, 1)
            act.wait_ge(relay, KG_VAR)
            act.activation(k_work[:, 5:6], k_work[:, 4:5], ACT.Sqrt).then_inc(relay, 1)
            act.wait_ge(relay, KG_NORMED)
            act.activation(k1[:, :], k1[:, :], ACT.Gelu).then_inc(relay, 1)
            act.wait_ge(relay, TAPS_SHIFTED)
            act.activation(taps[:, :, :], taps[:, :, :], ACT.Exp).then_inc(relay, 1)

        @block.vector
        def _(v):
            steps = Steps(v, own)
            v.sem_inc(measured, 2)
            v.sem_inc(weights_kept, 2)
            v.wait_ge(loaded, 96)
            with v.Fori(0, TILES // 2) as i:
                for p in range(2):
                    t = 2 * i + p
                    v.wait_ge(hidden, t + 5)
                    v.bn_stats(st[:, t, :], ps_a[:, p, :]).then_inc(measured, 1)
            v.wait_ge(measured, TILES + 2)
            me, mo, se, so = st[:, :, 1], st[:, :, 4], st[:, :, 2], st[:, :, 5]
            v.tensor_tensor(mean[:, :], me, mo, ALU.add)
            v.tensor_tensor(work[:, 0, :], me, mo, ALU.subtract)
            steps.done(v.tensor_tensor(work[:, 1, :], se, so, ALU.add))
            v.tensor_scalar(mean[:, :], mean[:, :], 0.5, None, ALU.mult)
            v.tensor_scalar(work[:, 1, :], work[:, 1, :], 1.0 / C, LN_EPS, ALU.mult, ALU.add)
            steps.done(v.scalar_tensor_tensor(work[:, 2, :], work[:, 0, :], 0.25, work[:, 0, :],
                                              ALU.mult, ALU.mult))
            v.tensor_tensor(work[:, 3, :], work[:, 1, :], work[:, 2, :], ALU.add).then_inc(var_ready, 1)
            v.wait_ge(std_ready, 1)
            steps.done(v.reciprocal(rstd[:, :], work[:, 4, :]))
            v.wait_ge(copied, TILES + 2)
            start = steps.n
            with v.Fori(0, TILES // 2) as i:
                for p in range(2):
                    t = 2 * i + p
                    v.wait_ge(turned, t + 1)
                    steps.n = start + t
                    steps.done(v.tensor_scalar(row[:, p, :], z[:, t, :], mean[:, bass.ds(t, 1)],
                                               rstd[:, bass.ds(t, 1)], ALU.subtract, ALU.mult))
                    v.tensor_tensor(row[:, p, :], row[:, p, :], gb[:, 0, :], ALU.mult).then_inc(scaled, 1)
                    v.wait_ge(turned, t + 3)
                    v.tensor_copy(rowT[:, p, :, :], ps_b[:, p, :].rearrange("p (c n) -> p c n", c=CC))\
                        .then_inc(rowT_ready, 1)
                    v.wait_ge(weighed, t + 1)
                    v.tensor_scalar(pool_w[0:1, bass.ds(i, 1), p * P:(p + 1) * P],
                                    ps_d[0:1, p:p + 1, 0:P], b2, None, ALU.add).then_inc(weights_kept, 1)
            steps.n = start + TILES
            v.wait_ge(weights_kept, TILES + 2)
            steps.done(v.tensor_reduce(pool_n[:, 0, :], pool_w[:, :, :], X, ALU.max, negate=True))
            v.tensor_tensor(pool_w[:, :, :], pool_w[:, :, :],
                            pool_n[:, 0, :].unsqueeze(2).to_broadcast([1, B, SEQ]), ALU.add).then_inc(relay, 1)
            v.wait_ge(relay, POOL_EXPED)
            steps.done(v.reduce_sum(pool_n[:, 1, :], pool_w[:, :, :], X))
            steps.done(v.reciprocal(pool_n[:, 2, :], pool_n[:, 1, :]))
            v.tensor_tensor(pool_w[:, :, :], pool_w[:, :, :],
                            pool_n[:, 2, :].unsqueeze(2).to_broadcast([1, B, SEQ]), ALU.mult).then_inc(relay, 1)
            v.wait_ge(relay, COLUMNS)
            v.wait_ge(pool_own, 1)
            for b in range(B):
                last = v.tensor_copy(w_cols[:, b * QC:(b + 1) * QC, b:b + 1],
                                     ps_a[:, 0, b * QC:(b + 1) * QC].unsqueeze(2))
            last.then_inc(relay, 1)
            v.wait_ge(relay, POOLED)
            v.tensor_copy(cc[:, :], ps_b[0:B, 0, :]).then_inc(relay, 1)
            v.wait_ge(relay, POOLED_TURNED)
            v.tensor_copy(ccT[:, :, :], ps_c[:, 0, 0:CC * B].rearrange("p (c b) -> p c b", c=CC)).then_inc(relay, 1)
            v.wait_ge(relay, KG_SUMMED)
            steps.done(v.bn_stats(k_st[:, :], ps_d[0:B, 0, 0:D]))
            v.tensor_tensor(k_work[:, 0:1], k_st[:, 1:2], k_st[:, 4:5], ALU.add)
            v.tensor_tensor(k_work[:, 1:2], k_st[:, 1:2], k_st[:, 4:5], ALU.subtract)
            steps.done(v.tensor_tensor(k_work[:, 2:3], k_st[:, 2:3], k_st[:, 5:6], ALU.add))
            v.tensor_scalar(k_work[:, 0:1], k_work[:, 0:1], 0.5, None, ALU.mult)
            v.tensor_scalar(k_work[:, 2:3], k_work[:, 2:3], 1.0 / D, LN_EPS, ALU.mult, ALU.add)
            steps.done(v.scalar_tensor_tensor(k_work[:, 3:4], k_work[:, 1:2], 0.25, k_work[:, 1:2],
                                              ALU.mult, ALU.mult))
            v.tensor_tensor(k_work[:, 4:5], k_work[:, 2:3], k_work[:, 3:4], ALU.add).then_inc(relay, 1)
            v.wait_ge(relay, KG_STD)
            steps.done(v.reciprocal(k_work[:, 6:7], k_work[:, 5:6]))
            steps.done(v.tensor_scalar(k1[:, :], ps_d[0:B, 0, 0:D], k_work[:, 0:1], k_work[:, 6:7],
                                       ALU.subtract, ALU.mult))
            steps.done(v.tensor_tensor(k1[:, :], k1[:, :], kg_gb[0:B, 0, :], ALU.mult))
            v.tensor_tensor(k1[:, :], k1[:, :], kg_gb[0:B, 1, :], ALU.add).then_inc(relay, 1)
            v.wait_ge(relay, KG_TURNED)
            v.tensor_copy(k1T[:, :, :], ps_c[:, 1, 0:DC * B].rearrange("p (c b) -> p c b", c=DC)).then_inc(relay, 1)
            v.wait_ge(relay, TAPS_SUMMED)
            kp = ps_d[0:B, 1, 0:T9].rearrange("b (h t) -> b h t", h=HEADS)
            over_taps = lambda n: taps_n[:, n, :].unsqueeze(2).to_broadcast([B, HEADS, TAPS * TAPS])
            steps.done(v.tensor_reduce(taps_n[:, 0, :], kp, X, ALU.max, negate=True))
            v.tensor_tensor(taps[:, :, :], kp, over_taps(0), ALU.add).then_inc(relay, 1)
            v.wait_ge(relay, TAPS_EXPED)
            steps.done(v.reduce_sum(taps_n[:, 1, :], taps[:, :, :], X))
            steps.done(v.reciprocal(taps_n[:, 2, :], taps_n[:, 1, :]))
            v.tensor_tensor(taps[:, :, :], taps[:, :, :], over_taps(2), ALU.mult).then_inc(relay, 1)
            v.wait_ge(relay, TAPS_SPREAD)
            for n, ps in enumerate((ps_a, ps_b, ps_c)):
                m = min(3, B - 3 * n)
                v.tensor_copy(kernels[:, 3 * n * T9:(3 * n + m) * T9], ps[:, 1, 0:m * T9])



HALF = HEADS // 2
PIECES = 3
PRODUCTS = ((0, 0), (1, 0), (2, 0), (0, 1), (1, 1), (0, 2))
STACK = len(PRODUCTS) * HD
RUNS = tuple((HD * sum(range(n + 1, PIECES + 1)), n) for n in range(PIECES, 0, -1))
SLOTS = 4
LOOPS = 2 * B // SLOTS
VW = LANE


def split_heads_stage(core, name, mode, xnT, ctxT, w_dram, dst, ident, ident16, ones, piece_rows,
                      mask=None):
    WB = 3 * DC * D
    masking = mode == MASKED
    loads = 2 if masking else 1
    piece_dmas, stack_dmas = 2, 2 * len(RUNS)

    def at(i, r):
        return i + r // SLOTS, r % SLOTS

    with Stage(core, name) as s:
        w = s.sb("w", [P, WB + 2 * DC + D])
        wq, wk, wv = (w[:, n * DC * D:(n + 1) * DC * D].rearrange("p (c n) -> p c n", c=DC) for n in range(3))
        bv = w[0:1, WB + 2 * DC:]
        ctx = s.sb("ctx", [P, DC, SEQ])
        qk, rest = s.sb("qk", [P, 2, SEQ]), s.sb("rest", [P, 2, SEQ])
        pieces = s.sb("pieces", [P, PIECES, 2, SEQ], BF16)
        stackQ, stackK = (s.sb(n, [P, SLOTS, HALF, SEQ], BF16) for n in ("stackQ", "stackK"))
        vv = s.sb("v", [P, SLOTS, QC, HALF, VW])
        probsT = s.sb("probsT", [P, 4, QC * SEQ])
        negmax, max_rest = s.sb("negmax", [P, HALF * QC]), s.sb("max_rest", [P, HALF * QC])
        max_pieces = s.sb("max_pieces", [P, P], BF16)
        max_rows = s.sb("max_rows", [PIECES * HALF * QC, P], BF16)
        mixedT = s.sb("mixedT", [P, QC * SEQ])
        inv, mixed_sb = s.sb("inv", [P, QC, HALF]), s.sb("mixed_sb", [P, QC, HALF, HD])
        warm = s.sb("warm", [P, 1])
        max_piece = [max_pieces[:, n * HALF * QC:(n + 1) * HALF * QC] for n in range(PIECES)]
        ps_m, ps_e = s.psum("ps_m", [P, 2, 512]), s.psum("ps_e", [P, 2, 512])
        ps_qk, ps_v, ps_o = (s.psum(n, [P, 512]) for n in ("ps_qk", "ps_v", "ps_o"))
        ps_r = s.psum("ps_r", [P, 1024], BF16)
        sp_passed, split_steps = s.sem("sp_passed"), s.sem("split_steps")
        w_loaded, ctx_loaded, constants, written = (s.sem(n) for n in ("w_loaded", "ctx_loaded", "constants", "written"))
        projected, v_projected, qk_taken, v_placed = (s.sem(n) for n in
                                                      ("projected", "v_projected", "qk_taken", "v_placed"))
        pieces_ready, scored, maxed, max_split, max_turned, rows_ready = (
            s.sem(n) for n in ("pieces_ready", "scored", "maxed", "max_split", "max_turned", "rows_ready"))
        stacked, max_placed = ([s.sem(f"{n}{r}") for r in range(SLOTS)] for n in ("stacked", "max_placed"))
        scoredT, exped, mixed, mixedT_ready, turned_back, taken, own = (
            s.sem(n) for n in ("scoredT", "exped", "mixed", "mixedT_ready", "turned_back", "taken", "own"))
        if masking:
            mask_in = s.sb("mask_in", [P, 2, QC * SEQ], I32)
            mask_add = s.sb("mask_add", [P, 2, QC * SEQ], BF16)
            mask_loaded, mask_ready, maskT_ready = s.sem("mask_loaded"), s.sem("mask_ready"), s.sem("maskT_ready")
        block = s.block()

        @block.sync
        def _(sp):
            sp.dma_start(w[:, :], w_dram).then_inc(w_loaded, 16)
            sp.dma_start(ctx[:, :, :].rearrange("p c n -> p (c n)"), ctxT[0:P, :]).then_inc(ctx_loaded, 16)
            if masking:
                sp.dma_start(mask_in[:, :, :].rearrange("p a n -> p (a n)"), mask[0:P, :]).then_inc(mask_loaded, 16)

            def passed():
                sp.sem_inc(sp_passed, 1)

            def put_pieces(i, r):
                u = SLOTS * i + r
                if not (isinstance(i, int) and u < 2):
                    sp.wait_ge(stacked[(r - 2) % SLOTS], 16 * stack_dmas * (i + (r - 2) // SLOTS + 1))
                    passed()
                sp.wait_ge(pieces_ready, u + 1)
                for side in range(2):
                    sp.dma_start(piece_rows[r % 2, side].rearrange("a d j n -> (d j) a n"),
                                 pieces[:, :, side, :]).then_inc(written, 16)

            def stack(i, r):
                u = SLOTS * i + r
                sp.wait_ge(written, 16 * piece_dmas * (u + 1))
                passed()
                sp.wait_ge(mixed, u + 1)
                for row, count in RUNS:
                    sp.dma_start(stackQ[row:row + count * HD, r, :, :].rearrange("r j n -> r (j n)"),
                                 piece_rows[r % 2, 0, 0:count].rearrange("a d j n -> (a d) (j n)"))\
                        .then_inc(stacked[r], 16)
                    same = piece_rows[r % 2, 1, PIECES - count].rearrange("d j n -> d (j n)").unsqueeze(0)
                    sp.dma_start(stackK[row:row + count * HD, r, :, :].rearrange("r j n -> r (j n)"),
                                 same.to_broadcast([count, HD, HALF * SEQ])).then_inc(stacked[r], 16)

            def context(b):
                sp.wait_ge(v_projected, 2 * b)
                passed()
                sp.dma_start(ctx[:, :, :].rearrange("p c n -> p (c n)"), ctxT[dyn(b), :]).then_inc(ctx_loaded, 16)

            def sequence(i, r, more):
                b = 2 * i + r // 2
                stack(*at(i, r - 1))
                put_pieces(i, r)
                stack(i, r)
                if masking:
                    sp.wait_ge(maskT_ready, b)
                    passed()
                    sp.dma_start(mask_in[:, :, :].rearrange("p a n -> p (a n)"), mask[dyn(b), :])\
                        .then_inc(mask_loaded, 16)
                if more:
                    context(b + 1)
                put_pieces(i, r + 1)

            put_pieces(0, 0)
            stack(0, 0)
            context(1)
            put_pieces(0, 1)
            sequence(0, 2, True)
            with sp.Fori(1, LOOPS - 1) as i:
                sequence(i, 0, True)
                sequence(i, 2, True)
            sequence(LOOPS - 1, 0, True)
            sequence(LOOPS - 1, 2, False)
            stack(LOOPS - 1, SLOTS - 1)

        @block.gpsimd
        def _(pool):
            pool.memset(vv[:, :, :, :, HD + 1:VW], 0.0)
            pool.memset(vv[:, :, :, :, HD:HD + 1], 1.0)
            pool.memset(max_pieces[:, PIECES * HALF * QC:], 0.0).then_inc(constants, 1)

        @block.tensor
        def _(pe):
            pe.sem_inc(mixed, SLOTS)
            pe.wait_ge(w_loaded, 16)

            def project_query(i, r):
                b, p = 2 * i + r // 2, r % 2
                pe.wait_ge(ctx_loaded, 16 * (b + 1))
                pe.wait_ge(qk_taken, SLOTS * i + r + 1)
                for c in range(DC):
                    pe.matmul(ps_qk[:, 0:SEQ], wq[:, c, p * P:(p + 1) * P], xnT[:, c, dyn(b, SEQ)],
                              start=(c == 0), stop=(c == DC - 1))

            def project_key_value(i, r):
                p = r % 2
                for c in range(DC):
                    last = pe.matmul(ps_qk[:, SEQ:2 * SEQ], wk[:, c, p * P:(p + 1) * P], ctx[:, c, :],
                                     start=(c == 0), stop=(c == DC - 1))
                last.then_inc(projected, 1)
                pe.wait_ge(v_placed, SLOTS * i + r + 1)
                for tc in range(QC):
                    out = ps_v[:, tc * P:(tc + 1) * P]
                    for c in range(DC):
                        pe.matmul(out, ctx[:, c, tc * P:(tc + 1) * P], wv[:, c, p * P:(p + 1) * P],
                                  start=(c == 0), stop=False)
                    last = pe.matmul(out, ones[0:1, 0:P], bv[:, p * P:(p + 1) * P], start=False, stop=True)
                last.then_inc(v_projected, 1)

            def score(i, r, h):
                out = ps_m[:, h % 2, :]
                if h == 0:
                    pe.wait_ge(stacked[r], 16 * stack_dmas * (i + 1))
                    if masking:
                        pe.wait_ge(mask_ready, 2 * i + r // 2 + 1)
                pe.wait_ge(maxed, HALF * (SLOTS * i + r) + h + 1)
                if masking:
                    pe.matmul(out, ident16[:, :], mask_add[:, 0, :], start=True, stop=False, skip_group_check=True)
                for qc in range(QC):
                    last = pe.matmul(out[:, qc * SEQ:(qc + 1) * SEQ], stackQ[0:STACK, r, h, qc * P:(qc + 1) * P],
                                     stackK[0:STACK, r, h, :], start=not masking,
                                     stop=(qc == QC - 1 or not masking), skip_group_check=True)
                last.then_inc(scored, 1)

            def turn_max(i, r):
                pe.wait_ge(max_split, SLOTS * i + r + 1)
                pe.transpose(ps_r[:, 0:P], max_pieces[:, :], ident16[:, :]).then_inc(max_turned, 1)

            def scoreT(i, r, h):
                out = ps_e[:, h % 2, :]
                pe.wait_ge(exped, HALF * (SLOTS * i + r) + h + 1)
                rows = STACK + PIECES
                if masking:
                    pe.matmul(out, ident16[:, :], mask_add[:, 1, :], start=True, stop=False, skip_group_check=True)
                for kc in range(QC):
                    last = pe.matmul(out[:, kc * SEQ:(kc + 1) * SEQ], stackK[0:rows, r, h, kc * P:(kc + 1) * P],
                                     stackQ[0:rows, r, h, :], start=not masking,
                                     stop=(kc == QC - 1 or not masking), skip_group_check=True)
                last.then_inc(scoredT, 1)

            def mix(i, r, h):
                pe.wait_ge(exped, HALF * (SLOTS * i + r) + h + 3)
                out = ps_o[LANE * (h % GH):LANE * (h % GH) + VW, h // GH * SEQ:(h // GH + 1) * SEQ]
                for kc in range(QC):
                    last = pe.matmul(out, vv[:, r, kc, h, :], probsT[:, h % 4, kc * SEQ:(kc + 1) * SEQ],
                                     start=(kc == 0), stop=(kc == QC - 1), skip_group_check=True)
                if h == HALF - 1:
                    last.then_inc(mixed, 1)

            def turn_back(i, r):
                pe.wait_ge(mixedT_ready, SLOTS * i + r + 1)
                for n in range(2 * QC):
                    last = pe.transpose(ps_o[:, n * P:(n + 1) * P], mixedT[:, n * P:(n + 1) * P], ident[:, :])
                last.then_inc(turned_back, 1)

            def turn(i, r, projects, maxes):
                if maxes:
                    for h in range(2):
                        score(*at(i, r + 1), h)
                pe.wait_ge(max_placed[r], 16 * PIECES * (i + 1))
                pe.wait_ge(taken, SLOTS * i + r + 1)
                if masking:
                    pe.wait_ge(maskT_ready, 2 * i + r // 2 + 1)
                for h in range(HALF + 2):
                    if h < HALF:
                        scoreT(i, r, h)
                    if h >= 2:
                        mix(i, r, h - 2)
                    if maxes and h + 2 < HALF:
                        score(*at(i, r + 1), h + 2)
                if projects:
                    project_query(*at(i, r + 4))
                if maxes:
                    turn_max(*at(i, r + 1))
                turn_back(i, r)
                if projects:
                    project_key_value(*at(i, r + 4))

            for r in range(3):
                project_query(0, r)
                project_key_value(0, r)
            pe.wait_ge(constants, 2)
            for h in range(HALF):
                score(0, 0, h)
            project_query(0, 3)
            turn_max(0, 0)
            project_key_value(0, 3)
            with pe.Fori(0, LOOPS - 1) as i:
                for r in range(SLOTS):
                    turn(i, r, True, True)
            for r in range(SLOTS):
                turn(LOOPS - 1, r, False, r + 1 < SLOTS)

        @block.scalar
        def _(act):
            act.sem_inc(exped, 2)
            act.sem_inc(v_placed, 1)
            act.activation(warm[:, :], ones[:, 0:1], ACT.Exp)
            act.wait_ge(constants, 2)

            def place_values(i, r):
                act.wait_ge(v_projected, SLOTS * i + r + 1)
                act.wait_ge(mixed, SLOTS * i + r + 1)
                for tc in range(QC):
                    last = act.copy(vv[:, r, tc, :, 0:HD],
                                    ps_v[:, tc * P:(tc + 1) * P].rearrange("p (j d) -> p j d", d=HD))
                last.then_inc(v_placed, 1)

            def place_max(i, r):
                u = SLOTS * i + r
                act.wait_ge(max_turned, u + 1)
                act.copy(max_rows[:, :], ps_r[0:PIECES * HALF * QC, 0:P]).then_inc(rows_ready, 1)
                act.wait_ge(rows_ready, u + 1)
                for n in range(PIECES):
                    act.dma_start(stackQ[STACK + n:STACK + n + 1, r, :, :].rearrange("a j (q n) -> a (j q) n", q=QC),
                                  max_rows[n * HALF * QC:(n + 1) * HALF * QC, :])\
                        .then_inc(max_placed[r], 16)

            def turn(i, r, projects, maxes):
                u = SLOTS * i + r
                for h in range(HALF):
                    act.wait_ge(scoredT, HALF * u + h + 1)
                    act.activation(probsT[:, h % 4, :], ps_e[:, h % 2, :], ACT.Exp).then_inc(exped, 1)
                act.wait_ge(mixed, u + 1 + SLOTS)
                act.copy(mixedT[:, :], ps_o[:, :]).then_inc(mixedT_ready, 1)
                if maxes:
                    place_max(*at(i, r + 1))
                if projects:
                    place_values(*at(i, r + 4))

            for r in range(3):
                place_values(0, r)
            place_max(0, 0)
            place_values(0, 3)
            with act.Fori(0, LOOPS - 1) as i:
                for r in range(SLOTS):
                    turn(i, r, True, True)
            for r in range(SLOTS):
                turn(LOOPS - 1, r, False, r + 1 < SLOTS)

        @block.vector
        def _(v):
            steps = Steps(v, own)
            v.memset(stackK[STACK:STACK + PIECES, :, :, :], 1.0).then_inc(constants, 1)
            v.sem_inc(maxed, 2)
            v.sem_inc(qk_taken, 1)
            v.sem_inc(taken, 1)
            v.wait_ge(w_loaded, 16)

            def split(i, r, part):
                u, p = SLOTS * i + r, r % 2
                flat = lambda t: t.rearrange("p a n -> p (a n)")
                if part == 0:
                    v.wait_ge(projected, u + 1)
                    v.tensor_scalar(qk[:, 0, :], ps_qk[:, 0:SEQ], w[:, WB + p:WB + p + 1], HD ** -0.5,
                                    ALU.add, ALU.mult)
                    v.tensor_scalar(qk[:, 1, :], ps_qk[:, SEQ:], w[:, WB + DC + p:WB + DC + p + 1], None,
                                    ALU.add).then_inc(qk_taken, 1)
                elif part == 1:
                    v.wait_ge(qk_taken, u + 2)
                    if not (isinstance(i, int) and u == 0):
                        v.wait_ge(written, 16 * piece_dmas * u)
                    v.tensor_copy(flat(pieces[:, 0, :, :]), flat(qk[:, :, :])).then_inc(split_steps, 1)
                elif part == 2:
                    v.wait_ge(split_steps, 3 * u + 1)
                    v.tensor_tensor(flat(rest[:, :, :]), flat(qk[:, :, :]), flat(pieces[:, 0, :, :]), ALU.subtract)\
                        .then_inc(split_steps, 1)
                elif part == 3:
                    v.wait_ge(split_steps, 3 * u + 2)
                    v.tensor_copy(flat(pieces[:, 1, :, :]), flat(rest[:, :, :])).then_inc(split_steps, 1)
                elif part == 4:
                    v.wait_ge(split_steps, 3 * u + 3)
                    v.tensor_tensor(flat(pieces[:, 2, :, :]), flat(rest[:, :, :]), flat(pieces[:, 1, :, :]),
                                    ALU.subtract).then_inc(pieces_ready, 1)

            def make_mask(which, ready):
                v.tensor_scalar(mask_add[:, which, :], mask_in[:, which, :], 0.0, NEG_BIG, ALU.is_equal, ALU.mult)\
                    .then_inc(ready, 1)

            def row_max(i, r, h):
                v.wait_ge(scored, HALF * (SLOTS * i + r) + h + 1)
                v.tensor_reduce(negmax[:, QC * h:QC * (h + 1)],
                                ps_m[:, h % 2, :].rearrange("p (k n) -> p k n", k=QC), X,
                                ALU.max, negate=True).then_inc(maxed, 1)

            def split_max(i, r):
                v.wait_ge(maxed, HALF * (SLOTS * i + r + 1) + 2)
                steps.done(v.tensor_copy(max_piece[0], negmax[:, :]))
                steps.done(v.tensor_tensor(max_rest[:, :], negmax[:, :], max_piece[0], ALU.subtract))
                steps.done(v.tensor_copy(max_piece[1], max_rest[:, :]))
                v.tensor_tensor(max_piece[2], max_rest[:, :], max_piece[1], ALU.subtract).then_inc(max_split, 1)

            def finish(i, r):
                u, p, b = SLOTS * i + r, r % 2, 2 * i + r // 2
                v.wait_ge(turned_back, u + 1)
                for n in range(2):
                    out = ps_o[:, n * SEQ:(n + 1) * SEQ].rearrange("p (q j d) -> p q j d", q=QC, j=GH)
                    last = v.reciprocal(inv[:, :, n * GH:(n + 1) * GH], out[:, :, :, HD])
                steps.done(last)
                for n in range(2):
                    out = ps_o[:, n * SEQ:(n + 1) * SEQ].rearrange("p (q j d) -> p q j d", q=QC, j=GH)
                    last = v.tensor_tensor(mixed_sb[:, :, n * GH:(n + 1) * GH, :], out[:, :, :, 0:HD],
                                           inv[:, :, n * GH:(n + 1) * GH].unsqueeze(3).to_broadcast([P, QC, GH, HD]),
                                           ALU.mult)
                last.then_inc(taken, 1)
                v.wait_ge(taken, u + 2)
                to = dst[:, dyn(b, QC), p * P:(p + 1) * P]
                got = mixed_sb[:, :, :, :].rearrange("p q j d -> p q (j d)")
                if masking:
                    v.tensor_tensor(to, to, got, ALU.add)
                else:
                    v.tensor_copy(to, got)

            def turn(i, r, projects, maxes):
                more_masks = masking and not (isinstance(i, int) and r >= 2)
                for h in range(HALF):
                    if maxes:
                        row_max(*at(i, r + 1), h)
                    if projects and h > 0:
                        split(*at(i, r + 3), h - 1)
                if maxes:
                    split_max(*at(i, r + 1))
                if more_masks and r % 2 == 0:
                    v.wait_ge(mask_loaded, 16 * (2 * i + r // 2 + 2))
                    make_mask(0, mask_ready)
                finish(i, r)
                if more_masks and r % 2 == 1:
                    make_mask(1, maskT_ready)

            if masking:
                v.wait_ge(mask_loaded, 16)
                make_mask(0, mask_ready)
                make_mask(1, maskT_ready)
            for r in range(3):
                for part in range(5):
                    split(0, r, part)
            for h in range(HALF):
                row_max(0, 0, h)
            split_max(0, 0)
            first, per_loop = steps.n, SLOTS * (3 + 1)
            with v.Fori(0, LOOPS - 1) as i:
                steps.n = first + per_loop * i
                for r in range(SLOTS):
                    turn(i, r, True, True)
            steps.n = first + per_loop * (LOOPS - 1)
            for r in range(SLOTS):
                turn(LOOPS - 1, r, r + 3 < SLOTS, r + 1 < SLOTS)




def build(nc, ins, outs, stages=99):
    i = ins
    with ExitStack() as whole:
        core = Core(nc, whole)
        x = core.keep("x", [P, TILES, D])
        xn = core.keep("xn", [P, TILES, D])
        xnT = core.keep("xnT", [P, DC, TILES * P])
        ident = core.keep("ident", [P, P])
        ones = core.keep("ones", [P, P])
        ident16 = core.keep("ident16", [P, P], BF16)
        logits = core.keep("logits", [P, TILES, 64])
        tb = Tables(core, MOST_TILES)
        xn_dram = nc.dram_tensor("xn_rows", (TILES * P, D), F32).ap()
        y_dram = nc.dram_tensor("y_rows", (MOST_TILES * P, D), F32).ap()
        piece_rows = nc.dram_tensor("piece_rows", (2, 2, PIECES, HD, HALF, SEQ), BF16).ap()
        x_rows = i["x"].rearrange("(t p) d -> p t d", p=P)

        with Stage(core, "load") as s:
            x_loaded, zeroed = s.sem("x_loaded"), s.sem("zeroed")
            block = s.block()

            @block.sync
            def _(sp):
                sp.dma_start(x[:, :, :], x_rows).then_inc(x_loaded, 16)
                sp.wait_ge(x_loaded, 16)

            @block.gpsimd
            def _(pool):
                pool.memset(ones[:, :], 1.0)
                pool.memset(tb.zeros[:, :], 0.0)
                pool.iota(tb.row_iota[:, :], [[1, P]], base=0, channel_multiplier=0,
                          allow_small_or_imprecise_dtypes=True)
                pool.iota(tb.column[:, :], [[0, 1]], base=0, channel_multiplier=1,
                          allow_small_or_imprecise_dtypes=True)
                for k in (1, 2):
                    pool.iota(tb.token_id[k][:, :].rearrange("p (t k) -> p t k", k=k), [[P, TILES], [0, k]],
                              base=0, channel_multiplier=1, allow_small_or_imprecise_dtypes=True)
                pool.memset(tb.before[:, :], 1.0).then_inc(zeroed, 1)
                pool.memset(ident16[:, :], 0.0)
                pool.memset(ident[:, :], 0.0).then_inc(zeroed, 1)
                pool.wait_ge(zeroed, 2)
                pool.affine_select(out=tb.before[:, :], in_=tb.before[:, :], compare_op=ALU.is_gt, fill=0.0,
                                   base=0, pattern=[[1, P]], channel_multiplier=-1)
                for eye in (ident, ident16):
                    pool.affine_select(out=eye[:, :], in_=eye[:, :], compare_op=ALU.not_equal, fill=1.0,
                                       base=0, pattern=[[-1, P]], channel_multiplier=1)

        norm_stage(core, "norm0", x, xn, xnT, ident)
        single_head_stage(core, "attn0", xn, xnT, i["ctxT"], i["w0"], ident, ones)
        post_norm_stage(core, "post0", x, xn, i["gb0"])
        norm_stage(core, "norm0f", x, xn, xnT, ident, i["router0"], logits)
        NT = TILES * 2 + 8
        route_stage(core, "route0", logits[:, :, 0:8], 8, 2, NT, tb, ones, xn, xn_dram)
        experts_stage(core, "experts0", NT, P, [128, 128, 96], i["experts0"], tb, xn_dram, y_dram, ident, ones)
        shared_stage(core, "shared0", xnT, logits[:, :, 8], i["shared0"], x)
        combine_stage(core, "combine0", 2, tb, y_dram[0:NT * P, :], x)
        kernels = core.keep("kernels", [P, B * HEADS * TAPS * TAPS])
        context_kernels_stage(core, "kernels1", i["ctxT"], i, ident, ones, tb, kernels)
        norm_stage(core, "norm1", x, xn, xnT, ident)
        heads_stage(core, "heads1", CONV, xnT, None, i["heads1"], xn, ident, mask=i["mask1"],
                    ident16=ident16, kernels=kernels, ones=ones)
        project_stage(core, "proj1", x, xn, i["proj1"], ident, ones)
        norm_stage(core, "norm1f", x, xn, xnT, ident, i["router1"], logits)
        NT = TILES + 8
        route_stage(core, "route1", logits[:, :, 0:8], 8, 1, NT, tb, ones, xn, xn_dram, bias=i["router_bias1"])
        experts_stage(core, "experts1", NT, P, [P] * 8, i["experts1"], tb, xn_dram, y_dram, ident, ones,
                      biased=True)
        combine_stage(core, "combine1", 1, tb, y_dram[0:NT * P, :], x)
        norm_stage(core, "norm2", x, xn, xnT, ident)
        split_heads_stage(core, "heads2", MASKED, xnT, i["ctxT"], i["heads2"], x, ident, ident16, ones, piece_rows, mask=i["mask2"])
        norm_stage(core, "norm2f", x, xn, xnT, ident, i["router2"], logits)
        NT = TILES * 2 + 32
        for n in range(2):
            route_stage(core, f"route2_{n}", logits[:, :, 32 * n:32 * n + 32], 32, 2, NT, tb, ones, xn,
                        None if n else xn_dram, factor=0.5)
            experts_stage(core, f"experts2_{n}", NT, P, [P], i[f"experts2_{n}"], tb, xn_dram, y_dram, ident, ones)
            combine_stage(core, f"combine2_{n}", 2, tb, y_dram[0:NT * P, :], x)
        norm_stage(core, "norm3", x, xn, xnT, ident)
        split_heads_stage(core, "heads3", PLAIN, xnT, i["ctxT"], i["heads3"], xn, ident, ident16, ones, piece_rows)
        project_stage(core, "proj3", x, xn, i["proj3"], ident, ones)
        norm_stage(core, "norm3f", x, xn, xnT, ident, i["router3"], logits)
        CAP = -(-5 * TILES * P // (4 * 32))
        route_stage(core, "route3", logits[:, :, 0:32], 32, 1, 32, tb, ones, xn, xn_dram, capacity=CAP)
        experts_stage(core, "experts3", 32, CAP, [P, P], i["experts3"], tb, xn_dram, y_dram, ident, ones)
        combine_stage(core, "combine3", 1, tb, y_dram[0:32 * CAP, :], x, xn)
        with Stage(core, "store") as s:
            stored = s.sem("stored")
            block = s.block()

            @block.sync
            def _(sp):
                sp.dma_start(outs.rearrange("(t p) d -> p t d", p=P), x[:, :, :]).then_inc(stored, 16)
                sp.wait_ge(stored, 16)


def _columns(w):
    K, n = w.shape
    return w.reshape(K // P, P, n).transpose(1, 0, 2).reshape(P, -1)


def _in_partition_0(row):
    import numpy as np

    out = np.zeros((P, row.size), row.dtype)
    out[0] = row.reshape(-1)
    return out


def _layouts(a):
    import numpy as np

    cat = lambda *parts: np.ascontiguousarray(np.concatenate(parts, axis=1))
    o = {"x": a["x"].reshape(B * SEQ, D)}
    o["ctxT"] = a["ctx_1024"].transpose(0, 2, 1).reshape(B, DC, P, SEQ).transpose(0, 2, 1, 3).reshape(B * P, DC * SEQ)
    col = lambda b: b.reshape(DC, P).T
    g = lambda n: a[n]
    o["w0"] = cat(_columns(g("L0_xattn_Wq")), _columns(g("L0_xattn_Wk")), _columns(g("L0_xattn_Wv")),
                  col(g("L0_xattn_bq")), col(g("L0_xattn_bk")), _in_partition_0(g("L0_xattn_bv")))
    o["gb0"] = np.stack([g("L0_xattn_gamma"), g("L0_xattn_beta")])

    def expert_rows(gate, up, down):
        E, _, F = gate.shape
        NF = -(-F // P)
        parts = [m.reshape(E, DC, P, F).transpose(0, 2, 1, 3).reshape(E, P, DC * F) for m in (gate, up) if m is not None]
        full = np.zeros((E, NF * P, D), down.dtype)
        full[:, :F] = down
        parts.append(full.reshape(E, NF, P, D).transpose(0, 2, 1, 3).reshape(E, P, NF * D))
        return np.concatenate(parts, axis=2).reshape(E * P, -1)

    swap = lambda m: np.swapaxes(m, -1, -2)
    I = g("L0_ffn_experts_down").shape[2]
    gu = swap(g("L0_ffn_experts_gate_up"))
    o["experts0"] = expert_rows(gu[:, :, :I], gu[:, :, I:], swap(g("L0_ffn_experts_down")))
    o["shared0"] = expert_rows(g("L0_ffn_shared_gate_w").T[None], g("L0_ffn_shared_up_w").T[None],
                               g("L0_ffn_shared_down_w").T[None])
    o["router0"] = _columns(cat(g("L0_ffn_gate_w").T, g("L0_ffn_shared_expert_gate_w").T))
    w1 = expert_rows(g("L1_ffn_W1"), None, g("L1_ffn_W2")).reshape(8, P, -1)
    b1 = g("L1_ffn_b1").reshape(8, -1, P).transpose(0, 2, 1)
    b2 = np.zeros((8, P, D), w1.dtype)
    b2[:, 0] = g("L1_ffn_b2")
    o["experts1"] = np.concatenate([w1, b1, b2], axis=2).reshape(8 * P, -1)
    o["router1"], o["router_bias1"] = _columns(g("L1_ffn_Wg")), g("L1_ffn_bg").reshape(1, -1)
    o["router2"] = _columns(cat(g("L2_ffn_router_w0"), g("L2_ffn_router_w1")))
    for n in "01":
        o["experts2_" + n] = expert_rows(g("L2_ffn_wg" + n), g("L2_ffn_wu" + n), g("L2_ffn_wd" + n))
    o["router3"] = _columns(g("L3_ffn_w_router"))
    o["experts3"] = expert_rows(g("L3_ffn_w_gate"), g("L3_ffn_w_up"), g("L3_ffn_w_down"))

    def heads_rows(wq, bq, wk, bk, wv, bv):
        def lanes(m):
            out = np.zeros((m.shape[0], HEADS, LANE), m.dtype)
            out[:, :, :HD] = m.reshape(-1, HEADS, HD)
            return out.reshape(-1, GROUPS, GH * LANE)
        wq, wk = lanes(wq), lanes(wk)
        bq, bk = lanes(bq[None])[0], lanes(bk[None])[0]
        wv, bv = wv.reshape(D, GROUPS, -1), bv.reshape(GROUPS, -1)
        return np.concatenate([cat(_columns(wq[:, n]), _columns(wk[:, n]), _columns(wv[:, n]),
                                   bq[n][:, None], bk[n][:, None], _in_partition_0(bv[n]))
                               for n in range(GROUPS)])

    none = np.zeros(D, a["x"].dtype)
    o["heads1"] = heads_rows(g("L1_xattn_Wq"), none, g("L1_xattn_Wk"), none, g("L1_xattn_Wv"), none)
    by_width = lambda m: m.reshape(len(m), 2, HALF, HD).transpose(0, 1, 3, 2).reshape(len(m), D)
    for n in "23":
        L = f"L{n}_xattn_"
        o["heads" + n] = cat(_columns(by_width(g(L + "Wq").T)), _columns(by_width(g(L + "Wk").T)),
                             _columns(g(L + "Wv").T), col(by_width(g(L + "bq")[None])[0]),
                             col(by_width(g(L + "bk")[None])[0]), _in_partition_0(g(L + "bv")))
    o["proj1"] = cat(_columns(g("L1_xattn_proj_W")), _in_partition_0(g("L1_xattn_proj_b")))
    o["proj3"] = cat(_columns(g("L3_xattn_Wo").T), _in_partition_0(g("L3_xattn_bo")))
    m = g("mask_SxS_bc0")
    o["mask1"] = cat(_columns(m), _columns(m.T))
    m = g("mask_BxSxS2_if1")
    o["mask2"] = np.concatenate([k.reshape(B, QC, P, SEQ).transpose(0, 2, 1, 3).reshape(B * P, QC * SEQ)
                                 for k in (m, m.transpose(0, 2, 1))], axis=1)

    L = "L1_xattn_"
    o["hist"] = cat(_columns(g(L + "hist_W")), _in_partition_0(g(L + "hist_b")))
    o["hist_gb"] = np.stack([g(L + "hist_ln_g"), g(L + "hist_ln_b")])
    o["ctx_net"] = cat(_columns(g(L + "ctx_W1")), g(L + "ctx_b1")[:, None], g(L + "ctx_W2"),
                       _in_partition_0(g(L + "ctx_b2")))
    o["kg1"] = cat(_columns(g(L + "kg_W1")), _in_partition_0(g(L + "kg_b1")))
    o["kg_gb"] = np.stack([g(L + "kg_ln_g"), g(L + "kg_ln_b")])
    o["kg2"] = cat(_columns(g(L + "kg_W2")), _in_partition_0(g(L + "kg_b2")))
    return {k: np.ascontiguousarray(v) for k, v in o.items()}


def kernel(**inputs):
    import numpy as _np
    import concourse.bacc as _bacc
    from concourse.bass_utils import run_bass_kernel_spmd as _run

    nc = _bacc.Bacc("TRN2", target_bir_lowering=False, num_devices=1)
    arrays = _layouts({k: _np.asarray(v) for k, v in inputs.items()})
    ins = {k: nc.dram_tensor(f"in_{k}_dram", v.shape, mybir.dt.from_np(v.dtype), kind="ExternalInput").ap()
           for k, v in arrays.items()}
    out = nc.dram_tensor("out", (B * SEQ, D), F32, kind="ExternalOutput").ap()
    build(nc, ins, out)
    r = _run(nc, [{f"in_{k}_dram": v for k, v in arrays.items()}], core_ids=[0])
    return r.results[0]["out"].reshape(B, SEQ, D)
```

```python
from contextlib import ExitStack

import concourse.bass as bass
from concourse import mybir

F32 = mybir.dt.float32
BF16 = mybir.dt.bfloat16
I32 = mybir.dt.int32
U32 = mybir.dt.uint32
U8 = mybir.dt.uint8
ALU = mybir.AluOpType
ACT = mybir.ActivationFunctionType
X = mybir.AxisListType.X

P = 128
B, SEQ, D = 8, 256, 256
TILES = B * SEQ // P
DC = D // P
QC = SEQ // P
HEADS, HD = 16, 16
GH = 4
LANE = P // GH
NEG_BIG = -1.0e30
LN_EPS = 1e-5
TAPS = 3
MOST_TILES = 64


class Steps:

    def __init__(self, engine, semaphore):
        self.engine, self.semaphore, self.n = engine, semaphore, 0

    def done(self, instruction):
        instruction.then_inc(self.semaphore, 1)
        self.n = self.n + 1
        self.engine.wait_ge(self.semaphore, self.n)


class Core:

    def __init__(self, nc, whole):
        self.nc, self.whole = nc, whole

    def keep(self, name, shape, dtype=F32):
        return self.whole.enter_context(self.nc.sbuf_tensor(name, shape, dtype))


class Stage:

    def __init__(self, core, name):
        self.core, self.name, self.nc = core, name, core.nc
        self.stack = ExitStack()
        self.sems = []

    def __enter__(self):
        return self

    def __exit__(self, *error):
        self.stack.__exit__(*error)
        if error[0] is None:
            self.nc.clear_and_free_semaphores(self.sems)
            self.nc.all_engine_barrier()

    def sb(self, name, shape, dtype=F32):
        return self.stack.enter_context(self.nc.sbuf_tensor(f"{self.name}_{name}", shape, dtype))

    def psum(self, name, shape, dtype=F32):
        return self.stack.enter_context(self.nc.psum_tensor(f"{self.name}_{name}", shape, dtype))

    def sem(self, name):
        self.sems.append(self.nc.alloc_semaphore(f"{self.name}_{name}"))
        return self.sems[-1]

    def block(self):
        return self.stack.enter_context(self.nc.Block())


def dyn(index, size=P):
    return bass.ds(index * size, size)



def row_statistics(v, steps, src, st, mean, rstd, work, stats_done, var_ready, std_ready):
    with v.Fori(0, TILES // 8) as i:
        for p in range(8):
            v.bn_stats(st[:, 8 * i + p, :], src[:, 8 * i + p, :]).then_inc(stats_done, 1)
    v.wait_ge(stats_done, TILES)
    me, mo, se, so = st[:, :, 1], st[:, :, 4], st[:, :, 2], st[:, :, 5]
    v.tensor_tensor(mean[:, :], me, mo, ALU.add)
    v.tensor_tensor(work[:, 0, :], me, mo, ALU.subtract)
    steps.done(v.tensor_tensor(work[:, 1, :], se, so, ALU.add))
    v.tensor_scalar(mean[:, :], mean[:, :], 0.5, None, ALU.mult)
    v.tensor_scalar(work[:, 1, :], work[:, 1, :], 1.0 / D, LN_EPS, ALU.mult, ALU.add)
    steps.done(v.scalar_tensor_tensor(work[:, 2, :], work[:, 0, :], 0.25, work[:, 0, :],
                                      ALU.mult, ALU.mult))
    v.tensor_tensor(work[:, 3, :], work[:, 1, :], work[:, 2, :], ALU.add).then_inc(var_ready, 1)
    v.wait_ge(std_ready, 1)
    steps.done(v.reciprocal(rstd[:, :], work[:, 4, :]))


def norm_stage(core, name, x, xn, xnT, ident, router=None, logits=None):
    nc = core.nc
    with Stage(core, name) as s:
        st = s.sb("st", [P, TILES, 6])
        mean = s.sb("mean", [P, TILES])
        rstd = s.sb("rstd", [P, TILES])
        work = s.sb("work", [P, 5, TILES])
        row = s.sb("row", [P, 4, D])
        ps_t = s.psum("ps_t", [P, 2, 512])
        stats_done, var_ready, std_ready = s.sem("stats_done"), s.sem("var_ready"), s.sem("std_ready")
        own = s.sem("own")
        row_ready, row_copied = s.sem("row_ready"), [s.sem(f"row_copied{p}") for p in range(4)]
        turned, tile_free = s.sem("turned"), s.sem("tile_free")
        if router is not None:
            E = router.shape[1] // DC
            w = s.sb("router", [P, DC, E])
            colT = s.sb("colT", [P, 4, DC, P])
            ps_l = s.psum("ps_l", [P, TILES, E])
            w_loaded, col_ready, logits_ready = s.sem("w_loaded"), s.sem("col_ready"), s.sem("logits_ready")
        block = s.block()

        @block.sync
        def _(sp):
            if router is not None:
                sp.dma_start(w[:, :, :], router.rearrange("p (c e) -> p c e", c=DC)).then_inc(w_loaded, 16)

        @block.vector
        def _(v):
            steps = Steps(v, own)
            row_statistics(v, steps, x, st, mean, rstd, work, stats_done, var_ready, std_ready)
            with v.Fori(0, TILES // 4) as i:
                for p in range(4):
                    t = 4 * i + p
                    v.wait_ge(turned, t + 1)
                    v.wait_ge(row_copied[p], i + 1)
                    v.tensor_scalar(row[:, p, :], x[:, t, :], mean[:, bass.ds(t, 1)], rstd[:, bass.ds(t, 1)],
                                    ALU.subtract, ALU.mult).then_inc(row_ready, 1)
            if router is not None:
                v.wait_ge(logits_ready, TILES + 4)
                v.tensor_copy(logits[:, :, 0:E], ps_l[:, :, :])

        @block.gpsimd
        def _(pool):
            for copied in row_copied:
                pool.sem_inc(copied, 1)
            with pool.Fori(0, TILES // 4) as i:
                for p in (0, 2):
                    t = 4 * i + p
                    pool.wait_ge(row_ready, t + 1)
                    pool.tensor_copy(xn[:, t, :], row[:, p, :]).then_inc(row_copied[p], 1)

        @block.scalar
        def _(act):
            act.sem_inc(tile_free, 2)
            act.wait_ge(var_ready, 1)
            act.activation(work[:, 4, :], work[:, 3, :], ACT.Sqrt).then_inc(std_ready, 1)
            with act.Fori(0, TILES // 4) as i:
                for p in range(4):
                    t = 4 * i + p
                    if p % 2:
                        act.wait_ge(row_ready, t + 1)
                        act.copy(xn[:, t, :], row[:, p, :]).then_inc(row_copied[p], 1)
                    act.wait_ge(turned, t + 5)
                    tile_T = ps_t[:, p % 2, 0:D].rearrange("p (c n) -> p c n", c=DC)
                    if router is not None:
                        act.wait_ge(logits_ready, t + 1)
                        act.copy(colT[:, p, :, :], tile_T).then_inc(col_ready, 1)
                    act.copy(xnT[:, :, dyn(t)], tile_T).then_inc(tile_free, 1)

        @block.tensor
        def _(pe):
            pe.sem_inc(turned, 4)
            if router is not None:
                pe.sem_inc(logits_ready, 4)
                pe.wait_ge(w_loaded, 16)

            def turn(i, p):
                t = 4 * i + p
                pe.wait_ge(row_ready, t + 1)
                pe.wait_ge(tile_free, t + 1)
                for c in range(DC):
                    last = pe.transpose(ps_t[:, p % 2, c * P:(c + 1) * P], row[:, p, c * P:(c + 1) * P], ident[:, :])
                last.then_inc(turned, 1)

            def route(i, p):
                t = 4 * i + p
                pe.wait_ge(col_ready, t + 1)
                for c in range(DC):
                    last = pe.matmul(ps_l[:, t, :], colT[:, p, c, :], w[:, c, :],
                                     start=(c == 0), stop=(c == DC - 1), skip_group_check=True)
                last.then_inc(logits_ready, 1)

            with pe.Fori(0, TILES // 4) as i:
                for step in range(5):
                    if step < 4:
                        turn(i, step)
                    if step >= 1 and router is not None:
                        route(i, step - 1)



def single_head_stage(core, name, xn, xnT, ctxT, w_dram, ident, ones):
    nc = core.nc
    W3 = 3 * DC * D
    with Stage(core, name) as s:
        w = s.sb("w", [P, W3 + 2 * DC + D])
        wq, wk, wv = (w[:, n * DC * D:(n + 1) * DC * D].rearrange("p (c n) -> p c n", c=DC) for n in range(3))
        bq, bk, bv = w[:, W3:W3 + DC], w[:, W3 + DC:W3 + 2 * DC], w[0:1, W3 + 2 * DC:]
        ctx = s.sb("ctx", [P, 2, DC, SEQ])
        qT, kT, vv = s.sb("qT", [P, DC, SEQ]), s.sb("kT", [P, DC, SEQ]), s.sb("v", [P, QC, D])
        probs, probsT = s.sb("probs", [P, QC, SEQ]), s.sb("probsT", [P, QC, SEQ])
        warm = s.sb("warm", [P, 1])
        negmax, total, inv = s.sb("negmax", [P, QC]), s.sb("total", [P, QC]), s.sb("inv", [P, QC])
        ps_q, ps_k, ps_v, ps_s, ps_pT, ps_o = (s.psum(n, [P, 2, D]) for n in
                                               ("ps_q", "ps_k", "ps_v", "ps_s", "ps_pT", "ps_o"))
        w_loaded, ctx_loaded = s.sem("w_loaded"), [s.sem("ctx_loaded0"), s.sem("ctx_loaded1")]
        projected, q_ready, k_ready, v_ready = (s.sem(n) for n in ("projected", "q_ready", "k_ready", "v_ready"))
        scored, max_ready, probs_ready = s.sem("scored"), s.sem("max_ready"), s.sem("probs_ready")
        turned, probsT_ready, mixed, added, own = (s.sem(n) for n in
                                                   ("turned", "probsT_ready", "mixed", "added", "own"))
        block = s.block()

        @block.sync
        def _(sp):
            sp.dma_start(w[:, :], w_dram).then_inc(w_loaded, 16)
            with sp.Fori(0, B // 2) as i:
                for p in range(2):
                    b = 2 * i + p
                    sp.wait_ge(projected, 3 * b + 3)
                    sp.dma_start(ctx[:, p, :, :].rearrange("p c n -> p (c n)"), ctxT[dyn(b), :])\
                        .then_inc(ctx_loaded[p], 16)

        @block.tensor
        def _(pe):
            pe.sem_inc(projected, 6)
            pe.wait_ge(w_loaded, 16)
            with pe.Fori(0, B // 2) as i:
                for p in range(2):
                    b = 2 * i + p
                    for oc in range(DC):
                        for c in range(DC):
                            last = pe.matmul(ps_q[:, oc, :], wq[:, c, oc * P:(oc + 1) * P],
                                             xnT[:, c, dyn(b, SEQ)], start=(c == 0), stop=(c == DC - 1))
                    last.then_inc(projected, 1)
                    pe.wait_ge(ctx_loaded[p], 16 * (i + 1))
                    for oc in range(DC):
                        for c in range(DC):
                            last = pe.matmul(ps_k[:, oc, :], wk[:, c, oc * P:(oc + 1) * P],
                                             ctx[:, p, c, :], start=(c == 0), stop=(c == DC - 1))
                    last.then_inc(projected, 1)
                    for tc in range(QC):
                        for c in range(DC):
                            pe.matmul(ps_v[:, tc, :], ctx[:, p, c, tc * P:(tc + 1) * P], wv[:, c, :],
                                      start=(c == 0), stop=False)
                        last = pe.matmul(ps_v[:, tc, :], ones[0:1, 0:P], bv, start=False, stop=True)
                    last.then_inc(projected, 1)
                    pe.wait_ge(q_ready, b + 1)
                    pe.wait_ge(k_ready, b + 1)
                    for qc in range(QC):
                        for c in range(DC):
                            last = pe.matmul(ps_s[:, qc, :], qT[:, c, qc * P:(qc + 1) * P], kT[:, c, :],
                                             start=(c == 0), stop=(c == DC - 1))
                    last.then_inc(scored, 1)
                    pe.wait_ge(probs_ready, b + 1)
                    for kc in range(QC):
                        for qc in range(QC):
                            last = pe.transpose(ps_pT[:, kc, qc * P:(qc + 1) * P],
                                                probs[:, qc, kc * P:(kc + 1) * P], ident[:, :])
                    last.then_inc(turned, 1)
                    pe.wait_ge(probsT_ready, b + 1)
                    pe.wait_ge(v_ready, b + 1)
                    pe.wait_ge(added, b + 1)
                    for qc in range(QC):
                        for kc in range(QC):
                            last = pe.matmul(ps_o[:, qc, :], probsT[:, kc, qc * P:(qc + 1) * P], vv[:, kc, :],
                                             start=(kc == 0), stop=(kc == QC - 1))
                    last.then_inc(mixed, 1)

        @block.scalar
        def _(act):
            act.activation(warm[:, :], ones[:, 0:1], ACT.Exp)
            with act.Fori(0, B) as b:
                act.wait_ge(projected, 3 * b + 8)
                for c in range(DC):
                    last = act.activation(kT[:, c, :], ps_k[:, c, :], ACT.Identity, bias=bk[:, c:c + 1])
                last.then_inc(k_ready, 1)
                act.wait_ge(projected, 3 * b + 9)
                act.wait_ge(added, b + 1)
                act.copy(vv[:, :, :], ps_v[:, :, :]).then_inc(v_ready, 1)
                act.wait_ge(max_ready, b + 1)
                for qc in range(QC):
                    last = act.activation(probs[:, qc, :], ps_s[:, qc, :], ACT.Exp, bias=negmax[:, qc:qc + 1],
                                          accum_out=total[:, qc:qc + 1])
                last.then_inc(probs_ready, 1)

        @block.vector
        def _(v):
            steps = Steps(v, own)
            v.sem_inc(added, 1)
            with v.Fori(0, B) as b:
                v.wait_ge(projected, 3 * b + 7)
                for c in range(DC):
                    last = v.tensor_scalar(qT[:, c, :], ps_q[:, c, :], bq[:, c:c + 1], None, ALU.add)
                last.then_inc(q_ready, 1)
                v.wait_ge(scored, b + 1)
                v.tensor_reduce(negmax[:, :], ps_s[:, :, :], X, ALU.max, negate=True).then_inc(max_ready, 1)
                v.wait_ge(turned, b + 1)
                v.tensor_copy(probsT[:, :, :], ps_pT[:, :, :]).then_inc(probsT_ready, 1)
                steps.n = b
                steps.done(v.reciprocal(inv[:, :], total[:, :]))
                v.wait_ge(mixed, b + 1)
                for qc in range(QC):
                    last = v.scalar_tensor_tensor(xn[:, 2 * b + qc, :], ps_o[:, qc, :], inv[:, qc:qc + 1],
                                                  xn[:, 2 * b + qc, :], ALU.mult, ALU.add)
                last.then_inc(added, 1)


def post_norm_stage(core, name, x, r, gain_bias):
    with Stage(core, name) as s:
        st, mean, rstd = s.sb("st", [P, TILES, 6]), s.sb("mean", [P, TILES]), s.sb("rstd", [P, TILES])
        work = s.sb("work", [P, 5, TILES])
        row = s.sb("row", [P, 4, D])
        gb = s.sb("gb", [P, 2, D])
        stats_done, var_ready, std_ready = s.sem("stats_done"), s.sem("var_ready"), s.sem("std_ready")
        own, gb_loaded, normed = s.sem("own"), s.sem("gb_loaded"), s.sem("normed")
        scaled, row_free = s.sem("scaled"), s.sem("row_free")
        block = s.block()

        @block.sync
        def _(sp):
            sp.dma_start(gb[:, :, :], gain_bias.rearrange("(o a) n -> o a n", o=1).to_broadcast([P, 2, D]))\
                .then_inc(gb_loaded, 16)

        @block.scalar
        def _(act):
            act.wait_ge(var_ready, 1)
            act.activation(work[:, 4, :], work[:, 3, :], ACT.Sqrt).then_inc(std_ready, 1)

        @block.gpsimd
        def _(pool):
            pool.sem_inc(row_free, 4)
            pool.wait_ge(gb_loaded, 16)
            with pool.Fori(0, TILES // 4) as i:
                for p in range(4):
                    t = 4 * i + p
                    pool.wait_ge(scaled, t + 1)
                    pool.tensor_tensor(row[:, p, :], row[:, p, :], gb[:, 1, :], ALU.add).then_inc(normed, 1)
                    pool.wait_ge(normed, t + 1)
                    pool.tensor_tensor(x[:, t, :], x[:, t, :], row[:, p, :], ALU.add).then_inc(row_free, 1)
            pool.wait_ge(row_free, TILES + 4)

        @block.vector
        def _(v):
            steps = Steps(v, own)
            row_statistics(v, steps, r, st, mean, rstd, work, stats_done, var_ready, std_ready)
            v.wait_ge(gb_loaded, 16)
            start = steps.n
            with v.Fori(0, TILES // 4) as i:
                for p in range(4):
                    t = 4 * i + p
                    v.wait_ge(row_free, t + 1)
                    steps.n = start + t
                    steps.done(v.tensor_scalar(row[:, p, :], r[:, t, :], mean[:, bass.ds(t, 1)],
                                               rstd[:, bass.ds(t, 1)], ALU.subtract, ALU.mult))
                    v.tensor_tensor(row[:, p, :], row[:, p, :], gb[:, 0, :], ALU.mult).then_inc(scaled, 1)





class Tables:

    def __init__(self, core, most_tiles):
        self.row_iota = core.keep("row_iota", [P, P])
        self.column = core.keep("column", [P, 1])
        self.before = core.keep("before", [P, P])
        self.token_id = {1: core.keep("token_id1", [P, TILES]), 2: core.keep("token_id2", [P, TILES * 2])}
        self.zeros = core.keep("zeros", [P, 64])
        self.token_of = core.keep("token_of", [P, most_tiles], U32)
        self.weights_of = core.keep("weights_of", [P, most_tiles], U32)
        self.slot_of = core.keep("slot_of", [P, TILES * 2], U32)
        self.coef = core.keep("coef", [P, TILES * 2])


def route_stage(core, name, lg, E, K, NT, tb, ones, xn, xn_dram, bias=None, capacity=None, factor=1.0):
    NK = TILES * K
    with Stage(core, name) as s:
        top, top_ix = s.sb("top", [P, TILES, 8]), s.sb("top_ix", [P, TILES, 8], U32)
        expert = s.sb("expert", [P, TILES, K])
        ex, hot, pos = (s.sb(n, [P, TILES, E]) for n in ("ex", "hot", "pos"))
        hot_k = s.sb("hot_k", [P, K, TILES, E])
        picked = s.sb("picked", [P, K, TILES, E])
        ek = s.sb("ek", [P, TILES, K])
        den = s.sb("den", [P, 2, TILES])
        earlier = s.sb("earlier", [P, TILES + 1, E])
        count_i = s.sb("count_i", [P, 2, E], I32)
        tiles_of, tiles_end, first = (s.sb(n, [P, E]) for n in ("tiles_of", "tiles_end", "first"))
        ended = s.sb("ended", [P, NT, E])
        tile_expert = s.sb("tile_expert", [P, NT])
        slot = s.sb("slot", [P, TILES, K])
        kept = s.sb("kept", [P, TILES, K])
        slot_i = s.sb("slot_i", [P, 3, NK], I32)
        lo, hi = s.sb("lo", [P, NK]), s.sb("hi", [P, NK])
        lane_hot, tile_hot = s.sb("lane_hot", [P, 4, P]), s.sb("tile_hot", [P, 4, NT])
        ps_pos, ps_all = (s.psum(n, [P, 512])[:, 0:TILES * E].rearrange("p (t e) -> p t e", e=E)
                          for n in ("ps_pos", "ps_all"))
        ps_tok = s.psum("ps_tok", [P, 512])
        own, maxed, shifted, exped = s.sem("own"), s.sem("maxed"), s.sem("shifted"), s.sem("exped")
        hot_ready, counted, perm_ready = s.sem("hot_ready"), s.sem("counted"), s.sem("perm_ready")
        perm_used, xn_stored, bias_loaded = s.sem("perm_used"), s.sem("xn_stored"), s.sem("bias_loaded")
        if bias is not None:
            bias_sb = s.sb("bias", [P, E])
        block = s.block()

        @block.sync
        def _(sp):
            if bias is not None:
                sp.dma_start(bias_sb[:, :], bias.to_broadcast([P, E])).then_inc(bias_loaded, 16)
            if xn_dram is not None:
                sp.dma_start(xn_dram.rearrange("(t p) d -> p t d", p=P), xn[:, :, :]).then_inc(xn_stored, 16)
                sp.wait_ge(xn_stored, 16)

        @block.scalar
        def _(act):
            act.wait_ge(shifted, 2)
            act.activation(ex[:, :, :], ex[:, :, :], ACT.Exp).then_inc(exped, 1)
            act.activation(ek[:, :, :], ek[:, :, :], ACT.Exp).then_inc(exped, 1)

        @block.tensor
        def _(pe):
            pe.wait_ge(hot_ready, 1)
            flat = hot[:, :, :].rearrange("p t e -> p (t e)")
            pe.matmul(ps_pos.rearrange("p t e -> p (t e)"), tb.before[:, :], flat)
            pe.matmul(ps_all.rearrange("p t e -> p (t e)"), ones[:, :], flat).then_inc(counted, 1)
            out = ps_tok[:, 0:NT]
            pe.sem_inc(perm_used, 4)
            pe.matmul(out, ones[:, :], tb.zeros[:, 0:NT], start=True, stop=False, skip_group_check=True)
            with pe.Fori(0, NK // 4) as i:
                for p in range(4):
                    pe.wait_ge(perm_ready, 4 * i + p + 1)
                    pe.matmul(out, lane_hot[:, p, :], tile_hot[:, p, :], start=False, stop=False,
                              skip_group_check=True).then_inc(perm_used, 1)
            pe.matmul(out, ones[:, :], tb.zeros[:, 0:NT], start=False, stop=True,
                      skip_group_check=True).then_inc(perm_used, 1)

        @block.vector
        def _(v):
            steps = Steps(v, own)
            over_e = lambda ap: ap.unsqueeze(2).to_broadcast([P, TILES, E])
            if bias is not None:
                v.wait_ge(bias_loaded, 16)
                steps.done(v.tensor_tensor(lg, lg, bias_sb[:, :].unsqueeze(1).to_broadcast([P, TILES, E]),
                                           ALU.add))
            for t in range(TILES):
                v.max(top[:, t, :], lg[:, t, :]).then_inc(maxed, 1)
            v.wait_ge(maxed, TILES)
            for t in range(TILES):
                v.max_index(top_ix[:, t, :], top[:, t, :], lg[:, t, :]).then_inc(maxed, 1)
            v.tensor_tensor(ex[:, :, :], lg, over_e(top[:, :, 0]), ALU.subtract).then_inc(shifted, 1)
            v.tensor_tensor(ek[:, :, :], top[:, :, 0:K], top[:, :, 0:1].to_broadcast([P, TILES, K]),
                            ALU.subtract).then_inc(shifted, 1)
            v.wait_ge(maxed, 2 * TILES)
            steps.done(v.tensor_copy(expert[:, :, :], top_ix[:, :, 0:K]))
            for k in range(K):
                last = v.tensor_tensor(hot_k[:, k, :, :],
                                       tb.row_iota[:, 0:E].unsqueeze(1).to_broadcast([P, TILES, E]),
                                       over_e(expert[:, :, k]), ALU.is_equal)
            steps.done(last)
            if K == 2:
                v.tensor_tensor(hot[:, :, :], hot_k[:, 0, :, :], hot_k[:, 1, :, :], ALU.add)\
                    .then_inc(hot_ready, 1)
            else:
                v.tensor_copy(hot[:, :, :], hot_k[:, 0, :, :]).then_inc(hot_ready, 1)
            v.wait_ge(exped, 2)
            steps.done(v.reduce_sum(den[:, 0, :], ex[:, :, :], X))
            steps.done(v.reciprocal(den[:, 1, :], den[:, 0, :]))
            coef = tb.coef[:, 0:NK].rearrange("p (t k) -> p t k", k=K)
            steps.done(v.tensor_tensor(coef, ek[:, :, :], den[:, 1, :].unsqueeze(2).to_broadcast([P, TILES, K]),
                                       ALU.mult))
            if factor != 1.0:
                steps.done(v.tensor_scalar(tb.coef[:, 0:NK], tb.coef[:, 0:NK], factor, None, ALU.mult))
            v.memset(earlier[:, 0, :], 0.0).then_inc(own, 1)
            steps.n += 1
            v.wait_ge(own, steps.n)
            v.wait_ge(counted, 1)
            for t in range(TILES):
                steps.done(v.tensor_tensor(earlier[:, t + 1, :], earlier[:, t, :], ps_all[:, t, :], ALU.add))
            steps.done(v.tensor_tensor(pos[:, :, :], ps_pos[:, :, :], earlier[:, 0:TILES, :], ALU.add))
            if capacity is None:
                steps.done(v.tensor_scalar(count_i[:, 0, :], earlier[:, TILES, :], float(P - 1), None, ALU.add))
                steps.done(v.tensor_scalar(count_i[:, 1, :], count_i[:, 0, :], 7, None, ALU.logical_shift_right))
                steps.done(v.tensor_copy(tiles_of[:, :], count_i[:, 1, :]))
                steps.done(v.tensor_tensor_scan(tiles_end[:, :], ones[:, 0:E], tiles_of[:, :], 0.0,
                                                ALU.mult, ALU.add))
                steps.done(v.tensor_tensor(first[:, :], tiles_end[:, :], tiles_of[:, :], ALU.subtract))
                steps.done(v.tensor_scalar(first[:, :], first[:, :], float(P), None, ALU.mult))
                steps.done(v.tensor_tensor(pos[:, :, :], pos[:, :, :],
                                           first[:, :].unsqueeze(1).to_broadcast([P, TILES, E]), ALU.add))
                steps.done(v.tensor_tensor(ended[:, :, :], tiles_end[:, :].unsqueeze(1).to_broadcast([P, NT, E]),
                                           tb.row_iota[:, 0:NT].unsqueeze(2).to_broadcast([P, NT, E]),
                                           ALU.is_le))
                steps.done(v.reduce_sum(tile_expert[:, :], ended[:, :, :], X))
                steps.done(v.tensor_scalar(tile_expert[:, :], tile_expert[:, :], float(E - 1), float(P),
                                           ALU.min, ALU.mult))
            else:
                steps.done(v.tensor_scalar(tile_expert[:, :], tb.row_iota[:, 0:NT], float(P), None, ALU.mult))
            v.tensor_scalar(tb.weights_of[:, 0:NT], tile_expert[:, :], tb.column[:, 0:1], None, ALU.add)
            for k in range(K):
                last = v.tensor_tensor(picked[:, k, :, :], hot_k[:, k, :, :], pos[:, :, :], ALU.mult)
            steps.done(last)
            for k in range(K):
                last = v.reduce_sum(slot[:, :, k], picked[:, k, :, :], X)
            steps.done(last)
            slots = slot[:, :, :].rearrange("p t k -> p (t k)")
            kept_k = kept[:, :, :].rearrange("p t k -> p (t k)")
            if capacity is None:
                steps.done(v.tensor_copy(slot_i[:, 0, :], slots))
                v.tensor_copy(tb.slot_of[:, 0:NK], slots)
                v.tensor_scalar(slot_i[:, 1, :], slot_i[:, 0, :], P - 1, None, ALU.bitwise_and)
                steps.done(v.tensor_scalar(slot_i[:, 2, :], slot_i[:, 0, :], 7, None, ALU.logical_shift_right))
                v.tensor_copy(lo[:, :], slot_i[:, 1, :])
                steps.done(v.tensor_copy(hi[:, :], slot_i[:, 2, :]))
            else:
                steps.done(v.tensor_scalar(kept_k, slots, float(capacity), None, ALU.is_lt))
                v.tensor_tensor(tb.coef[:, 0:NK], tb.coef[:, 0:NK], kept_k, ALU.mult)
                v.tensor_copy(lo[:, :], slots)
                steps.done(v.tensor_copy(hi[:, :], expert[:, :, :].rearrange("p t k -> p (t k)")))
                steps.done(v.tensor_scalar(slots, slots, float(capacity - 1), None, ALU.min))
                v.scalar_tensor_tensor(tb.slot_of[:, 0:NK], hi[:, :], float(capacity), slots,
                                       ALU.mult, ALU.add)
            start = steps.n
            with v.Fori(0, NK // 4) as i:
                for p in range(4):
                    n = 4 * i + p
                    v.wait_ge(perm_used, n + 1)
                    v.tensor_scalar(tile_hot[:, p, :], tb.row_iota[:, 0:NT], hi[:, bass.ds(n, 1)],
                                    tb.token_id[K][:, bass.ds(n, 1)], ALU.is_equal, ALU.mult)
                    v.tensor_scalar(lane_hot[:, p, :], tb.row_iota[:, :], lo[:, bass.ds(n, 1)], None,
                                    ALU.is_equal).then_inc(perm_ready, 1)
            v.wait_ge(perm_used, NK + 5)
            v.tensor_copy(tb.token_of[:, 0:NT], ps_tok[:, 0:NT])


def experts_stage(core, name, NT, rows, chunks, w_dram, tb, xn_dram, y_dram, ident, ones, biased=False, ahead=8):
    F = sum(chunks)
    NF = len(chunks)
    W = w_dram.shape[1]
    HB = -(-NF * P // 512)
    with Stage(core, name) as s:
        w = s.sb("w", [P, ahead, W])
        xg, xT = s.sb("xg", [P, ahead, D]), s.sb("xT", [P, 2, DC, P])
        x_ix = s.sb("x_ix", [P, ahead, 1], U32)
        warm = s.sb("warm", [P, 1])
        h = s.sb("h", [P, 2, NF, rows])
        y = s.sb("y", [P, 2, D])
        ps_x = s.psum("ps_x", [P, 2, 512])
        ps_g = s.psum("ps_g", [P, 2, HB * 512])
        if not biased:
            silu = s.sb("silu", [P, 2, NF, rows])
            ps_u = s.psum("ps_u", [P, 2, HB * 512])
        ps_y = s.psum("ps_y", [P, 2, 512])
        x_in, w_in = ([s.sem(f"{n}{u}") for u in range(ahead)] for n in ("x_in", "w_in"))
        stored = [s.sem(f"stored{p}") for p in range(2)]
        ix_ready, ix_passed, w_passed = s.sem("ix_ready"), s.sem("ix_passed"), s.sem("w_passed")
        turned, xT_ready = s.sem("turned"), s.sem("xT_ready")
        gu_ready, silu_ready, h_ready = s.sem("gu_ready"), s.sem("silu_ready"), s.sem("h_ready")
        y_ready, y_copied = s.sem("y_ready"), s.sem("y_copied")
        block = s.block()

        gate_w = lambda p: w[:, p, 0:DC * F].rearrange("p (c f) -> p c f", c=DC)
        up_w = lambda p: w[:, p, DC * F:2 * DC * F].rearrange("p (c f) -> p c f", c=DC)
        down_at = DC * F if biased else 2 * DC * F
        down_w = lambda p: w[:, p, down_at:down_at + NF * D].rearrange("p (j n) -> p j n", j=NF)
        b1 = lambda p, j: w[:, p, down_at + NF * D + j:down_at + NF * D + j + 1]
        b2 = lambda p: w[0:1, p, down_at + NF * D + NF:down_at + NF * D + NF + D]

        @block.gpsimd
        def _(pool):
            with pool.Fori(0, NT // ahead) as i:
                for u in range(ahead):
                    j = ahead * i + u
                    pool.wait_ge(y_ready, j + 1)
                    pool.tensor_copy(x_ix[:, u, :], tb.token_of[:, bass.ds(j, 1)]).then_inc(ix_ready, 1)
                    pool.wait_ge(ix_ready, j + 1)
                    pool.sem_inc(ix_passed, 1)
                    pool.indirect_dma_start(xg[:, u, :], None, xn_dram,
                                            bass.IndirectOffsetOnAxis(ap=x_ix[:, u, :], axis=0))\
                        .then_inc(x_in[u], 16)

        @block.tensor
        def _(pe):
            pe.sem_inc(y_ready, ahead)

            def turn_rows(i, u):
                pe.wait_ge(x_in[u], 16 * (i + 1))
                for c in range(DC):
                    last = pe.transpose(ps_x[:, u % 2, c * P:(c + 1) * P], xg[:, u, c * P:(c + 1) * P], ident[:, :])
                last.then_inc(turned, 1)

            def hidden_layer(i, u):
                p = u % 2
                pe.wait_ge(xT_ready, ahead * i + u + 1)
                pe.wait_ge(w_in[u], 16 * (i + 1))
                for ps, wt in ((ps_g, gate_w(u)),) if biased else ((ps_g, gate_w(u)), (ps_u, up_w(u))):
                    for j, m in enumerate(chunks):
                        for c in range(DC):
                            last = pe.matmul(ps[0:m, p, j * P:j * P + rows], wt[:, c, j * P:j * P + m],
                                             xT[:, p, c, 0:rows], start=(c == 0), stop=(c == DC - 1))
                last.then_inc(gu_ready, 1)

            def output_layer(i, u):
                p = u % 2
                pe.wait_ge(h_ready, ahead * i + u + 3)
                pe.wait_ge(y_copied, ahead * i + u + 1)
                for j, m in enumerate(chunks):
                    last = pe.matmul(ps_y[0:rows, p, 0:D], h[0:m, p, j, :], down_w(u)[0:m, j, :],
                                     start=(j == 0), stop=(j == NF - 1 and not biased))
                if biased:
                    last = pe.matmul(ps_y[0:rows, p, 0:D], ones[0:1, 0:rows], b2(u), start=False, stop=True)
                last.then_inc(y_ready, 1)

            with pe.Fori(0, NT // ahead) as i:
                for step in range(ahead + 2):
                    for lag, part in enumerate((turn_rows, hidden_layer, output_layer)):
                        if 0 <= step - lag < ahead:
                            part(i, step - lag)

        def parts():
            full = [j for j, m in enumerate(chunks) if m == P]
            if full:
                yield P, 0, len(full)
            if len(full) < NF:
                yield chunks[-1], len(full), NF

        def hidden(ps, p, m, a, b):
            return ps[0:m, p, a * P:b * P].rearrange("p (j n) -> p j n", n=P)[:, :, 0:rows]

        @block.scalar
        def _(act):
            if biased:
                act.sem_inc(h_ready, 2)
            act.activation(warm[:, :], ones[:, 0:1], ACT.Silu)

            def copy_rows(i, u):
                act.wait_ge(turned, ahead * i + u + 1)
                act.copy(xT[:, u % 2, :, :], ps_x[:, u % 2, 0:D].rearrange("p (c n) -> p c n", c=DC))\
                    .then_inc(xT_ready, 1)

            def nonlinear(i, u):
                p, j = u % 2, ahead * i + u
                act.wait_ge(gu_ready, j + 1)
                if biased:
                    act.wait_ge(y_ready, j + ahead - 1)
                    for c in range(NF):
                        last = act.activation(h[:, p, c, :], ps_g[:, p, c * P:c * P + rows], ACT.Silu,
                                              bias=b1(u, c))
                    last.then_inc(h_ready, 1)
                else:
                    act.wait_ge(h_ready, j + 1)
                    for m, a, b in parts():
                        last = act.activation(silu[0:m, p, a:b, :], hidden(ps_g, p, m, a, b), ACT.Silu)
                    last.then_inc(silu_ready, 1)

            with act.Fori(0, NT // ahead) as i:
                for step in range(ahead + 1):
                    if step < ahead:
                        copy_rows(i, step)
                    if step >= 1:
                        nonlinear(i, step - 1)

        @block.vector
        def _(v):
            if not biased:
                v.sem_inc(h_ready, 2)
            v.sem_inc(y_copied, 2)

            def multiply(i, u):
                p = u % 2
                v.wait_ge(silu_ready, ahead * i + u + 1)
                for m, a, b in parts():
                    last = v.tensor_tensor(h[0:m, p, a:b, :], hidden(ps_u, p, m, a, b), silu[0:m, p, a:b, :],
                                           ALU.mult)
                last.then_inc(h_ready, 1)

            def copy_out(i, u):
                v.wait_ge(y_ready, ahead * i + u + 1 + ahead)
                v.wait_ge(stored[u % 2], 16 * (ahead // 2 * i + u // 2 + 1))
                v.tensor_copy(y[0:rows, u % 2, :], ps_y[0:rows, u % 2, 0:D]).then_inc(y_copied, 1)

            with v.Fori(0, NT // ahead) as i:
                for step in range(ahead + 1):
                    if step < ahead and not biased:
                        multiply(i, step)
                    if step >= 1:
                        copy_out(i, step - 1)

        @block.sync
        def _(sp):
            for p in range(2):
                sp.sem_inc(stored[p], 16)

            def load_weights(i, u):
                j = ahead * i + u
                sp.wait_ge(y_ready, j + 1)
                sp.sem_inc(w_passed, 1)
                row = sp.value_load(tb.weights_of[0:1, bass.ds(j, 1)], min_val=0, max_val=w_dram.shape[0] - P)
                sp.dma_start(w[:, u, :], w_dram[bass.ds(row, P), :]).then_inc(w_in[u], 16)

            def store(i, u):
                j = ahead * i + u
                sp.wait_ge(y_copied, j + 3)
                sp.dma_start(y_dram[dyn(j, rows), :], y[0:rows, u % 2, :]).then_inc(stored[u % 2], 16)

            for u in range(ahead):
                load_weights(0, u)
            with sp.Fori(1, NT // ahead) as i:
                for u in range(ahead):
                    load_weights(i, u)
                    store(i - 1, u)
            for u in range(ahead):
                store(NT // ahead - 1, u)
            for p in range(2):
                sp.wait_ge(stored[p], 16 * (NT // 2 + 1))


def combine_stage(core, name, K, tb, y_dram, x, xn=None):
    with Stage(core, name) as s:
        yg = s.sb("yg", [P, 4, K, D])
        ix = s.sb("ix", [P, 4, K], U32)
        y_in = [[s.sem(f"y_in{p}{k}") for k in range(K)] for p in range(4)]
        ix_ready, ix_passed, used, own = s.sem("ix_ready"), s.sem("ix_passed"), s.sem("used"), s.sem("own")
        block = s.block()

        @block.gpsimd
        def _(pool):
            with pool.Fori(0, TILES // 4) as i:
                for p in range(4):
                    t = 4 * i + p
                    pool.wait_ge(used, t + 1)
                    pool.tensor_copy(ix[:, p, :], tb.slot_of[:, dyn(t, K)]).then_inc(ix_ready, 1)
                    pool.wait_ge(ix_ready, t + 1)
                    pool.sem_inc(ix_passed, 1)
                    for k in range(K):
                        pool.indirect_dma_start(yg[:, p, k, :], None, y_dram,
                                                bass.IndirectOffsetOnAxis(ap=ix[:, p, k:k + 1], axis=0))\
                            .then_inc(y_in[p][k], 16)

        @block.vector
        def _(v):
            v.sem_inc(used, 4)
            if xn is not None:
                v.tensor_tensor(x[:, :, :], x[:, :, :], xn[:, :, :], ALU.add).then_inc(own, 1)
                v.wait_ge(own, 1)
            first = 1 if xn is not None else 0
            with v.Fori(0, TILES // 4) as i:
                for p in range(4):
                    t = 4 * i + p
                    for k in range(K):
                        v.wait_ge(y_in[p][k], 16 * (i + 1))
                        if k == K - 1:
                            if K == 2:
                                v.wait_ge(own, first + t + 1)
                            v.scalar_tensor_tensor(x[:, t, :], yg[:, p, k, :], tb.coef[:, bass.ds(t * K + k, 1)],
                                                   x[:, t, :], ALU.mult, ALU.add).then_inc(used, 1)
                        else:
                            v.scalar_tensor_tensor(x[:, t, :], yg[:, p, k, :], tb.coef[:, bass.ds(t * K + k, 1)],
                                                   x[:, t, :], ALU.mult, ALU.add).then_inc(own, 1)


def shared_stage(core, name, xnT, gate_logit, w_dram, x):
    F = 704
    chunks = [P] * (F // P) + [F % P]
    NF = len(chunks)
    BANKS = NF // 2

    def bank_parts(n):
        return ((P, 2 * n, 2 * n + 2),) if chunks[2 * n + 1] == P else ((P, 2 * n, 2 * n + 1),
                                                                       (chunks[-1], 2 * n + 1, 2 * n + 2))

    with Stage(core, name) as s:
        w = s.sb("w", [P, w_dram.shape[1]])
        gate_w = w[:, 0:DC * F].rearrange("p (c f) -> p c f", c=DC)
        up_w = w[:, DC * F:2 * DC * F].rearrange("p (c f) -> p c f", c=DC)
        down_w = w[:, 2 * DC * F:].rearrange("p (j n) -> p j n", j=NF)
        silu, h = s.sb("silu", [P, NF, SEQ]), s.sb("h", [P, NF, SEQ])
        share, warm = s.sb("share", [P, TILES]), s.sb("warm", [P, 1])
        ps_g, ps_u, ps_y = (s.psum(n, [P, m, 256]) for n, m in (("ps_g", NF), ("ps_u", NF), ("ps_y", 2)))
        w_loaded, share_ready, gu_ready, silu_ready = (s.sem(n) for n in
                                                       ("w_loaded", "share_ready", "gu_ready", "silu_ready"))
        h_ready, y_ready, added = s.sem("h_ready"), s.sem("y_ready"), s.sem("added")
        block = s.block()

        @block.sync
        def _(sp):
            sp.dma_start(w[:, :], w_dram).then_inc(w_loaded, 16)

        @block.tensor
        def _(pe):
            pe.wait_ge(w_loaded, 16)
            with pe.Fori(0, B) as b:
                for j, m in enumerate(chunks):
                    for ps, wt in ((ps_g, gate_w), (ps_u, up_w)):
                        for c in range(DC):
                            last = pe.matmul(ps[0:m, j, :], wt[:, c, j * P:j * P + m], xnT[:, c, dyn(b, SEQ)],
                                             start=(c == 0), stop=(c == DC - 1))
                    if j % 2:
                        last.then_inc(gu_ready, 1)
                pe.wait_ge(h_ready, BANKS * (b + 1))
                pe.wait_ge(added, b + 1)
                for q in range(QC):
                    for j, m in enumerate(chunks):
                        last = pe.matmul(ps_y[:, q, :], h[0:m, j, q * P:(q + 1) * P], down_w[0:m, j, :],
                                         start=(j == 0), stop=(j == NF - 1))
                last.then_inc(y_ready, 1)

        @block.scalar
        def _(act):
            act.wait_ge(w_loaded, 16)
            act.activation(share[:, :], gate_logit, ACT.Sigmoid).then_inc(share_ready, 1)
            act.activation(warm[:, :], w[:, 0:1], ACT.Silu)
            with act.Fori(0, B) as b:
                for n in range(BANKS):
                    act.wait_ge(gu_ready, b * BANKS + n + 1)
                    for m, j0, j1 in bank_parts(n):
                        last = act.activation(silu[0:m, j0:j1, :], ps_g[0:m, j0:j1, :], ACT.Silu)
                    last.then_inc(silu_ready, 1)

        @block.vector
        def _(v):
            v.sem_inc(added, 1)
            v.wait_ge(share_ready, 1)
            with v.Fori(0, B) as b:
                for n in range(BANKS):
                    v.wait_ge(silu_ready, b * BANKS + n + 1)
                    for m, j0, j1 in bank_parts(n):
                        last = v.tensor_tensor(h[0:m, j0:j1, :], ps_u[0:m, j0:j1, :], silu[0:m, j0:j1, :],
                                               ALU.mult)
                    last.then_inc(h_ready, 1)
                v.wait_ge(y_ready, b + 1)
                for q in range(QC):
                    t = 2 * b + q
                    last = v.scalar_tensor_tensor(x[:, t, :], ps_y[:, q, :], share[:, bass.ds(t, 1)],
                                                  x[:, t, :], ALU.mult, ALU.add)
                last.then_inc(added, 1)



def project_stage(core, name, x, mixed, w_dram, ident, ones):
    with Stage(core, name) as s:
        w = s.sb("w", [P, DC * D + D])
        row, rowT = s.sb("row", [P, 4, D]), s.sb("rowT", [P, 2, DC, P])
        ps_t, ps_y = s.psum("ps_t", [P, 2, 512]), s.psum("ps_y", [P, 2, 512])
        w_loaded, row_ready, turned, rowT_ready, summed, added = (
            s.sem(n) for n in ("w_loaded", "row_ready", "turned", "rowT_ready", "summed", "added"))
        block = s.block()

        @block.sync
        def _(sp):
            sp.dma_start(w[:, :], w_dram).then_inc(w_loaded, 16)

        @block.gpsimd
        def _(pool):
            with pool.Fori(0, TILES // 4) as i:
                for p in range(4):
                    pool.wait_ge(turned, 4 * i + p + 1)
                    pool.tensor_copy(row[:, p, :], mixed[:, 4 * i + p, :]).then_inc(row_ready, 1)

        @block.scalar
        def _(act):
            with act.Fori(0, TILES // 4) as i:
                for p in range(4):
                    act.wait_ge(turned, 4 * i + p + 5)
                    act.wait_ge(added, 4 * i + p + 1)
                    act.copy(rowT[:, p % 2, :, :], ps_t[:, p % 2, 0:D].rearrange("p (c n) -> p c n", c=DC))\
                        .then_inc(rowT_ready, 1)

        @block.tensor
        def _(pe):
            pe.sem_inc(turned, 4)
            pe.sem_inc(rowT_ready, 2)
            pe.wait_ge(w_loaded, 16)

            def turn(i, p):
                pe.wait_ge(row_ready, 4 * i + p + 1)
                pe.wait_ge(rowT_ready, 4 * i + p + 1)
                for c in range(DC):
                    last = pe.transpose(ps_t[:, p % 2, c * P:(c + 1) * P], row[:, p, c * P:(c + 1) * P], ident[:, :])
                last.then_inc(turned, 1)

            def product(i, p):
                out = ps_y[:, p % 2, 0:D]
                pe.wait_ge(rowT_ready, 4 * i + p + 3)
                for c in range(DC):
                    pe.matmul(out, rowT[:, p % 2, c, :], w[:, c * D:(c + 1) * D], start=(c == 0), stop=False)
                pe.matmul(out, ones[0:1, 0:P], w[0:1, DC * D:], start=False, stop=True).then_inc(summed, 1)

            with pe.Fori(0, TILES // 4) as i:
                for step in range(5):
                    if step < 4:
                        turn(i, step)
                    if step >= 1:
                        product(i, step - 1)

        @block.vector
        def _(v):
            v.sem_inc(added, 2)
            with v.Fori(0, TILES // 2) as i:
                for p in range(2):
                    t = 2 * i + p
                    v.wait_ge(summed, t + 1)
                    v.tensor_tensor(x[:, t, :], x[:, t, :], ps_y[:, p, 0:D], ALU.add).then_inc(added, 1)



def context_kernels_stage(core, name, ctxT, a, ident, ones, tb, kernels):
    C, A1, T9 = 2 * D, P, HEADS * TAPS * TAPS
    CC = C // P
    with Stage(core, name) as s:
        hist = s.sb("hist", [P, DC * C + C])
        gb = s.sb("gb", [P, 2, C])
        w1 = s.sb("w1", [P, CC * A1 + 3])
        kg1 = s.sb("kg1", [P, CC * D + D])
        kg_gb = s.sb("kg_gb", [P, 2, D])
        kg2 = s.sb("kg2", [P, DC * T9 + T9])
        ctx = s.sb("ctx", [P, 2, DC, SEQ])
        z = s.sb("z", [P, TILES, C])
        st = s.sb("st", [P, TILES, 6])
        mean, rstd, work = s.sb("mean", [P, TILES]), s.sb("rstd", [P, TILES]), s.sb("work", [P, 5, TILES])
        row = s.sb("row", [P, 4, C])
        rowT = s.sb("rowT", [P, 2, CC, P])
        a1 = s.sb("a1", [P, 2, P])
        pool_w = s.sb("pool_w", [1, B, SEQ])
        pool_n = s.sb("pool_n", [1, 3, B])
        w_cols = s.sb("w_cols", [P, TILES, B])
        cc, ccT = s.sb("cc", [B, C]), s.sb("ccT", [P, CC, B])
        k1, k1T = s.sb("k1", [B, D]), s.sb("k1T", [P, DC, B])
        k_st, k_work = s.sb("k_st", [B, 6]), s.sb("k_work", [B, 8])
        taps = s.sb("taps", [B, HEADS, TAPS * TAPS])
        taps_n = s.sb("taps_n", [B, 3, HEADS])
        pick = s.sb("pick", [B, B, P])
        ps_a, ps_b = s.psum("ps_a", [P, 2, 512]), s.psum("ps_b", [P, 2, 512])
        ps_c, ps_d = s.psum("ps_c", [P, 2, 512]), s.psum("ps_d", [P, 2, 512])
        loaded, ctx_in = s.sem("loaded"), [s.sem("ctx_in0"), s.sem("ctx_in1")]
        hidden, copied, measured = s.sem("hidden"), s.sem("copied"), s.sem("measured")
        var_ready, std_ready, own, pool_own = (s.sem(n) for n in ("var_ready", "std_ready", "own", "pool_own"))
        normed, scaled, gelued, turned = (s.sem(n) for n in ("normed", "scaled", "gelued", "turned"))
        rowT_ready, a1_summed, a1_ready, weighed, weights_kept = (
            s.sem(n) for n in ("rowT_ready", "a1_summed", "a1_ready", "weighed", "weights_kept"))
        relay, z_kept = s.sem("relay"), s.sem("z_kept")
        warm = s.sb("warm", [P, 1])

        def tiles(engine, parts):
            with engine.Fori(0, TILES // 4) as i:
                for step in range(4 + len(parts) - 1):
                    for lag, part in enumerate(parts):
                        if part and 0 <= step - lag < 4:
                            part(4 * i + step - lag, 2 * i + (step - lag) // 2, step - lag)

        block = s.block()
        (POOL_SHIFTED, POOL_EXPED, POOL_NORMED, COLUMNS, COLUMNS_SPREAD, POOLED, POOLED_COPIED, POOLED_TURNED,
         POOLED_T_COPIED, KG_SUMMED, KG_VAR, KG_STD, KG_NORMED, KG_GELUED, KG_TURNED, KG_T_COPIED, TAPS_SUMMED,
         TAPS_SHIFTED, TAPS_EXPED, TAPS_NORMED, TAPS_SPREAD) = range(1, 22)
        b1, w2, b2 = w1[:, CC * A1:CC * A1 + 1], w1[:, CC * A1 + 1:CC * A1 + 2], w1[0:1, CC * A1 + 2:CC * A1 + 3]

        @block.sync
        def _(sp):
            for to, of in ((hist, a["hist"]), (w1, a["ctx_net"]), (kg1, a["kg1"]), (kg2, a["kg2"])):
                sp.dma_start(to[:, :], of).then_inc(loaded, 16)
            for to, of, n in ((gb, a["hist_gb"], C), (kg_gb, a["kg_gb"], D)):
                sp.dma_start(to[:, :, :], of.rearrange("(o a) n -> o a n", o=1).to_broadcast([P, 2, n]))\
                    .then_inc(loaded, 16)
            with sp.Fori(0, B // 2) as i:
                for p in range(2):
                    sp.wait_ge(hidden, 2 * (2 * i + p) + 2)
                    sp.dma_start(ctx[:, p, :, :].rearrange("p c n -> p (c n)"), ctxT[dyn(2 * i + p), :])\
                        .then_inc(ctx_in[p], 16)

        @block.tensor
        def _(pe):
            pe.sem_inc(hidden, 4)
            pe.sem_inc(turned, 4)
            pe.sem_inc(a1_summed, 2)
            pe.sem_inc(weighed, 2)
            pe.wait_ge(loaded, 96)
            with pe.Fori(0, B // 2) as i:
                for p in range(2):
                    pe.wait_ge(ctx_in[p], 16 * (i + 1))
                    for q in range(QC):
                        t = 2 * (2 * i + p) + q
                        pe.wait_ge(copied, t + 1)
                        pe.wait_ge(measured, t + 1)
                        for c in range(DC):
                            pe.matmul(ps_a[:, q, :], ctx[:, p, c, q * P:(q + 1) * P], hist[:, c * C:(c + 1) * C],
                                      start=(c == 0), stop=False)
                        pe.matmul(ps_a[:, q, :], ones[0:1, 0:P], hist[0:1, DC * C:], start=False, stop=True)\
                            .then_inc(hidden, 1)
            def turn(t, b, u):
                pe.wait_ge(gelued, t + 1)
                pe.wait_ge(rowT_ready, t + 1)
                for c in range(CC):
                    last = pe.transpose(ps_b[:, u % 2, c * P:(c + 1) * P], row[:, u, c * P:(c + 1) * P], ident[:, :])
                last.then_inc(turned, 1)

            def first_layer(t, b, u):
                pe.wait_ge(rowT_ready, t + 3)
                pe.wait_ge(a1_ready, t + 1)
                for c in range(CC):
                    last = pe.matmul(ps_c[:, u % 2, 0:P], w1[:, c * A1:(c + 1) * A1], rowT[:, u % 2, c, :],
                                     start=(c == 0), stop=(c == CC - 1))
                last.then_inc(a1_summed, 1)

            def second_layer(t, b, u):
                pe.wait_ge(a1_ready, t + 3)
                pe.wait_ge(weights_kept, t + 1)
                pe.matmul(ps_d[0:1, u % 2, 0:P], w2, a1[:, u % 2, :]).then_inc(weighed, 1)

            tiles(pe, (turn, first_layer, second_layer))
            pe.wait_ge(relay, POOL_NORMED)
            for t in range(TILES):
                last = pe.matmul(ps_a[:, 0, t:t + 1], pool_w[0:1, t // QC, (t % QC) * P:(t % QC + 1) * P],
                                 ones[0:1, 0:1])
            last.then_inc(relay, 1)
            pe.wait_ge(relay, COLUMNS_SPREAD)
            for t in range(TILES):
                last = pe.matmul(ps_b[0:B, 0, :], w_cols[:, t, :], z[:, t, :], start=(t == 0), stop=(t == TILES - 1))
            last.then_inc(relay, 1)
            pe.wait_ge(relay, POOLED_COPIED)
            for c in range(CC):
                last = pe.transpose(ps_c[:, 0, c * B:(c + 1) * B], cc[:, c * P:(c + 1) * P], ident[0:B, 0:B])
            last.then_inc(relay, 1)
            pe.wait_ge(relay, POOLED_T_COPIED)
            for c in range(CC):
                pe.matmul(ps_d[0:B, 0, 0:D], ccT[:, c, :], kg1[:, c * D:(c + 1) * D], start=(c == 0), stop=False)
            pe.matmul(ps_d[0:B, 0, 0:D], ones[0:1, 0:B], kg1[0:1, CC * D:], start=False, stop=True).then_inc(relay, 1)
            pe.wait_ge(relay, KG_GELUED)
            for c in range(DC):
                last = pe.transpose(ps_c[:, 1, c * B:(c + 1) * B], k1[:, c * P:(c + 1) * P], ident[0:B, 0:B])
            last.then_inc(relay, 1)
            pe.wait_ge(relay, KG_T_COPIED)
            for c in range(DC):
                pe.matmul(ps_d[0:B, 1, 0:T9], k1T[:, c, :], kg2[:, c * T9:(c + 1) * T9], start=(c == 0), stop=False)
            pe.matmul(ps_d[0:B, 1, 0:T9], ones[0:1, 0:B], kg2[0:1, DC * T9:], start=False, stop=True)\
                .then_inc(relay, 1)
            pe.wait_ge(relay, TAPS_NORMED)
            pe.wait_ge(pool_own, 2)
            for b in range(B):
                bank = (ps_a[:, 1], ps_b[:, 1], ps_c[:, 1])[b // 3]
                last = pe.matmul(bank[:, (b % 3) * T9:(b % 3 + 1) * T9], pick[:, b, :],
                                 taps[:, :, :].rearrange("b h t -> b (h t)"), start=True, stop=True,
                                 skip_group_check=True)
            last.then_inc(relay, 1)

        @block.gpsimd
        def _(pool):
            pool.memset(w_cols[:, :, :], 0.0)
            pool.memset(pick[:, :, :], 1.0).then_inc(pool_own, 1)
            pool.wait_ge(pool_own, 1)
            pool.affine_select(out=pick[:, :, :], in_=pick[:, :, :], compare_op=ALU.is_equal, fill=0.0, base=0,
                               pattern=[[-1, B], [0, P]], channel_multiplier=1).then_inc(pool_own, 1)
            pool.wait_ge(loaded, 96)

            def add_bias(t, b, u):
                pool.wait_ge(scaled, t + 1)
                pool.tensor_tensor(row[:, u, :], row[:, u, :], gb[:, 1, :], ALU.add).then_inc(normed, 1)

            tiles(pool, (add_bias,))

        @block.scalar
        def _(act):
            act.sem_inc(copied, 2)
            act.sem_inc(a1_ready, 2)
            act.sem_inc(z_kept, 4)
            act.activation(warm[:, :], ones[:, 0:1], ACT.Gelu)
            with act.Fori(0, TILES // 2) as i:
                for p in range(2):
                    t = 2 * i + p
                    act.wait_ge(hidden, t + 5)
                    act.wait_ge(measured, t + 3)
                    act.copy(z[:, t, :], ps_a[:, p, :]).then_inc(copied, 1)
            act.wait_ge(var_ready, 1)
            act.activation(work[:, 4, :], work[:, 3, :], ACT.Sqrt).then_inc(std_ready, 1)
            act.activation(warm[:, :], ones[:, 0:1], ACT.Gelu)

            def nonlinear(t, b, u):
                act.wait_ge(normed, t + 1)
                act.activation(row[:, u, :], row[:, u, :], ACT.Gelu).then_inc(gelued, 1)
                act.wait_ge(gelued, t + 1)
                act.copy(z[:, t, :], row[:, u, :]).then_inc(z_kept, 1)

            def first_layer(t, b, u):
                act.wait_ge(a1_summed, t + 3)
                act.wait_ge(weighed, t + 1)
                act.activation(a1[:, u % 2, :], ps_c[:, u % 2, 0:P], ACT.Gelu, bias=b1).then_inc(a1_ready, 1)

            tiles(act, (nonlinear, first_layer))
            act.wait_ge(relay, POOL_SHIFTED)
            act.activation(pool_w[:, :, :], pool_w[:, :, :], ACT.Exp).then_inc(relay, 1)
            act.wait_ge(relay, KG_VAR)
            act.activation(k_work[:, 5:6], k_work[:, 4:5], ACT.Sqrt).then_inc(relay, 1)
            act.wait_ge(relay, KG_NORMED)
            act.activation(k1[:, :], k1[:, :], ACT.Gelu).then_inc(relay, 1)
            act.wait_ge(relay, TAPS_SHIFTED)
            act.activation(taps[:, :, :], taps[:, :, :], ACT.Exp).then_inc(relay, 1)

        @block.vector
        def _(v):
            steps = Steps(v, own)
            v.sem_inc(measured, 2)
            v.sem_inc(weights_kept, 2)
            v.sem_inc(rowT_ready, 2)
            v.wait_ge(loaded, 96)
            with v.Fori(0, TILES // 2) as i:
                for p in range(2):
                    t = 2 * i + p
                    v.wait_ge(hidden, t + 5)
                    v.bn_stats(st[:, t, :], ps_a[:, p, :]).then_inc(measured, 1)
            v.wait_ge(measured, TILES + 2)
            me, mo, se, so = st[:, :, 1], st[:, :, 4], st[:, :, 2], st[:, :, 5]
            v.tensor_tensor(mean[:, :], me, mo, ALU.add)
            v.tensor_tensor(work[:, 0, :], me, mo, ALU.subtract)
            steps.done(v.tensor_tensor(work[:, 1, :], se, so, ALU.add))
            v.tensor_scalar(mean[:, :], mean[:, :], 0.5, None, ALU.mult)
            v.tensor_scalar(work[:, 1, :], work[:, 1, :], 1.0 / C, LN_EPS, ALU.mult, ALU.add)
            steps.done(v.scalar_tensor_tensor(work[:, 2, :], work[:, 0, :], 0.25, work[:, 0, :],
                                              ALU.mult, ALU.mult))
            v.tensor_tensor(work[:, 3, :], work[:, 1, :], work[:, 2, :], ALU.add).then_inc(var_ready, 1)
            v.wait_ge(std_ready, 1)
            steps.done(v.reciprocal(rstd[:, :], work[:, 4, :]))
            v.wait_ge(copied, TILES + 2)
            start = steps.n

            def normalise(t, b, u):
                v.wait_ge(turned, t + 1)
                v.wait_ge(z_kept, t + 1)
                steps.n = start + t
                steps.done(v.tensor_scalar(row[:, u, :], z[:, t, :], mean[:, bass.ds(t, 1)],
                                           rstd[:, bass.ds(t, 1)], ALU.subtract, ALU.mult))
                v.tensor_tensor(row[:, u, :], row[:, u, :], gb[:, 0, :], ALU.mult).then_inc(scaled, 1)

            def copy_turned(t, b, u):
                v.wait_ge(turned, t + 5)
                v.wait_ge(a1_summed, t + 1)
                v.tensor_copy(rowT[:, u % 2, :, :], ps_b[:, u % 2, :].rearrange("p (c n) -> p c n", c=CC))\
                    .then_inc(rowT_ready, 1)

            def keep_weights(t, b, u):
                v.wait_ge(weighed, t + 3)
                v.tensor_scalar(pool_w[0:1, bass.ds(b, 1), (u % 2) * P:(u % 2 + 1) * P],
                                ps_d[0:1, u % 2:u % 2 + 1, 0:P], b2, None, ALU.add).then_inc(weights_kept, 1)

            tiles(v, (normalise, None, copy_turned, keep_weights))
            steps.n = start + TILES
            v.wait_ge(weights_kept, TILES + 2)
            steps.done(v.tensor_reduce(pool_n[:, 0, :], pool_w[:, :, :], X, ALU.max, negate=True))
            v.tensor_tensor(pool_w[:, :, :], pool_w[:, :, :],
                            pool_n[:, 0, :].unsqueeze(2).to_broadcast([1, B, SEQ]), ALU.add).then_inc(relay, 1)
            v.wait_ge(relay, POOL_EXPED)
            steps.done(v.reduce_sum(pool_n[:, 1, :], pool_w[:, :, :], X))
            steps.done(v.reciprocal(pool_n[:, 2, :], pool_n[:, 1, :]))
            v.tensor_tensor(pool_w[:, :, :], pool_w[:, :, :],
                            pool_n[:, 2, :].unsqueeze(2).to_broadcast([1, B, SEQ]), ALU.mult).then_inc(relay, 1)
            v.wait_ge(relay, COLUMNS)
            v.wait_ge(pool_own, 1)
            for b in range(B):
                last = v.tensor_copy(w_cols[:, b * QC:(b + 1) * QC, b:b + 1],
                                     ps_a[:, 0, b * QC:(b + 1) * QC].unsqueeze(2))
            last.then_inc(relay, 1)
            v.wait_ge(relay, POOLED)
            v.tensor_copy(cc[:, :], ps_b[0:B, 0, :]).then_inc(relay, 1)
            v.wait_ge(relay, POOLED_TURNED)
            v.tensor_copy(ccT[:, :, :], ps_c[:, 0, 0:CC * B].rearrange("p (c b) -> p c b", c=CC)).then_inc(relay, 1)
            v.wait_ge(relay, KG_SUMMED)
            steps.done(v.bn_stats(k_st[:, :], ps_d[0:B, 0, 0:D]))
            v.tensor_tensor(k_work[:, 0:1], k_st[:, 1:2], k_st[:, 4:5], ALU.add)
            v.tensor_tensor(k_work[:, 1:2], k_st[:, 1:2], k_st[:, 4:5], ALU.subtract)
            steps.done(v.tensor_tensor(k_work[:, 2:3], k_st[:, 2:3], k_st[:, 5:6], ALU.add))
            v.tensor_scalar(k_work[:, 0:1], k_work[:, 0:1], 0.5, None, ALU.mult)
            v.tensor_scalar(k_work[:, 2:3], k_work[:, 2:3], 1.0 / D, LN_EPS, ALU.mult, ALU.add)
            steps.done(v.scalar_tensor_tensor(k_work[:, 3:4], k_work[:, 1:2], 0.25, k_work[:, 1:2],
                                              ALU.mult, ALU.mult))
            v.tensor_tensor(k_work[:, 4:5], k_work[:, 2:3], k_work[:, 3:4], ALU.add).then_inc(relay, 1)
            v.wait_ge(relay, KG_STD)
            steps.done(v.reciprocal(k_work[:, 6:7], k_work[:, 5:6]))
            steps.done(v.tensor_scalar(k1[:, :], ps_d[0:B, 0, 0:D], k_work[:, 0:1], k_work[:, 6:7],
                                       ALU.subtract, ALU.mult))
            steps.done(v.tensor_tensor(k1[:, :], k1[:, :], kg_gb[0:B, 0, :], ALU.mult))
            v.tensor_tensor(k1[:, :], k1[:, :], kg_gb[0:B, 1, :], ALU.add).then_inc(relay, 1)
            v.wait_ge(relay, KG_TURNED)
            v.tensor_copy(k1T[:, :, :], ps_c[:, 1, 0:DC * B].rearrange("p (c b) -> p c b", c=DC)).then_inc(relay, 1)
            v.wait_ge(relay, TAPS_SUMMED)
            kp = ps_d[0:B, 1, 0:T9].rearrange("b (h t) -> b h t", h=HEADS)
            over_taps = lambda n: taps_n[:, n, :].unsqueeze(2).to_broadcast([B, HEADS, TAPS * TAPS])
            steps.done(v.tensor_reduce(taps_n[:, 0, :], kp, X, ALU.max, negate=True))
            v.tensor_tensor(taps[:, :, :], kp, over_taps(0), ALU.add).then_inc(relay, 1)
            v.wait_ge(relay, TAPS_EXPED)
            steps.done(v.reduce_sum(taps_n[:, 1, :], taps[:, :, :], X))
            steps.done(v.reciprocal(taps_n[:, 2, :], taps_n[:, 1, :]))
            v.tensor_tensor(taps[:, :, :], taps[:, :, :], over_taps(2), ALU.mult).then_inc(relay, 1)
            v.wait_ge(relay, TAPS_SPREAD)
            for n, ps in enumerate((ps_a, ps_b, ps_c)):
                m = min(3, B - 3 * n)
                v.tensor_copy(kernels[:, 3 * n * T9:(3 * n + m) * T9], ps[:, 1, 0:m * T9])



PLAIN, MASKED = range(2)
HALF = HEADS // 2
PIECES = 3
PRODUCTS = ((0, 0), (1, 0), (2, 0), (0, 1), (1, 1), (0, 2))
STACK = len(PRODUCTS) * HD
RUNS = tuple((HD * sum(range(n + 1, PIECES + 1)), n) for n in range(PIECES, 0, -1))
SLOTS = 4
LOOPS = 2 * B // SLOTS
VW = LANE


def split_heads_stage(core, name, mode, xnT, ctxT, w_dram, dst, ident, ident16, ones, piece_rows,
                      mask=None):
    WB = 3 * DC * D
    masking = mode == MASKED
    piece_dmas, stack_dmas = 2, 2 * len(RUNS)

    def at(i, r):
        return i + r // SLOTS, r % SLOTS

    with Stage(core, name) as s:
        w = s.sb("w", [P, WB + 2 * DC + D])
        wq, wk, wv = (w[:, n * DC * D:(n + 1) * DC * D].rearrange("p (c n) -> p c n", c=DC) for n in range(3))
        bv = w[0:1, WB + 2 * DC:]
        ctx = s.sb("ctx", [P, DC, SEQ])
        qk, rest = s.sb("qk", [P, 2, SEQ]), s.sb("rest", [P, 2, SEQ])
        pieces = s.sb("pieces", [P, PIECES, 2, SEQ], BF16)
        stackQ, stackK = (s.sb(n, [P, SLOTS, HALF, SEQ], BF16) for n in ("stackQ", "stackK"))
        vv = s.sb("v", [P, SLOTS, QC, HALF, VW])
        probsT = s.sb("probsT", [P, 4, QC * SEQ])
        negmax, max_rest = s.sb("negmax", [P, HALF * QC]), s.sb("max_rest", [P, HALF * QC])
        max_pieces = s.sb("max_pieces", [P, P], BF16)
        max_rows = s.sb("max_rows", [PIECES * HALF * QC, P], BF16)
        mixedT = s.sb("mixedT", [P, QC * SEQ])
        inv, mixed_sb = s.sb("inv", [P, QC, HALF]), s.sb("mixed_sb", [P, QC, HALF, HD])
        warm = s.sb("warm", [P, 1])
        max_piece = [max_pieces[:, n * HALF * QC:(n + 1) * HALF * QC] for n in range(PIECES)]
        ps_m, ps_e = s.psum("ps_m", [P, 2, 512]), s.psum("ps_e", [P, 2, 512])
        ps_qk, ps_v, ps_o = (s.psum(n, [P, 512]) for n in ("ps_qk", "ps_v", "ps_o"))
        ps_r = s.psum("ps_r", [P, 1024], BF16)
        sp_passed, split_steps = s.sem("sp_passed"), s.sem("split_steps")
        w_loaded, ctx_loaded, constants, written = (
            s.sem(n) for n in ("w_loaded", "ctx_loaded", "constants", "written"))
        projected, v_projected, qk_taken, v_placed = (s.sem(n) for n in
                                                      ("projected", "v_projected", "qk_taken", "v_placed"))
        pieces_ready, scored, maxed, max_split, max_turned, rows_ready = (
            s.sem(n) for n in ("pieces_ready", "scored", "maxed", "max_split", "max_turned", "rows_ready"))
        stacked, max_placed = ([s.sem(f"{n}{r}") for r in range(SLOTS)] for n in ("stacked", "max_placed"))
        scoredT, exped, mixed, mixedT_ready, turned_back, taken, own = (
            s.sem(n) for n in ("scoredT", "exped", "mixed", "mixedT_ready", "turned_back", "taken", "own"))
        if masking:
            mask_in = s.sb("mask_in", [P, 2, QC * SEQ], I32)
            mask_add = s.sb("mask_add", [P, 2, QC * SEQ], BF16)
            mask_loaded, mask_ready, maskT_ready = s.sem("mask_loaded"), s.sem("mask_ready"), s.sem("maskT_ready")
        block = s.block()

        @block.sync
        def _(sp):
            sp.dma_start(w[:, :], w_dram).then_inc(w_loaded, 16)
            sp.dma_start(ctx[:, :, :].rearrange("p c n -> p (c n)"), ctxT[0:P, :]).then_inc(ctx_loaded, 16)
            if masking:
                sp.dma_start(mask_in[:, :, :].rearrange("p a n -> p (a n)"), mask[0:P, :]).then_inc(mask_loaded, 16)

            def passed():
                sp.sem_inc(sp_passed, 1)

            def put_pieces(i, r):
                u = SLOTS * i + r
                if not (isinstance(i, int) and u < 2):
                    sp.wait_ge(stacked[(r - 2) % SLOTS], 16 * stack_dmas * (i + (r - 2) // SLOTS + 1))
                    passed()
                sp.wait_ge(pieces_ready, u + 1)
                for side in range(2):
                    sp.dma_start(piece_rows[r % 2, side].rearrange("a d j n -> (d j) a n"),
                                 pieces[:, :, side, :]).then_inc(written, 16)

            def stack(i, r):
                u = SLOTS * i + r
                sp.wait_ge(written, 16 * piece_dmas * (u + 1))
                passed()
                sp.wait_ge(mixed, u + 1)
                for row, count in RUNS:
                    sp.dma_start(stackQ[row:row + count * HD, r, :, :].rearrange("r j n -> r (j n)"),
                                 piece_rows[r % 2, 0, 0:count].rearrange("a d j n -> (a d) (j n)"))\
                        .then_inc(stacked[r], 16)
                    same = piece_rows[r % 2, 1, PIECES - count].rearrange("d j n -> d (j n)").unsqueeze(0)
                    sp.dma_start(stackK[row:row + count * HD, r, :, :].rearrange("r j n -> r (j n)"),
                                 same.to_broadcast([count, HD, HALF * SEQ])).then_inc(stacked[r], 16)

            def context(b):
                sp.wait_ge(v_projected, 2 * b)
                passed()
                sp.dma_start(ctx[:, :, :].rearrange("p c n -> p (c n)"), ctxT[dyn(b), :]).then_inc(ctx_loaded, 16)

            def sequence(i, r, more):
                b = 2 * i + r // 2
                stack(*at(i, r - 1))
                put_pieces(i, r)
                stack(i, r)
                if masking:
                    sp.wait_ge(maskT_ready, b)
                    passed()
                    sp.dma_start(mask_in[:, :, :].rearrange("p a n -> p (a n)"), mask[dyn(b), :])\
                        .then_inc(mask_loaded, 16)
                if more:
                    context(b + 1)
                put_pieces(i, r + 1)

            put_pieces(0, 0)
            stack(0, 0)
            context(1)
            put_pieces(0, 1)
            sequence(0, 2, True)
            with sp.Fori(1, LOOPS - 1) as i:
                sequence(i, 0, True)
                sequence(i, 2, True)
            sequence(LOOPS - 1, 0, True)
            sequence(LOOPS - 1, 2, False)
            stack(LOOPS - 1, SLOTS - 1)

        @block.gpsimd
        def _(pool):
            pool.memset(vv[:, :, :, :, HD + 1:VW], 0.0)
            pool.memset(vv[:, :, :, :, HD:HD + 1], 1.0)
            pool.memset(max_pieces[:, PIECES * HALF * QC:], 0.0).then_inc(constants, 1)

        @block.tensor
        def _(pe):
            pe.sem_inc(mixed, SLOTS)
            pe.wait_ge(w_loaded, 16)

            def project_query(i, r):
                b, p = 2 * i + r // 2, r % 2
                pe.wait_ge(ctx_loaded, 16 * (b + 1))
                pe.wait_ge(qk_taken, SLOTS * i + r + 1)
                for c in range(DC):
                    pe.matmul(ps_qk[:, 0:SEQ], wq[:, c, p * P:(p + 1) * P], xnT[:, c, dyn(b, SEQ)],
                              start=(c == 0), stop=(c == DC - 1))

            def project_key_value(i, r):
                p = r % 2
                for c in range(DC):
                    last = pe.matmul(ps_qk[:, SEQ:2 * SEQ], wk[:, c, p * P:(p + 1) * P], ctx[:, c, :],
                                     start=(c == 0), stop=(c == DC - 1))
                last.then_inc(projected, 1)
                pe.wait_ge(v_placed, SLOTS * i + r + 1)
                for tc in range(QC):
                    out = ps_v[:, tc * P:(tc + 1) * P]
                    for c in range(DC):
                        pe.matmul(out, ctx[:, c, tc * P:(tc + 1) * P], wv[:, c, p * P:(p + 1) * P],
                                  start=(c == 0), stop=False)
                    last = pe.matmul(out, ones[0:1, 0:P], bv[:, p * P:(p + 1) * P], start=False, stop=True)
                last.then_inc(v_projected, 1)

            def score(i, r, h):
                out = ps_m[:, h % 2, :]
                if h == 0:
                    pe.wait_ge(stacked[r], 16 * stack_dmas * (i + 1))
                    if masking:
                        pe.wait_ge(mask_ready, 2 * i + r // 2 + 1)
                pe.wait_ge(maxed, HALF * (SLOTS * i + r) + h + 1)
                if masking:
                    pe.matmul(out, ident16[:, :], mask_add[:, 0, :], start=True, stop=False, skip_group_check=True)
                for qc in range(QC):
                    last = pe.matmul(out[:, qc * SEQ:(qc + 1) * SEQ], stackQ[0:STACK, r, h, qc * P:(qc + 1) * P],
                                     stackK[0:STACK, r, h, :], start=not masking,
                                     stop=(qc == QC - 1 or not masking), skip_group_check=True)
                last.then_inc(scored, 1)

            def turn_max(i, r):
                pe.wait_ge(max_split, SLOTS * i + r + 1)
                pe.transpose(ps_r[:, 0:P], max_pieces[:, :], ident16[:, :]).then_inc(max_turned, 1)

            def scoreT(i, r, h):
                out = ps_e[:, h % 2, :]
                pe.wait_ge(exped, HALF * (SLOTS * i + r) + h + 1)
                rows = STACK + PIECES
                if masking:
                    pe.matmul(out, ident16[:, :], mask_add[:, 1, :], start=True, stop=False, skip_group_check=True)
                for kc in range(QC):
                    last = pe.matmul(out[:, kc * SEQ:(kc + 1) * SEQ], stackK[0:rows, r, h, kc * P:(kc + 1) * P],
                                     stackQ[0:rows, r, h, :], start=not masking,
                                     stop=(kc == QC - 1 or not masking), skip_group_check=True)
                last.then_inc(scoredT, 1)

            def mix(i, r, h):
                pe.wait_ge(exped, HALF * (SLOTS * i + r) + h + 3)
                out = ps_o[LANE * (h % GH):LANE * (h % GH) + VW, h // GH * SEQ:(h // GH + 1) * SEQ]
                for kc in range(QC):
                    last = pe.matmul(out, vv[:, r, kc, h, :], probsT[:, h % 4, kc * SEQ:(kc + 1) * SEQ],
                                     start=(kc == 0), stop=(kc == QC - 1), skip_group_check=True)
                if h == HALF - 1:
                    last.then_inc(mixed, 1)

            def turn_back(i, r):
                pe.wait_ge(mixedT_ready, SLOTS * i + r + 1)
                for n in range(2 * QC):
                    last = pe.transpose(ps_o[:, n * P:(n + 1) * P], mixedT[:, n * P:(n + 1) * P], ident[:, :])
                last.then_inc(turned_back, 1)

            def turn(i, r, projects, maxes):
                if maxes:
                    for h in range(2):
                        score(*at(i, r + 1), h)
                pe.wait_ge(max_placed[r], 16 * PIECES * (i + 1))
                pe.wait_ge(taken, SLOTS * i + r + 1)
                if masking:
                    pe.wait_ge(maskT_ready, 2 * i + r // 2 + 1)
                for h in range(HALF + 2):
                    if h < HALF:
                        scoreT(i, r, h)
                    if h >= 2:
                        mix(i, r, h - 2)
                    if maxes and h + 2 < HALF:
                        score(*at(i, r + 1), h + 2)
                if projects:
                    project_query(*at(i, r + 4))
                if maxes:
                    turn_max(*at(i, r + 1))
                turn_back(i, r)
                if projects:
                    project_key_value(*at(i, r + 4))

            for r in range(3):
                project_query(0, r)
                project_key_value(0, r)
            pe.wait_ge(constants, 2)
            for h in range(HALF):
                score(0, 0, h)
            project_query(0, 3)
            turn_max(0, 0)
            project_key_value(0, 3)
            with pe.Fori(0, LOOPS - 1) as i:
                for r in range(SLOTS):
                    turn(i, r, True, True)
            for r in range(SLOTS):
                turn(LOOPS - 1, r, False, r + 1 < SLOTS)

        @block.scalar
        def _(act):
            act.sem_inc(exped, 2)
            act.sem_inc(v_placed, 1)
            act.activation(warm[:, :], ones[:, 0:1], ACT.Exp)
            act.wait_ge(constants, 2)

            def place_values(i, r):
                act.wait_ge(v_projected, SLOTS * i + r + 1)
                act.wait_ge(mixed, SLOTS * i + r + 1)
                for tc in range(QC):
                    last = act.copy(vv[:, r, tc, :, 0:HD],
                                    ps_v[:, tc * P:(tc + 1) * P].rearrange("p (j d) -> p j d", d=HD))
                last.then_inc(v_placed, 1)

            def place_max(i, r):
                u = SLOTS * i + r
                act.wait_ge(max_turned, u + 1)
                act.copy(max_rows[:, :], ps_r[0:PIECES * HALF * QC, 0:P]).then_inc(rows_ready, 1)
                act.wait_ge(rows_ready, u + 1)
                for n in range(PIECES):
                    act.dma_start(stackQ[STACK + n:STACK + n + 1, r, :, :].rearrange("a j (q n) -> a (j q) n", q=QC),
                                  max_rows[n * HALF * QC:(n + 1) * HALF * QC, :])\
                        .then_inc(max_placed[r], 16)

            def turn(i, r, projects, maxes):
                u = SLOTS * i + r
                for h in range(HALF):
                    act.wait_ge(scoredT, HALF * u + h + 1)
                    act.activation(probsT[:, h % 4, :], ps_e[:, h % 2, :], ACT.Exp).then_inc(exped, 1)
                act.wait_ge(mixed, u + 1 + SLOTS)
                act.copy(mixedT[:, :], ps_o[:, :]).then_inc(mixedT_ready, 1)
                if maxes:
                    place_max(*at(i, r + 1))
                if projects:
                    place_values(*at(i, r + 4))

            for r in range(3):
                place_values(0, r)
            place_max(0, 0)
            place_values(0, 3)
            with act.Fori(0, LOOPS - 1) as i:
                for r in range(SLOTS):
                    turn(i, r, True, True)
            for r in range(SLOTS):
                turn(LOOPS - 1, r, False, r + 1 < SLOTS)

        @block.vector
        def _(v):
            steps = Steps(v, own)
            v.memset(stackK[STACK:STACK + PIECES, :, :, :], 1.0).then_inc(constants, 1)
            v.sem_inc(maxed, 2)
            v.sem_inc(qk_taken, 1)
            v.sem_inc(taken, 1)
            v.wait_ge(w_loaded, 16)

            def split(i, r, part):
                u, p = SLOTS * i + r, r % 2
                flat = lambda t: t.rearrange("p a n -> p (a n)")
                if part == 0:
                    v.wait_ge(projected, u + 1)
                    v.tensor_scalar(qk[:, 0, :], ps_qk[:, 0:SEQ], w[:, WB + p:WB + p + 1], HD ** -0.5,
                                    ALU.add, ALU.mult)
                    v.tensor_scalar(qk[:, 1, :], ps_qk[:, SEQ:], w[:, WB + DC + p:WB + DC + p + 1], None,
                                    ALU.add).then_inc(qk_taken, 1)
                elif part == 1:
                    v.wait_ge(qk_taken, u + 2)
                    if not (isinstance(i, int) and u == 0):
                        v.wait_ge(written, 16 * piece_dmas * u)
                    v.tensor_copy(flat(pieces[:, 0, :, :]), flat(qk[:, :, :])).then_inc(split_steps, 1)
                elif part == 2:
                    v.wait_ge(split_steps, 3 * u + 1)
                    v.tensor_tensor(flat(rest[:, :, :]), flat(qk[:, :, :]), flat(pieces[:, 0, :, :]), ALU.subtract)\
                        .then_inc(split_steps, 1)
                elif part == 3:
                    v.wait_ge(split_steps, 3 * u + 2)
                    v.tensor_copy(flat(pieces[:, 1, :, :]), flat(rest[:, :, :])).then_inc(split_steps, 1)
                elif part == 4:
                    v.wait_ge(split_steps, 3 * u + 3)
                    v.tensor_tensor(flat(pieces[:, 2, :, :]), flat(rest[:, :, :]), flat(pieces[:, 1, :, :]),
                                    ALU.subtract).then_inc(pieces_ready, 1)

            def make_mask(which, ready):
                v.tensor_scalar(mask_add[:, which, :], mask_in[:, which, :], 0.0, NEG_BIG, ALU.is_equal, ALU.mult)\
                    .then_inc(ready, 1)

            def row_max(i, r, h):
                v.wait_ge(scored, HALF * (SLOTS * i + r) + h + 1)
                v.tensor_reduce(negmax[:, QC * h:QC * (h + 1)],
                                ps_m[:, h % 2, :].rearrange("p (k n) -> p k n", k=QC), X,
                                ALU.max, negate=True).then_inc(maxed, 1)

            def split_max(i, r):
                v.wait_ge(maxed, HALF * (SLOTS * i + r + 1) + 2)
                steps.done(v.tensor_copy(max_piece[0], negmax[:, :]))
                steps.done(v.tensor_tensor(max_rest[:, :], negmax[:, :], max_piece[0], ALU.subtract))
                steps.done(v.tensor_copy(max_piece[1], max_rest[:, :]))
                v.tensor_tensor(max_piece[2], max_rest[:, :], max_piece[1], ALU.subtract).then_inc(max_split, 1)

            def finish(i, r):
                u, p, b = SLOTS * i + r, r % 2, 2 * i + r // 2
                v.wait_ge(turned_back, u + 1)
                for n in range(2):
                    out = ps_o[:, n * SEQ:(n + 1) * SEQ].rearrange("p (q j d) -> p q j d", q=QC, j=GH)
                    last = v.reciprocal(inv[:, :, n * GH:(n + 1) * GH], out[:, :, :, HD])
                steps.done(last)
                for n in range(2):
                    out = ps_o[:, n * SEQ:(n + 1) * SEQ].rearrange("p (q j d) -> p q j d", q=QC, j=GH)
                    last = v.tensor_tensor(mixed_sb[:, :, n * GH:(n + 1) * GH, :], out[:, :, :, 0:HD],
                                           inv[:, :, n * GH:(n + 1) * GH].unsqueeze(3).to_broadcast([P, QC, GH, HD]),
                                           ALU.mult)
                last.then_inc(taken, 1)
                v.wait_ge(taken, u + 2)
                to = dst[:, dyn(b, QC), p * P:(p + 1) * P]
                got = mixed_sb[:, :, :, :].rearrange("p q j d -> p q (j d)")
                if masking:
                    v.tensor_tensor(to, to, got, ALU.add)
                else:
                    v.tensor_copy(to, got)

            def turn(i, r, projects, maxes):
                more_masks = masking and not (isinstance(i, int) and r >= 2)
                for h in range(HALF):
                    if maxes:
                        row_max(*at(i, r + 1), h)
                    if projects and h > 0:
                        split(*at(i, r + 3), h - 1)
                if maxes:
                    split_max(*at(i, r + 1))
                if more_masks and r % 2 == 0:
                    v.wait_ge(mask_loaded, 16 * (2 * i + r // 2 + 2))
                    make_mask(0, mask_ready)
                finish(i, r)
                if more_masks and r % 2 == 1:
                    make_mask(1, maskT_ready)

            if masking:
                v.wait_ge(mask_loaded, 16)
                make_mask(0, mask_ready)
                make_mask(1, maskT_ready)
            for r in range(3):
                for part in range(5):
                    split(0, r, part)
            for h in range(HALF):
                row_max(0, 0, h)
            split_max(0, 0)
            first, per_loop = steps.n, SLOTS * (3 + 1)
            with v.Fori(0, LOOPS - 1) as i:
                steps.n = first + per_loop * i
                for r in range(SLOTS):
                    turn(i, r, True, True)
            steps.n = first + per_loop * (LOOPS - 1)
            for r in range(SLOTS):
                turn(LOOPS - 1, r, r + 3 < SLOTS, r + 1 < SLOTS)



def conv_heads_stage(core, name, xnT, w_dram, dst, ident, ident16, ones, mask, kernels, piece_rows):
    WB = 3 * DC * D
    ALL = SLOTS * HALF
    piece_dmas, stack_dmas = 2, 2 * len(RUNS)

    def at(i, r):
        return i + r // SLOTS, r % SLOTS

    with Stage(core, name) as s:
        w = s.sb("w", [P, WB + 2 * DC + D])
        wq, wk, wv = (w[:, n * DC * D:(n + 1) * DC * D].rearrange("p (c n) -> p c n", c=DC) for n in range(3))
        bv = w[0:1, WB + 2 * DC:]
        ctx = s.sb("ctx", [P, DC, SEQ])
        qk, rest = s.sb("qk", [P, 2, SEQ]), s.sb("rest", [P, 2, SEQ])
        pieces = s.sb("pieces", [P, PIECES, 2, SEQ], BF16)
        stackQ, stackK = (s.sb(n, [STACK, SLOTS, HALF, SEQ], BF16) for n in ("stackQ", "stackK"))
        vv = s.sb("v", [P, SLOTS, QC, HALF * HD])
        mask_in = s.sb("mask_in", [P, 2, QC * SEQ], U8)
        keepT, mask_add = s.sb("keepT", [P, QC, SEQ]), s.sb("mask_add", [P, QC * SEQ], BF16)
        shifts, band = s.sb("shifts", [P, TAPS, P + 2]), s.sb("band", [P, 2, TAPS, P + 2])
        taps = s.sb("taps", [P, 2, HALF, TAPS * TAPS])
        sT = s.sb("sT", [P, 2, QC, SEQ + 2])
        probs, probsT = s.sb("probs", [P, 2, QC, SEQ]), s.sb("probsT", [P, 2, QC, SEQ])
        negmax = s.sb("negmax", [P, 2, QC])
        total, inv = s.sb("total", [P, 2, HALF, QC]), s.sb("inv", [P, HALF, QC])
        mixed_sb = s.sb("mixed_sb", [P, QC, HALF, HD])
        warm = s.sb("warm", [P, 1])
        ps_s, ps_c, ps_t = (s.psum(n, [P, 2, 512]) for n in ("ps_s", "ps_c", "ps_t"))
        ps_p, ps_o = s.psum("ps_p", [P, 512]), s.psum("ps_o", [P, 512])
        sp_passed, split_steps, w_loaded, ctx_loaded, written = (
            s.sem(n) for n in ("sp_passed", "split_steps", "w_loaded", "ctx_loaded", "written"))
        projected, v_projected, qk_taken, v_placed, pieces_ready = (
            s.sem(n) for n in ("projected", "v_projected", "qk_taken", "v_placed", "pieces_ready"))
        masks_loaded, masks_ready, shifts_ready, taps_ready = (
            s.sem(n) for n in ("masks_loaded", "masks_ready", "shifts_ready", "taps_ready"))
        scored, masked, band_free, band_begun, band_ready, convolved = (
            s.sem(n) for n in ("scored", "masked", "band_free", "band_begun", "band_ready", "convolved"))
        maxed, exped, turned, probsT_ready, mixed, taken, own = (
            s.sem(n) for n in ("maxed", "exped", "turned", "probsT_ready", "mixed", "taken", "own"))
        stacked = [s.sem(f"stacked{r}") for r in range(SLOTS)]
        block = s.block()

        def heads(i, r, lags):
            for h in range(HALF):
                for lag, step in lags:
                    H = HALF * r + h - lag
                    if not (isinstance(i, int) and ALL * i + H < 0):
                        step(i + H // ALL, H % ALL)
                yield h

        @block.sync
        def _(sp):
            sp.dma_start(w[:, :], w_dram).then_inc(w_loaded, 16)
            sp.dma_start(ctx[:, :, :], xnT[:, :, 0:SEQ]).then_inc(ctx_loaded, 16)
            sp.dma_start(mask_in[:, :, :], mask.rearrange("p (a n) -> p a n", a=2)).then_inc(masks_loaded, 16)

            def passed():
                sp.sem_inc(sp_passed, 1)

            def put_pieces(i, r):
                u = SLOTS * i + r
                if not (isinstance(i, int) and u < 2):
                    sp.wait_ge(stacked[(r - 2) % SLOTS], 16 * stack_dmas * (i + (r - 2) // SLOTS + 1))
                    passed()
                sp.wait_ge(pieces_ready, u + 1)
                for side in range(2):
                    sp.dma_start(piece_rows[r % 2, side].rearrange("a d j n -> (d j) a n"),
                                 pieces[:, :, side, :]).then_inc(written, 16)

            def stack(i, r):
                u = SLOTS * i + r
                sp.wait_ge(written, 16 * piece_dmas * (u + 1))
                passed()
                if not (isinstance(i, int) and u < SLOTS):
                    sp.wait_ge(mixed, HALF * (u - SLOTS + 1) + 2)
                for row, count in RUNS:
                    sp.dma_start(stackQ[row:row + count * HD, r, :, :].rearrange("r j n -> r (j n)"),
                                 piece_rows[r % 2, 0, 0:count].rearrange("a d j n -> (a d) (j n)"))\
                        .then_inc(stacked[r], 16)
                    same = piece_rows[r % 2, 1, PIECES - count].rearrange("d j n -> d (j n)").unsqueeze(0)
                    sp.dma_start(stackK[row:row + count * HD, r, :, :].rearrange("r j n -> r (j n)"),
                                 same.to_broadcast([count, HD, HALF * SEQ])).then_inc(stacked[r], 16)

            def context(b):
                sp.wait_ge(v_projected, 2 * b)
                passed()
                sp.dma_start(ctx[:, :, :], xnT[:, :, dyn(b, SEQ)]).then_inc(ctx_loaded, 16)

            def sequence(i, r, more):
                stack(*at(i, r - 1))
                put_pieces(i, r)
                stack(i, r)
                if more:
                    context(2 * i + r // 2 + 1)
                put_pieces(i, r + 1)

            put_pieces(0, 0)
            stack(0, 0)
            context(1)
            put_pieces(0, 1)
            sequence(0, 2, True)
            with sp.Fori(1, LOOPS - 1) as i:
                sequence(i, 0, True)
                sequence(i, 2, True)
            sequence(LOOPS - 1, 0, True)
            sequence(LOOPS - 1, 2, False)
            stack(LOOPS - 1, SLOTS - 1)

        @block.tensor
        def _(pe):
            for credit in (turned, mixed, convolved):
                pe.sem_inc(credit, 2)
            pe.wait_ge(w_loaded, 16)

            def project_query_key(i, r):
                b, p = 2 * i + r // 2, r % 2
                pe.wait_ge(v_placed, SLOTS * i + r + 1)
                for n, weights in enumerate((wq, wk)):
                    for c in range(DC):
                        last = pe.matmul(ps_p[:, n * SEQ:(n + 1) * SEQ], weights[:, c, p * P:(p + 1) * P],
                                         xnT[:, c, dyn(b, SEQ)], start=(c == 0), stop=(c == DC - 1))
                last.then_inc(projected, 1)

            def project_value(i, r):
                b, p = 2 * i + r // 2, r % 2
                pe.wait_ge(ctx_loaded, 16 * (b + 1))
                pe.wait_ge(qk_taken, SLOTS * i + r + 1)
                for tc in range(QC):
                    out = ps_p[:, tc * P:(tc + 1) * P]
                    for c in range(DC):
                        pe.matmul(out, ctx[:, c, tc * P:(tc + 1) * P], wv[:, c, p * P:(p + 1) * P],
                                  start=(c == 0), stop=False)
                    last = pe.matmul(out, ones[0:1, 0:P], bv[:, p * P:(p + 1) * P], start=False, stop=True)
                last.then_inc(v_projected, 1)

            def score(i, H):
                r, h, n = H // HALF, H % HALF, ALL * i + H
                if h == 0:
                    pe.wait_ge(stacked[r], 16 * stack_dmas * (i + 1))
                pe.wait_ge(masked, n + 1)
                for kc in range(QC):
                    last = pe.matmul(ps_s[:, h % 2, kc * SEQ:(kc + 1) * SEQ], stackK[:, r, h, kc * P:(kc + 1) * P],
                                     stackQ[:, r, h, :], start=True, stop=True)
                last.then_inc(scored, 1)

            def convolve(i, H):
                h, n = H % HALF, ALL * i + H
                out = ps_c[:, h % 2, :]
                pe.wait_ge(exped, n + 1)
                pe.matmul(out, ident16[:, :], mask_add[:, :], start=True, stop=False, skip_group_check=True)
                pe.wait_ge(masked, n + 3)
                pe.wait_ge(band_ready, n + 1)
                for qc in range(QC):
                    for kc in range(QC):
                        k0, k1 = max(kc * P - 1, 0), min(kc * P + P + 1, SEQ)
                        w0 = k0 - (kc * P - 1)
                        for dq in range(TAPS):
                            last = pe.matmul(out[:, qc * SEQ + k0:qc * SEQ + k1],
                                             sT[:, h % 2, kc, qc * P + dq:qc * P + dq + P],
                                             band[:, h % 2, dq, w0:w0 + k1 - k0], start=False,
                                             stop=(qc == kc == QC - 1 and dq == TAPS - 1), skip_group_check=True)
                last.then_inc(convolved, 1)

            def turn(i, H):
                h, n = H % HALF, ALL * i + H
                pe.wait_ge(exped, n + 3)
                pe.wait_ge(probsT_ready, n + 1)
                for kc in range(QC):
                    for qc in range(QC):
                        last = pe.transpose(ps_t[:, h % 2, kc * SEQ + qc * P:kc * SEQ + (qc + 1) * P],
                                            probs[:, h % 2, qc, kc * P:(kc + 1) * P], ident[:, :])
                last.then_inc(turned, 1)

            def mix(i, H):
                r, h, n = H // HALF, H % HALF, ALL * i + H
                pe.wait_ge(probsT_ready, n + 3)
                if h == 0:
                    pe.wait_ge(taken, SLOTS * i + r + 1)
                for qc in range(QC):
                    for kc in range(QC):
                        last = pe.matmul(ps_o[:, (qc * HALF + h) * HD:(qc * HALF + h + 1) * HD],
                                         probsT[:, h % 2, kc, qc * P:(qc + 1) * P],
                                         vv[:, r, kc, h * HD:(h + 1) * HD],
                                         start=(kc == 0), stop=(kc == QC - 1), skip_group_check=True)
                last.then_inc(mixed, 1)

            def loop(i, projections):
                for r in range(SLOTS):
                    for h in heads(i, r, ((0, score), (1, convolve), (2, turn), (3, mix))):
                        if h == 1 and r < projections:
                            project_query_key(*at(i, r + 3))
                        if h == 3 and r < projections:
                            project_value(*at(i, r + 3))

            for r in range(3):
                project_query_key(0, r)
                project_value(0, r)
            pe.wait_ge(masks_ready, 1)
            loop(0, SLOTS)
            with pe.Fori(1, LOOPS - 1) as i:
                loop(i, SLOTS)
            loop(LOOPS - 1, 1)
            last = ALL - 1
            convolve(LOOPS - 1, last)
            turn(LOOPS - 1, last - 1)
            mix(LOOPS - 1, last - 2)
            turn(LOOPS - 1, last)
            mix(LOOPS - 1, last - 1)
            mix(LOOPS - 1, last)

        @block.scalar
        def _(act):
            act.sem_inc(exped, 2)
            act.sem_inc(probsT_ready, 2)
            act.sem_inc(v_placed, 1)
            act.activation(warm[:, :], ones[:, 0:1], ACT.Exp)

            def place_values(i, r):
                u = SLOTS * i + r
                act.wait_ge(v_projected, u + 1)
                if not (isinstance(i, int) and u < SLOTS):
                    act.wait_ge(mixed, HALF * (u - SLOTS + 1) + 2)
                act.copy(vv[:, r, :, :], ps_p[:, 0:QC * P].rearrange("p (t n) -> p t n", t=QC)).then_inc(v_placed, 1)

            def exponential(i, H):
                r, h, n = H // HALF, H % HALF, ALL * i + H
                act.wait_ge(maxed, n + 1)
                act.wait_ge(turned, n + 1)
                for qc in range(QC):
                    last = act.activation(probs[:, h % 2, qc, :], ps_c[:, h % 2, qc * SEQ:(qc + 1) * SEQ], ACT.Exp,
                                          bias=negmax[:, h % 2, qc:qc + 1], accum_out=total[:, r % 2, h, qc:qc + 1])
                last.then_inc(exped, 1)

            def copy_turned(i, H):
                h, n = H % HALF, ALL * i + H
                act.wait_ge(turned, n + 3)
                act.wait_ge(mixed, n + 1)
                act.copy(probsT[:, h % 2, :, :], ps_t[:, h % 2, :].rearrange("p (k n) -> p k n", k=QC))\
                    .then_inc(probsT_ready, 1)

            def loop(i, projections):
                for r in range(SLOTS):
                    for h in heads(i, r, ((0, exponential), (1, copy_turned))):
                        if h == 3 and r < projections:
                            place_values(*at(i, r + 3))

            for r in range(3):
                place_values(0, r)
            loop(0, SLOTS)
            with act.Fori(1, LOOPS - 1) as i:
                loop(i, SLOTS)
            loop(LOOPS - 1, 1)
            copy_turned(LOOPS - 1, ALL - 1)

        @block.gpsimd
        def _(pool):
            pool.memset(sT[:, :, :, :], 0.0)
            pool.memset(shifts[:, :, :], 0.0).then_inc(shifts_ready, 1)
            pool.wait_ge(shifts_ready, 1)
            for d in range(TAPS):
                last = pool.affine_select(out=shifts[:, d, :], in_=shifts[:, d, :], compare_op=ALU.not_equal,
                                          fill=1.0, base=d - 2, pattern=[[1, P + 2]], channel_multiplier=-1)
            last.then_inc(shifts_ready, 1)
            pool.wait_ge(shifts_ready, 2)
            with pool.Fori(0, LOOPS) as i:
                for r in range(SLOTS):
                    u = SLOTS * i + r
                    pool.wait_ge(convolved, HALF * u + 1)
                    pool.sem_inc(band_free, 1)
                    pool.tensor_copy(taps[:, r % 2, :, :].rearrange("p j t -> p (j t)"),
                                     kernels[:, dyn(u, HALF * TAPS * TAPS)]).then_inc(taps_ready, 1)
                    pool.wait_ge(taps_ready, u + 1)
                    for h in range(HALF):
                        pool.wait_ge(convolved, HALF * u + h + 1)
                        pool.sem_inc(band_free, 1)
                        for dq in range(TAPS):
                            last = pool.tensor_scalar(band[:, h % 2, dq, :], shifts[:, 0, :],
                                                      taps[:, r % 2, h, dq * TAPS:dq * TAPS + 1], None, ALU.mult)
                        last.then_inc(band_begun, 1)

        @block.vector
        def _(v):
            steps = Steps(v, own)
            v.sem_inc(masked, 2)
            v.sem_inc(taken, 1)
            v.wait_ge(masks_loaded, 16)
            v.tensor_scalar(keepT[:, :, :].rearrange("p k n -> p (k n)"), mask_in[:, 1, :], -1.0, 1.0,
                            ALU.mult, ALU.add).then_inc(own, 1)
            v.tensor_scalar(mask_add[:, :], mask_in[:, 0, :], NEG_BIG, None, ALU.mult).then_inc(masks_ready, 1)
            v.wait_ge(own, 1)
            v.wait_ge(w_loaded, 16)
            v.wait_ge(shifts_ready, 1)
            steps.n = 1

            def split(i, r, part):
                u, p = SLOTS * i + r, r % 2
                flat = lambda t: t.rearrange("p a n -> p (a n)")
                if part == 0:
                    v.wait_ge(projected, u + 1)
                    v.tensor_scalar(qk[:, 0, :], ps_p[:, 0:SEQ], w[:, WB + p:WB + p + 1], HD ** -0.5,
                                    ALU.add, ALU.mult)
                    v.tensor_scalar(qk[:, 1, :], ps_p[:, SEQ:], w[:, WB + DC + p:WB + DC + p + 1], None,
                                    ALU.add).then_inc(qk_taken, 1)
                elif part == 1:
                    v.wait_ge(qk_taken, u + 1)
                    if not (isinstance(i, int) and u == 0):
                        v.wait_ge(written, 16 * piece_dmas * u)
                    v.tensor_copy(flat(pieces[:, 0, :, :]), flat(qk[:, :, :])).then_inc(split_steps, 1)
                elif part == 2:
                    v.wait_ge(split_steps, 3 * u + 1)
                    v.tensor_tensor(flat(rest[:, :, :]), flat(qk[:, :, :]), flat(pieces[:, 0, :, :]), ALU.subtract)\
                        .then_inc(split_steps, 1)
                elif part == 3:
                    v.wait_ge(split_steps, 3 * u + 2)
                    v.tensor_copy(flat(pieces[:, 1, :, :]), flat(rest[:, :, :])).then_inc(split_steps, 1)
                elif part == 4:
                    v.wait_ge(split_steps, 3 * u + 3)
                    v.tensor_tensor(flat(pieces[:, 2, :, :]), flat(rest[:, :, :]), flat(pieces[:, 1, :, :]),
                                    ALU.subtract).then_inc(pieces_ready, 1)

            def drop_masked(i, H):
                h, n = H % HALF, ALL * i + H
                v.wait_ge(scored, n + 1)
                v.wait_ge(convolved, n + 1)
                v.tensor_tensor(sT[:, h % 2, :, 1:SEQ + 1], ps_s[:, h % 2, :].rearrange("p (k n) -> p k n", k=QC),
                                keepT[:, :, :], ALU.mult).then_inc(masked, 1)
                if h == 3 and not (isinstance(i, int) and n < HALF):
                    finish(i + (H // HALF - 1) // SLOTS, (H // HALF - 1) % SLOTS)

            def widen_band(i, H):
                r, h, n = H // HALF, H % HALF, ALL * i + H
                v.wait_ge(band_begun, n + 1)
                for d in range(1, TAPS):
                    for dq in range(TAPS):
                        out, tap = band[:, h % 2, dq, :], dq * TAPS + d
                        last = v.scalar_tensor_tensor(out, shifts[:, d, :], taps[:, r % 2, h, tap:tap + 1], out,
                                                      ALU.mult, ALU.add)
                    if d < TAPS - 1:
                        steps.done(last)
                last.then_inc(band_ready, 1)

            def row_max(i, H):
                h, n = H % HALF, ALL * i + H
                v.wait_ge(convolved, n + 3)
                v.tensor_reduce(negmax[:, h % 2, :], ps_c[:, h % 2, :].rearrange("p (k n) -> p k n", k=QC), X,
                                ALU.max, negate=True).then_inc(maxed, 1)

            def finish(i, r):
                u, p, b = SLOTS * i + r, r % 2, 2 * i + r // 2
                v.wait_ge(mixed, HALF * (u + 1) + 2)
                steps.done(v.reciprocal(inv[:, :, :], total[:, p, :, :]))
                factor = inv[:, :, :].rearrange("p j q -> p q j").unsqueeze(3).to_broadcast([P, QC, HALF, HD])
                steps.done(v.tensor_tensor(mixed_sb[:, :, :, :],
                                           ps_o[:, 0:QC * P].rearrange("p (q j d) -> p q j d", q=QC, j=HALF),
                                           factor, ALU.mult))
                v.tensor_copy(dst[:, dyn(b, QC), p * P:(p + 1) * P],
                              mixed_sb[:, :, :, :].rearrange("p q j d -> p q (j d)")).then_inc(taken, 1)

            def loop(i, projections):
                for r in range(SLOTS):
                    for h in heads(i, r, ((0, drop_masked), (0, widen_band), (1, row_max))):
                        if r < projections and h in (2, 4, 5, 6, 7):
                            split(*at(i, r + 3), (2, 4, 5, 6, 7).index(h))

            for r in range(3):
                for part in range(5):
                    split(0, r, part)
            loop(0, SLOTS)
            first, per_loop = steps.n, ALL + 2 * SLOTS
            with v.Fori(1, LOOPS - 1) as i:
                steps.n = first + per_loop * (i - 1)
                loop(i, SLOTS)
            steps.n = first + per_loop * (LOOPS - 2)
            loop(LOOPS - 1, 1)
            row_max(LOOPS - 1, ALL - 1)
            finish(LOOPS - 1, SLOTS - 1)





def build(nc, ins, outs, stages=99):
    i = ins
    with ExitStack() as whole:
        core = Core(nc, whole)
        x = core.keep("x", [P, TILES, D])
        xn = core.keep("xn", [P, TILES, D])
        xnT = core.keep("xnT", [P, DC, TILES * P])
        ident = core.keep("ident", [P, P])
        ones = core.keep("ones", [P, P])
        ident16 = core.keep("ident16", [P, P], BF16)
        logits = core.keep("logits", [P, TILES, 64])
        tb = Tables(core, MOST_TILES)
        xn_dram = nc.dram_tensor("xn_rows", (TILES * P, D), F32).ap()
        y_dram = nc.dram_tensor("y_rows", (MOST_TILES * P, D), F32).ap()
        piece_rows = nc.dram_tensor("piece_rows", (2, 2, PIECES, HD, HALF, SEQ), BF16).ap()
        x_rows = i["x"].rearrange("(t p) d -> p t d", p=P)

        with Stage(core, "load") as s:
            x_loaded, zeroed = s.sem("x_loaded"), s.sem("zeroed")
            block = s.block()

            @block.sync
            def _(sp):
                sp.dma_start(x[:, :, :], x_rows).then_inc(x_loaded, 16)
                sp.wait_ge(x_loaded, 16)

            @block.gpsimd
            def _(pool):
                pool.memset(ones[:, :], 1.0)
                pool.memset(tb.zeros[:, :], 0.0)
                pool.iota(tb.row_iota[:, :], [[1, P]], base=0, channel_multiplier=0,
                          allow_small_or_imprecise_dtypes=True)
                pool.iota(tb.column[:, :], [[0, 1]], base=0, channel_multiplier=1,
                          allow_small_or_imprecise_dtypes=True)
                for k in (1, 2):
                    pool.iota(tb.token_id[k][:, :].rearrange("p (t k) -> p t k", k=k), [[P, TILES], [0, k]],
                              base=0, channel_multiplier=1, allow_small_or_imprecise_dtypes=True)
                pool.memset(tb.before[:, :], 1.0).then_inc(zeroed, 1)
                pool.memset(ident16[:, :], 0.0)
                pool.memset(ident[:, :], 0.0).then_inc(zeroed, 1)
                pool.wait_ge(zeroed, 2)
                pool.affine_select(out=tb.before[:, :], in_=tb.before[:, :], compare_op=ALU.is_gt, fill=0.0,
                                   base=0, pattern=[[1, P]], channel_multiplier=-1)
                for eye in (ident, ident16):
                    pool.affine_select(out=eye[:, :], in_=eye[:, :], compare_op=ALU.not_equal, fill=1.0,
                                       base=0, pattern=[[-1, P]], channel_multiplier=1)

        norm_stage(core, "norm0", x, xn, xnT, ident)
        single_head_stage(core, "attn0", xn, xnT, i["ctxT"], i["w0"], ident, ones)
        post_norm_stage(core, "post0", x, xn, i["gb0"])
        norm_stage(core, "norm0f", x, xn, xnT, ident, i["router0"], logits)
        NT = TILES * 2 + 8
        route_stage(core, "route0", logits[:, :, 0:8], 8, 2, NT, tb, ones, xn, xn_dram)
        experts_stage(core, "experts0", NT, P, [128, 128, 96], i["experts0"], tb, xn_dram, y_dram, ident, ones)
        shared_stage(core, "shared0", xnT, logits[:, :, 8], i["shared0"], x)
        combine_stage(core, "combine0", 2, tb, y_dram[0:NT * P, :], x)
        kernels = core.keep("kernels", [P, B * HEADS * TAPS * TAPS])
        context_kernels_stage(core, "kernels1", i["ctxT"], i, ident, ones, tb, kernels)
        norm_stage(core, "norm1", x, xn, xnT, ident)
        conv_heads_stage(core, "heads1", xnT, i["heads1"], xn, ident, ident16, ones, i["mask1"],
                         kernels, piece_rows)
        project_stage(core, "proj1", x, xn, i["proj1"], ident, ones)
        norm_stage(core, "norm1f", x, xn, xnT, ident, i["router1"], logits)
        NT = TILES + 8
        route_stage(core, "route1", logits[:, :, 0:8], 8, 1, NT, tb, ones, xn, xn_dram, bias=i["router_bias1"])
        experts_stage(core, "experts1", NT, P, [P] * 8, i["experts1"], tb, xn_dram, y_dram, ident, ones,
                      biased=True, ahead=4)
        combine_stage(core, "combine1", 1, tb, y_dram[0:NT * P, :], x)
        norm_stage(core, "norm2", x, xn, xnT, ident)
        split_heads_stage(core, "heads2", MASKED, xnT, i["ctxT"], i["heads2"], x, ident, ident16, ones,
                          piece_rows, mask=i["mask2"])
        norm_stage(core, "norm2f", x, xn, xnT, ident, i["router2"], logits)
        NT = TILES * 2 + 32
        for n in range(2):
            route_stage(core, f"route2_{n}", logits[:, :, 32 * n:32 * n + 32], 32, 2, NT, tb, ones, xn,
                        None if n else xn_dram, factor=0.5)
            experts_stage(core, f"experts2_{n}", NT, P, [P], i[f"experts2_{n}"], tb, xn_dram, y_dram, ident, ones)
            combine_stage(core, f"combine2_{n}", 2, tb, y_dram[0:NT * P, :], x)
        norm_stage(core, "norm3", x, xn, xnT, ident)
        split_heads_stage(core, "heads3", PLAIN, xnT, i["ctxT"], i["heads3"], xn, ident, ident16, ones, piece_rows)
        project_stage(core, "proj3", x, xn, i["proj3"], ident, ones)
        norm_stage(core, "norm3f", x, xn, xnT, ident, i["router3"], logits)
        CAP = -(-5 * TILES * P // (4 * 32))
        route_stage(core, "route3", logits[:, :, 0:32], 32, 1, 32, tb, ones, xn, xn_dram, capacity=CAP)
        experts_stage(core, "experts3", 32, CAP, [P, P], i["experts3"], tb, xn_dram, y_dram, ident, ones)
        combine_stage(core, "combine3", 1, tb, y_dram[0:32 * CAP, :], x, xn)
        with Stage(core, "store") as s:
            stored = s.sem("stored")
            block = s.block()

            @block.sync
            def _(sp):
                sp.dma_start(outs.rearrange("(t p) d -> p t d", p=P), x[:, :, :]).then_inc(stored, 16)
                sp.wait_ge(stored, 16)


def _columns(w):
    K, n = w.shape
    return w.reshape(K // P, P, n).transpose(1, 0, 2).reshape(P, -1)


def _in_partition_0(row):
    import numpy as np

    out = np.zeros((P, row.size), row.dtype)
    out[0] = row.reshape(-1)
    return out


def _layouts(a):
    import numpy as np

    cat = lambda *parts: np.ascontiguousarray(np.concatenate(parts, axis=1))
    o = {"x": a["x"].reshape(B * SEQ, D)}
    o["ctxT"] = a["ctx_1024"].transpose(0, 2, 1).reshape(B, DC, P, SEQ).transpose(0, 2, 1, 3).reshape(B * P, DC * SEQ)
    col = lambda b: b.reshape(DC, P).T
    g = lambda n: a[n]
    o["w0"] = cat(_columns(g("L0_xattn_Wq")), _columns(g("L0_xattn_Wk")), _columns(g("L0_xattn_Wv")),
                  col(g("L0_xattn_bq")), col(g("L0_xattn_bk")), _in_partition_0(g("L0_xattn_bv")))
    o["gb0"] = np.stack([g("L0_xattn_gamma"), g("L0_xattn_beta")])

    def expert_rows(gate, up, down):
        E, _, F = gate.shape
        NF = -(-F // P)
        parts = [m.reshape(E, DC, P, F).transpose(0, 2, 1, 3).reshape(E, P, DC * F)
                 for m in (gate, up) if m is not None]
        full = np.zeros((E, NF * P, D), down.dtype)
        full[:, :F] = down
        parts.append(full.reshape(E, NF, P, D).transpose(0, 2, 1, 3).reshape(E, P, NF * D))
        return np.concatenate(parts, axis=2).reshape(E * P, -1)

    swap = lambda m: np.swapaxes(m, -1, -2)
    I = g("L0_ffn_experts_down").shape[2]
    gu = swap(g("L0_ffn_experts_gate_up"))
    o["experts0"] = expert_rows(gu[:, :, :I], gu[:, :, I:], swap(g("L0_ffn_experts_down")))
    o["shared0"] = expert_rows(g("L0_ffn_shared_gate_w").T[None], g("L0_ffn_shared_up_w").T[None],
                               g("L0_ffn_shared_down_w").T[None])
    o["router0"] = _columns(cat(g("L0_ffn_gate_w").T, g("L0_ffn_shared_expert_gate_w").T))
    w1 = expert_rows(g("L1_ffn_W1"), None, g("L1_ffn_W2")).reshape(8, P, -1)
    b1 = g("L1_ffn_b1").reshape(8, -1, P).transpose(0, 2, 1)
    b2 = np.zeros((8, P, D), w1.dtype)
    b2[:, 0] = g("L1_ffn_b2")
    o["experts1"] = np.concatenate([w1, b1, b2], axis=2).reshape(8 * P, -1)
    o["router1"], o["router_bias1"] = _columns(g("L1_ffn_Wg")), g("L1_ffn_bg").reshape(1, -1)
    o["router2"] = _columns(cat(g("L2_ffn_router_w0"), g("L2_ffn_router_w1")))
    for n in "01":
        o["experts2_" + n] = expert_rows(g("L2_ffn_wg" + n), g("L2_ffn_wu" + n), g("L2_ffn_wd" + n))
    o["router3"] = _columns(g("L3_ffn_w_router"))
    o["experts3"] = expert_rows(g("L3_ffn_w_gate"), g("L3_ffn_w_up"), g("L3_ffn_w_down"))

    by_width = lambda m: m.reshape(len(m), 2, HALF, HD).transpose(0, 1, 3, 2).reshape(len(m), D)

    def heads_rows(wq, wk, wv, bq, bk, bv):
        return cat(_columns(by_width(wq)), _columns(by_width(wk)), _columns(wv),
                   col(by_width(bq[None])[0]), col(by_width(bk[None])[0]), _in_partition_0(bv))

    none = np.zeros(D, a["x"].dtype)
    o["heads1"] = heads_rows(g("L1_xattn_Wq"), g("L1_xattn_Wk"), g("L1_xattn_Wv"), none, none, none)
    for n in "23":
        L = f"L{n}_xattn_"
        o["heads" + n] = heads_rows(g(L + "Wq").T, g(L + "Wk").T, g(L + "Wv").T, g(L + "bq"), g(L + "bk"), g(L + "bv"))
    o["proj1"] = cat(_columns(g("L1_xattn_proj_W")), _in_partition_0(g("L1_xattn_proj_b")))
    o["proj3"] = cat(_columns(g("L3_xattn_Wo").T), _in_partition_0(g("L3_xattn_bo")))
    m = g("mask_SxS_bc0")
    o["mask1"] = cat(_columns(m), _columns(m.T))
    m = g("mask_BxSxS2_if1")
    o["mask2"] = np.concatenate([k.reshape(B, QC, P, SEQ).transpose(0, 2, 1, 3).reshape(B * P, QC * SEQ)
                                 for k in (m, m.transpose(0, 2, 1))], axis=1)

    L = "L1_xattn_"
    o["hist"] = cat(_columns(g(L + "hist_W")), _in_partition_0(g(L + "hist_b")))
    o["hist_gb"] = np.stack([g(L + "hist_ln_g"), g(L + "hist_ln_b")])
    o["ctx_net"] = cat(_columns(g(L + "ctx_W1")), g(L + "ctx_b1")[:, None], g(L + "ctx_W2"),
                       _in_partition_0(g(L + "ctx_b2")))
    o["kg1"] = cat(_columns(g(L + "kg_W1")), _in_partition_0(g(L + "kg_b1")))
    o["kg_gb"] = np.stack([g(L + "kg_ln_g"), g(L + "kg_ln_b")])
    o["kg2"] = cat(_columns(g(L + "kg_W2")), _in_partition_0(g(L + "kg_b2")))
    return {k: np.ascontiguousarray(v) for k, v in o.items()}


def kernel(**inputs):
    import numpy as _np
    import concourse.bacc as _bacc
    from concourse.bass_utils import run_bass_kernel_spmd as _run

    nc = _bacc.Bacc("TRN2", target_bir_lowering=False, num_devices=1)
    arrays = _layouts({k: _np.asarray(v) for k, v in inputs.items()})
    ins = {k: nc.dram_tensor(f"in_{k}_dram", v.shape, mybir.dt.from_np(v.dtype), kind="ExternalInput").ap()
           for k, v in arrays.items()}
    out = nc.dram_tensor("out", (B * SEQ, D), F32, kind="ExternalOutput").ap()
    build(nc, ins, out)
    r = _run(nc, [{f"in_{k}_dram": v for k, v in arrays.items()}], core_ids=[0])
    return r.results[0]["out"].reshape(B, SEQ, D)
```
